# Optimizing a Trainium2 kernel written in Bass

```python
import numpy as np
import jax
import jax.numpy as jnp

def _softmax(x, axis=-1):
    return jax.nn.softmax(x, axis=axis)

def _gelu(x):
    return jax.nn.gelu(x, approximate=True)

def _silu(x):
    return jax.nn.silu(x)

def _sigmoid(x):
    return jax.nn.sigmoid(x)

def _layernorm(x, axis=-1, eps=1e-05):
    m = jnp.mean(x, axis=axis, keepdims=True)
    v = jnp.var(x, axis=axis, keepdims=True)
    return (x - m) / jnp.sqrt(v + eps)

def _scatter_add(tgt, idx, src, axis=0):
    return tgt.at[idx].add(src)

def _segment_sum(src, seg, n):
    return jax.ops.segment_sum(src, seg, n)
kernel_name = 'mk_gnn_ffn_d1_gnn_r8_b2bea6'

def setup_inputs(seed: int=0):
    np.random.seed(seed)
    _w = jnp.asarray

    def _rec_inputs():
        import jax
        import jax.numpy as jnp
        _gk = jax.random.key(seed)
        x = -6.415e-05 + 1 * jax.random.normal(jax.random.fold_in(_gk, 1), (1250, 512), jnp.float32)
        src = jax.random.randint(jax.random.fold_in(_gk, 2), (20000,), 0, 1250, jnp.int32)
        dst = jnp.minimum((1250 * jax.random.uniform(jax.random.fold_in(_gk, 3), (20000,)) ** 2.0).astype(jnp.int32), 9999)
        _o = jnp.argsort(dst, stable=True)
        src = src[_o]
        dst = dst[_o]
        edge_attr_64 = 0.000279952 + 1.00013 * jax.random.normal(jax.random.fold_in(_gk, 11), (20000, 64), jnp.float32)
        return (x, src, dst, edge_attr_64)
    x, src, dst, edge_attr_64 = _rec_inputs()

    def _L0_gnn_setup():
        import jax, jax.numpy as jnp
        import numpy as np
        N_NODES = 2500
        N_EDGES = 40000
        HIDDEN = 512
        EDGE_DIM = 64
        LN_EPS = 1e-05

        def mish(x):
            return x * jnp.tanh(jax.nn.softplus(x))
        key = jax.random.key(seed)
        ks = jax.random.split(key, 8)
        s = lambda fan_in: 1.0 / np.sqrt(fan_in)
        return {'x': jax.random.normal(ks[0], (N_NODES, HIDDEN), dtype=jnp.float32), 'edge_index': jax.random.randint(ks[1], (2, N_EDGES), 0, N_NODES, dtype=jnp.int64), 'edge_attr': jax.random.normal(ks[2], (N_EDGES, EDGE_DIM), dtype=jnp.float32), 'W1': jax.random.normal(ks[3], (2 * HIDDEN + EDGE_DIM, HIDDEN), dtype=jnp.float32) * s(2 * HIDDEN + EDGE_DIM), 'b1': jnp.zeros((HIDDEN,), dtype=jnp.float32), 'W2': jax.random.normal(ks[4], (HIDDEN, HIDDEN), dtype=jnp.float32) * s(HIDDEN), 'b2': jnp.zeros((HIDDEN,), dtype=jnp.float32), 'W3': jax.random.normal(ks[5], (2 * HIDDEN, HIDDEN), dtype=jnp.float32) * s(2 * HIDDEN), 'b3': jnp.zeros((HIDDEN,), dtype=jnp.float32), 'W4': jax.random.normal(ks[6], (HIDDEN, HIDDEN), dtype=jnp.float32) * s(HIDDEN), 'b4': jnp.zeros((HIDDEN,), dtype=jnp.float32), 'gamma': jnp.ones((HIDDEN,), dtype=jnp.float32), 'beta': jnp.zeros((HIDDEN,), dtype=jnp.float32)}
    _L0_gnn_all = _L0_gnn_setup()
    _L0_gnn_in = {k: v for k, v in _L0_gnn_all.items() if k in ('W1', 'b1', 'W2', 'b2', 'W3', 'b3', 'W4', 'b4', 'gamma', 'beta')}
    del _L0_gnn_all

    def _L0_ffn_setup():
        import jax, jax.numpy as jnp
        import numpy as np
        TOP_K = 2
        key = jax.random.key(seed)
        k1, k2, k3, k4 = jax.random.split(key, 4)
        B, S, D, F, E = (4, 512, 512, 256, 16)
        hidden_states = jax.random.normal(k1, (B, S, D), dtype=jnp.float32)
        gate_weight = jax.random.normal(k2, (E, D), dtype=jnp.float32) * 0.02
        w1 = jax.random.normal(k3, (E, F, D), dtype=jnp.float32) * 0.02
        w2 = jax.random.normal(k4, (E, D, F), dtype=jnp.float32) * 0.02
        return {'hidden_states': hidden_states, 'gate_weight': gate_weight, 'w1': w1, 'w2': w2}
    _L0_ffn_all = _L0_ffn_setup()
    _L0_ffn_in = {k: v for k, v in _L0_ffn_all.items() if k in ('gate_weight', 'w1', 'w2')}
    del _L0_ffn_all
    return {'x': x, 'src': src, 'dst': dst, 'edge_attr_64': edge_attr_64, 'L0_gnn_W1': _L0_gnn_in['W1'], 'L0_gnn_b1': _L0_gnn_in['b1'], 'L0_gnn_W2': _L0_gnn_in['W2'], 'L0_gnn_b2': _L0_gnn_in['b2'], 'L0_gnn_W3': _L0_gnn_in['W3'], 'L0_gnn_b3': _L0_gnn_in['b3'], 'L0_gnn_W4': _L0_gnn_in['W4'], 'L0_gnn_b4': _L0_gnn_in['b4'], 'L0_gnn_gamma': _L0_gnn_in['gamma'], 'L0_gnn_beta': _L0_gnn_in['beta'], 'L0_ffn_gate_weight': _L0_ffn_in['gate_weight'], 'L0_ffn_w1': _L0_ffn_in['w1'], 'L0_ffn_w2': _L0_ffn_in['w2']}

def reference(x, src, dst, edge_attr_64, L0_gnn_W1, L0_gnn_b1, L0_gnn_W2, L0_gnn_b2, L0_gnn_W3, L0_gnn_b3, L0_gnn_W4, L0_gnn_b4, L0_gnn_gamma, L0_gnn_beta, L0_ffn_gate_weight, L0_ffn_w1, L0_ffn_w2):
    import jax
    import jax.numpy as jnp

    def _L0_gnn_ref(x, edge_index, edge_attr, W1, b1, W2, b2, W3, b3, W4, b4, gamma, beta):
        import jax, jax.numpy as jnp
        import numpy as np
        N_NODES = 2500
        N_EDGES = 40000
        HIDDEN = 512
        EDGE_DIM = 64
        LN_EPS = 1e-05

        def mish(x):
            return x * jnp.tanh(jax.nn.softplus(x))
        src, dst = (edge_index[0], edge_index[1])
        edge_feat = jnp.concatenate([x[src], x[dst], edge_attr], axis=-1)
        h = mish(edge_feat @ W1 + b1)
        messages = mish(h @ W2 + b2)
        agg = jax.ops.segment_sum(messages, dst, num_segments=x.shape[0])
        u = mish(jnp.concatenate([x, agg], axis=-1) @ W3 + b3)
        out = u @ W4 + b4
        y = x + out
        mu = jnp.mean(y, axis=-1, keepdims=True)
        var = jnp.mean(jnp.square(y - mu), axis=-1, keepdims=True)
        return (y - mu) * jax.lax.rsqrt(var + LN_EPS) * gamma + beta

    def _L0_ffn_ref(hidden_states, gate_weight, w1, w2):
        import jax, jax.numpy as jnp
        import numpy as np
        TOP_K = 2
        B, S, D = hidden_states.shape
        E = gate_weight.shape[0]
        x = hidden_states.reshape(-1, D)
        gate_logits = x @ gate_weight.T
        top_vals, top_idx = jax.lax.top_k(gate_logits, TOP_K)
        routing_w = jax.nn.softmax(top_vals, axis=-1)
        mask = jnp.any(top_idx[:, :, None] == jnp.arange(E)[None, None, :], axis=1)
        h = jax.nn.silu(jnp.einsum('td,efd->tef', x, w1))
        counts = jnp.sum(mask, axis=0)
        h_sum = jnp.einsum('tef,te->ef', h, mask.astype(h.dtype))
        h_mean = h_sum / jnp.maximum(counts, 1)[:, None].astype(h.dtype)
        y_mean = jnp.einsum('ef,edf->ed', h_mean, w2)
        y_mean = jnp.where((counts > 0)[:, None], y_mean, 0.0)
        out = jnp.einsum('tk,tkd->td', routing_w, y_mean[top_idx])
        return out.reshape(B, S, D)
    edge_index = jnp.stack([src, dst])
    x = x + _L0_gnn_ref(_layernorm(x, axis=-1), edge_index, edge_attr_64, L0_gnn_W1, L0_gnn_b1, L0_gnn_W2, L0_gnn_b2, L0_gnn_W3, L0_gnn_b3, L0_gnn_W4, L0_gnn_b4, L0_gnn_gamma, L0_gnn_beta)
    x = x + _L0_ffn_ref(_layernorm(x, axis=-1)[None], L0_ffn_gate_weight, L0_ffn_w1, L0_ffn_w2)[0]
    return x

_drawn_inputs = setup_inputs


def setup_inputs(seed=0):
    import zlib

    import numpy as np

    out = dict(_drawn_inputs(seed))
    spreads = {'L0_gnn_b1': (0.0, 0.1),
     'L0_gnn_b2': (0.0, 0.1),
     'L0_gnn_b3': (0.0, 0.387),
     'L0_gnn_b4': (0.0, 0.295),
     'L0_gnn_gamma': (1.0, 0.2),
     'L0_gnn_beta': (0.0, 0.1)}
    factors = {'L0_ffn_gate_weight': 4.633, 'L0_ffn_w1': 5.026, 'L0_ffn_w2': 4.323}
    for name, (base, spread) in spreads.items():
        noise = np.random.default_rng([zlib.crc32(name.encode()), seed]).standard_normal(out[name].shape)
        drawn = base * np.exp(spread * noise) if base else spread * noise
        out[name] = jnp.asarray(drawn.astype(out[name].dtype))
    for name, factor in factors.items():
        out[name] = (out[name] * factor).astype(out[name].dtype)
    return out
```

```python
from contextlib import ExitStack

import concourse.bass as bass
from concourse import mybir

F32 = mybir.dt.float32
F32R = mybir.dt.float32r
I32 = mybir.dt.int32
ALU = mybir.AluOpType
ACT = mybir.ActivationFunctionType
AX_X = mybir.AxisListType.X

NODES, HID, EDGES, EDIM = 1250, 512, 20000, 64
EXPERTS, FFN = 16, 256
P = 128
NB = 125
NE = NB + 1
BLOCKS = NODES // NB
KC = HID // P
EP = 125
EJ = EDGES // EP
TILES = (EDGES + BLOCKS * (P - 1)) // P
PAIRS = TILES // 2
EPS = 1e-5
EXP_MAX = float(2 ** 30)
X_MAX = 20.75
EXP_LN_SET = "natural_log_exp_and_others"
NO_NODE = 1 << 20
assert TILES % 2 == 0 and PAIRS % 2 == 1


class Count:

    def __init__(self, eng, sem):
        self.eng, self.sem, self.n = eng, sem, 0

    def inc(self, ins):
        self.n += 1
        ins.then_inc(self.sem, 1)

    def wait(self):
        self.eng.wait_ge(self.sem, self.n)

    def step(self, ins):
        self.inc(ins)
        self.wait()


def f32(ap):
    return ap.bitcast(F32)


def need(eng, sem, n):
    if not isinstance(n, int) or n > 0:
        eng.wait_ge(sem, n)


def item(i, c):
    return i * 2 + c, c % 2, i + c // 2


def within(n, count):
    return not isinstance(n, int) or 0 <= n < count


def steps(eng, step, first, last, lo, hi):
    for s in range(first, lo):
        step(0, s)
    with eng.Fori(0, (hi - lo + 1) // 2) as i:
        for a in range(2):
            step(i, lo + a)
    for s in range(hi + 1, last + 1):
        step(0, s)


def gnn_ffn_kernel(nc, x, src, dst, edge_attr, W1, b1, W2, b2, W3, b3, W4, b4, gamma, beta, gate_w, w1, w2, out):
    top = ExitStack()
    with top:
        def dram(name, shape, dt):
            return nc.dram_tensor(name, shape, dt).ap()

        src_table = dram("src_table", (NODES, HID), F32)
        dst_table = dram("dst_table", (NODES, HID), F32)
        ea_scr = dram("ea_scr", (EDGES + P, EDIM), F32)
        idx_scr = dram("idx_scr", (EDGES + P, 3), I32)
        mask_scr = dram("mask_scr", (EXPERTS, BLOCKS * NE), F32)

        def sb(name, shape, dt, ctx=top):
            return ctx.enter_context(nc.sbuf_tensor(name, shape, dt))

        ident = sb("ident", [P, P], F32)
        ones = sb("ones", [P, P], F32)
        minus_r = sb("minus_r", [2, P], F32R)
        plus_r = sb("plus_r", [2, P], F32R)
        bias_r = sb("bias_r", [2, 4, HID], F32R)
        eps_col = sb("eps_col", [P, 1], F32)
        half_col = sb("half_col", [P, 1], F32)
        agg = sb("agg", [NB, BLOCKS, HID], F32)
        xn_all = sb("xn_all", [NB, BLOCKS, HID], F32)

        edge_ctx = ExitStack()
        W2h = sb("W2h", [P, KC, HID], F32R, edge_ctx)
        W2l = sb("W2l", [P, KC, HID], F32R, edge_ctx)
        Wch = sb("Wch", [P, HID], F32R, edge_ctx)
        Wcl = sb("Wcl", [P, HID], F32R, edge_ctx)
        start_i = sb("start_i", [P, TILES], I32, edge_ctx)
        block_i = sb("block_i", [P, TILES], I32, edge_ctx)
        block_off = sb("block_off", [P, TILES], F32, edge_ctx)
        iota_n = sb("iota_n", [P, NE], F32, edge_ctx)

        prologue(nc, locals())
        edge_phase(nc, locals())
        edge_ctx.close()

        x1_all = agg
        xlTh = sb("xlTh", [P, KC, BLOCKS * NE], F32R)
        xlTl = sb("xlTl", [P, KC, BLOCKS * NE], F32R)
        node_phase(nc, locals())
        ffn_phase(nc, locals())


def prologue(nc, T):
    x, src, dst, edge_attr = T["x"], T["src"], T["dst"], T["edge_attr"]
    W1, W2 = T["W1"], T["W2"]
    ident, ones, minus_r, plus_r, bias_r = T["ident"], T["ones"], T["minus_r"], T["plus_r"], T["bias_r"]
    eps_col, half_col, agg = T["eps_col"], T["half_col"], T["agg"]
    W2h, W2l, Wch, Wcl = T["W2h"], T["W2l"], T["Wch"], T["Wcl"]
    start_i, block_i, block_off, iota_n = T["start_i"], T["block_i"], T["block_off"], T["iota_n"]
    xn_all, src_table, dst_table = T["xn_all"], T["src_table"], T["dst_table"]
    ea_scr, idx_scr = T["ea_scr"], T["idx_scr"]

    ctx, sems = ExitStack(), []
    with ctx:
        def sb(name, shape, dt):
            return ctx.enter_context(nc.sbuf_tensor(name, shape, dt))

        def pb(name, shape, dt=F32):
            return ctx.enter_context(nc.psum_tensor(name, shape, dt))

        def sem(name):
            sems.append(nc.alloc_semaphore(name))
            return sems[-1]

        w1_raw = sb("w1_raw", [P, 2 * KC, HID], F32)
        w1h = sb("w1h", [P, 2 * KC, HID], F32R)
        w1l = sb("w1l", [P, 2 * KC, HID], F32R)
        wc_raw = sb("wc_raw", [P, HID], F32)
        bias_raw = sb("bias_raw", [2, 4, HID], F32)
        bias_hi = sb("bias_hi", [2, 4, HID], F32R)
        row_is1 = sb("row_is1", [P, 2], F32)
        x_raw = sb("x_raw", [P, BLOCKS, HID], F32)
        w2_raw = x_raw[:, 0:KC, :]
        rank = x_raw[0:EP, KC:2 * KC, :].rearrange("p a d -> p (a d)")[:, 0:(BLOCKS + 1) * EJ].rearrange("p (b j) -> p b j", j=EJ)
        xn_op = sb("xn_op", [NE, 2, HID], F32)
        xTh = sb("xTh", [P, 2, KC * NE], F32R)
        xTl = sb("xTl", [P, 2, KC * NE], F32R)
        tabs = sb("tabs", [NB, 2, 2, HID], F32)
        stats = sb("stats", [NB, BLOCKS, 6], F32)
        mv = sb("mv", [NB, BLOCKS, 2], F32)
        rs = sb("rs", [NB, 4, BLOCKS], F32)

        dst_i = sb("dst_i", [EP, EJ], I32)
        src_i = sb("src_i", [EP, EJ], I32)
        next_i = sb("next_i", [EP, EJ], I32)
        rec_i = sb("rec_i", [EP, EJ, 3], I32)
        tail_i = sb("tail_i", [P, 3], I32)
        tail_ea = sb("tail_ea", [P, EDIM], F32)
        below = sb("below", [EP, BLOCKS + 2, EJ], F32)
        row_cnt = sb("row_cnt", [EP, BLOCKS + 2], F32)
        tri = sb("tri", [EP, EP], F32)
        first = sb("first", [P, BLOCKS + 2], F32)
        row_off = sb("row_off", [EP, BLOCKS + 2], F32)
        cnt_i = sb("cnt_i", [P, BLOCKS], I32)
        nt = sb("nt", [P, BLOCKS], F32)
        tbase = sb("tbase", [P, BLOCKS + 1], F32)
        off = sb("off", [P, BLOCKS + 1], F32)
        doff = sb("doff", [P, BLOCKS], F32)
        iota_t = sb("iota_t", [P, TILES], F32)
        reached = sb("reached", [P, BLOCKS, TILES], F32)
        start_f = sb("start_f", [P, TILES], F32)
        block_f = sb("block_f", [P, TILES], F32)
        flag_i = sb("flag_i", [1, 1], I32)
        pos_f = sb("pos_f", [EP, EJ], F32)
        pos_i = sb("pos_i", [EP, EJ], I32)
        carrier = sb("carrier", [1, 2], F32)
        ea_row = sb("ea_row", [EP, EDIM], F32)
        rec_row = sb("rec_row", [EP, 3], I32)
        pos_row = sb("pos_row", [EP, 1], I32)

        ps_t = pb("ps_t", [P, 2, 512])
        ps_a = pb("ps_a", [P, 2, 512])
        ps_b = pb("ps_b", [P, 2, 512])
        ps_m = pb("ps_m", [P, 512])

        names = ("w1_in w2_in wc_in bias_in dst_in src_in next_in rec_out tail_out ea_out next_set const pool_step dve_step "
                 "w1_hi w1_lo edge_hi bias_hi_ready bias_ready cnt_ready cnt_sum var_ready rstd_ready xn_ready op_zero op_ready "
                 "xt_tr xT_hi xT_lo a_ready b_ready a_out b_out meta_ready rank_step pos_ready scat_in scat_out row_ready carried").split()
        S = {n: sem(n) for n in names}
        x_in = [sem(f"x_in{k}") for k in range(BLOCKS // 2)]
        a_stored = [sem(f"a_stored{k}") for k in range(2)]
        b_stored = [sem(f"b_stored{k}") for k in range(2)]
        block = ctx.enter_context(nc.Block())

        src_rows = src_table.rearrange("(i p) d -> i p d", p=NB)
        dst_rows = dst_table.rearrange("(i p) d -> i p d", p=NB)

        @block.sync
        def _(sp):
            x_rows = x.rearrange("(i p) d -> p i d", p=NB)
            for k in range(BLOCKS // 2):
                sp.dma_start(x_raw[0:NB, 2 * k:2 * k + 2, :], x_rows[:, 2 * k:2 * k + 2, :]).then_inc(x_in[k], 16)
            sp.dma_start(dst_i[:], dst.rearrange("(p j) -> p j", p=EP)).then_inc(S["dst_in"], 16)
            sp.wait_ge(S["next_set"], 1)
            sp.dma_start(next_i[0:EP - 1, :], dst[1:1 + (EP - 1) * EJ].rearrange("(p j) -> p j", j=EJ)).then_inc(S["next_in"], 16)
            sp.dma_start(next_i[EP - 1:EP, 0:EJ - 1], dst[1 + (EP - 1) * EJ:EDGES].rearrange("(p j) -> p j", p=1)).then_inc(S["next_in"], 16)
            sp.dma_start(w1_raw[:], W1[0:2 * HID, :].rearrange("(k p) n -> p k n", p=P)).then_inc(S["w1_in"], 16)
            for n, b in enumerate(("b1", "b2", "b3", "b4")):
                for r in range(2):
                    sp.dma_start(bias_raw[r:r + 1, n, :], T[b].rearrange("(a n) -> a n", a=1)).then_inc(S["bias_in"], 16)
            sp.dma_start(src_i[:], src.rearrange("(p j) -> p j", p=EP)).then_inc(S["src_in"], 16)
            for k in range(2):
                sp.dma_start(wc_raw[k * EDIM:(k + 1) * EDIM, :], W1[2 * HID:2 * HID + EDIM, :]).then_inc(S["wc_in"], 16)
            sp.wait_ge(S["xn_ready"], BLOCKS)
            sp.dma_start(w2_raw, W2.rearrange("(k p) n -> p k n", p=P)).then_inc(S["w2_in"], 16)

            def step(i, c):
                t, k, _ = item(i, c - 1)
                if within(t, BLOCKS):
                    sp.wait_ge(S["a_out"], t + 1)
                    sp.dma_start(src_rows[bass.ds(t, 1)].rearrange("a p d -> (a p) d"), tabs[:, k, 0, :]).then_inc(a_stored[k], 16)
                    sp.wait_ge(S["b_out"], t + 1)
                    sp.dma_start(dst_rows[bass.ds(t, 1)].rearrange("a p d -> (a p) d"), tabs[:, k, 1, :]).then_inc(b_stored[k], 16)

            steps(sp, step, 0, BLOCKS, 4, BLOCKS - 1)
            for k in range(2):
                sp.wait_ge(a_stored[k], 16 * (BLOCKS // 2))
                sp.wait_ge(b_stored[k], 16 * (BLOCKS // 2))

        @block.gpsimd
        def _(pool):
            nc.gpsimd.memset(next_i[:], NO_NODE).then_inc(S["next_set"], 1)
            c = Count(pool, S["pool_step"])
            c.inc(nc.gpsimd.memset(ident[:], 0.0))
            c.inc(nc.gpsimd.memset(ones[:], 1.0))
            c.inc(nc.gpsimd.memset(tri[:], 1.0))
            c.inc(nc.gpsimd.memset(row_is1[:], 0.0))
            c.inc(nc.gpsimd.memset(tail_i[:], 0))
            c.inc(nc.gpsimd.memset(tail_ea[:], 0.0))
            c.step(nc.gpsimd.iota(iota_t[:], [[1, TILES]], base=0, channel_multiplier=0, allow_small_or_imprecise_dtypes=True))
            c.inc(nc.gpsimd.iota(iota_n[:], [[1, NE]], base=0, channel_multiplier=0, allow_small_or_imprecise_dtypes=True))
            c.inc(nc.gpsimd.affine_select(out=ident[:], in_=ident[:], compare_op=ALU.not_equal, fill=1.0, base=0,
                                          pattern=[[-1, P]], channel_multiplier=1))
            c.inc(nc.gpsimd.affine_select(out=tri[:], in_=tri[:], compare_op=ALU.is_gt, fill=0.0, base=0,
                                          pattern=[[1, EP]], channel_multiplier=-1))
            c.inc(nc.gpsimd.affine_select(out=row_is1[:], in_=row_is1[:], compare_op=ALU.not_equal, fill=1.0, base=0,
                                          pattern=[[-1, 2]], channel_multiplier=1))
            c.inc(nc.gpsimd.memset(tail_i[:, 2:3], NO_NODE))
            c.inc(nc.gpsimd.memset(eps_col[:], EPS))
            c.step(nc.gpsimd.memset(half_col[:], 0.5))
            nc.gpsimd.memset(xn_op[:], 0.0).then_inc(S["const"], 1)
            pool.dma_start(idx_scr[EDGES:EDGES + P, :], tail_i[:]).then_inc(S["tail_out"], 16)
            pool.dma_start(ea_scr[EDGES:EDGES + P, :], tail_ea[:]).then_inc(S["tail_out"], 16)
            pool.wait_ge(S["dst_in"], 16)
            pool.wait_ge(S["src_in"], 16)
            c.inc(nc.gpsimd.tensor_copy(rec_i[:, :, 0], src_i[:]))
            c.inc(nc.gpsimd.tensor_copy(rec_i[:, :, 1], dst_i[:]))
            c.inc(nc.gpsimd.tensor_copy(rec_i[:, :, 2], dst_i[:]))
            pool.wait_ge(S["const"], 1)

            def step(i, c):
                t, k, _ = item(i, c)
                if within(t, BLOCKS):
                    pool.wait_ge(S["xn_ready"], t + 1)
                    need(pool, S["xt_tr"], t - 1)
                    nc.gpsimd.tensor_copy(xn_op[0:NB, k, :], xn_all[:, bass.ds(t, 1), :].rearrange("p a d -> p (a d)")).then_inc(S["op_ready"], 1)

            steps(pool, step, 0, BLOCKS - 1, 4, BLOCKS - 1)
            nc.gpsimd.memset(agg[:], 0.0).then_inc(S["pool_step"], 1)
            c.n += 1
            c.wait()
            pool.wait_ge(S["meta_ready"], 1)
            unsorted = pool.value_load(flag_i[0:1, 0:1], min_val=0, max_val=EDGES)
            nc.gpsimd.memset(carrier[:], 0.0).then_inc(S["carried"], 1)
            with pool.If(unsorted > 0):
                pool.wait_ge(S["pos_ready"], 1)
                ea_cols = edge_attr.rearrange("(p j) d -> j p d", p=EP)
                with pool.Fori(0, EJ) as j:
                    pool.dma_start(ea_row[:], ea_cols[bass.ds(j, 1)].rearrange("a p d -> (a p) d")).then_inc(S["scat_in"], 16)
                    nc.gpsimd.tensor_copy(rec_row[:], rec_i[:, bass.ds(j, 1), :].rearrange("p a r -> p (a r)")).then_inc(S["row_ready"], 1)
                    nc.gpsimd.tensor_copy(pos_row[:], pos_i[:, bass.ds(j, 1)]).then_inc(S["row_ready"], 1)
                    pool.wait_ge(S["row_ready"], j * 2 + 2)
                    pool.wait_ge(S["scat_in"], j * 16 + 16)
                    pool.wait_ge(S["carried"], j + 1)
                    nc.gpsimd.tensor_tensor(carrier[0:1, 0:1], carrier[0:1, 1:2], carrier[0:1, 1:2], ALU.add).then_inc(S["carried"], 1)
                    pool.indirect_dma_start(out=ea_scr[:, :], out_offset=bass.IndirectOffsetOnAxis(ap=pos_row[:, 0:1], axis=0),
                                            in_=ea_row[:], in_offset=None).then_inc(S["scat_out"], 16)
                    pool.indirect_dma_start(out=idx_scr[:, :], out_offset=bass.IndirectOffsetOnAxis(ap=pos_row[:, 0:1], axis=0),
                                            in_=rec_row[:], in_offset=None).then_inc(S["scat_out"], 16)
                    pool.wait_ge(S["scat_out"], j * 32 + 32)
            with pool.Else():
                pool.dma_start(ea_scr[0:EDGES, :].rearrange("(p j) d -> p (j d)", p=P - 3), edge_attr.rearrange("(p j) d -> p (j d)", p=P - 3)).then_inc(S["ea_out"], 16)
                pool.dma_start(idx_scr[0:EDGES, :].rearrange("(p j) r -> p (j r)", p=EP), rec_i[:].rearrange("p j r -> p (j r)")).then_inc(S["rec_out"], 16)
                pool.wait_ge(S["ea_out"], 16)
                pool.wait_ge(S["rec_out"], 16)
            pool.wait_ge(S["tail_out"], 32)
            c.wait()

        @block.scalar
        def _(act):
            nc.scalar.preload_act_table_set(EXP_LN_SET)
            act.wait_ge(S["w1_in"], 16)
            for k in range(2 * KC):
                nc.scalar.activation(w1h[:, k, :], w1_raw[:, k, :], ACT.Copy).then_inc(S["w1_hi"], 1)
            act.wait_ge(S["bias_in"], 128)
            nc.scalar.activation(bias_hi[:], bias_raw[:], ACT.Copy).then_inc(S["bias_hi_ready"], 1)
            act.wait_ge(S["const"], 1)
            act.wait_ge(S["var_ready"], 1)
            nc.scalar.activation(rs[:, 0, :], mv[:, :, 1], ACT.Ln, bias=eps_col[0:NB, :]).then_inc(S["rstd_ready"], 1)
            act.wait_ge(S["rstd_ready"], 1)
            nc.scalar.activation(rs[:, 1, :], rs[:, 0, :], ACT.Exp, scale=-0.5).then_inc(S["rstd_ready"], 1)

            def step(i, c):
                t, k, _ = item(i, c)
                if within(t, BLOCKS):
                    act.wait_ge(S["xt_tr"], t + 1)
                    need(act, S["b_ready"], t - 1)
                    nc.scalar.activation(xTh[:, k, :], ps_t[:, k, 0:KC * NE], ACT.Copy).then_inc(S["xT_hi"], 1)
                t, k, used = item(i, c - 1)
                if within(t, BLOCKS):
                    act.wait_ge(S["a_ready"], t + 1)
                    need(act, a_stored[k], used * 16)
                    nc.scalar.activation(tabs[:, k, 0, :], ps_a[0:NB, k, :], ACT.Copy).then_inc(S["a_out"], 1)

            steps(act, step, 0, BLOCKS, 4, BLOCKS - 1)
            act.wait_ge(S["w2_in"], 16)
            nc.scalar.activation(W2h[:], w2_raw, ACT.Copy).then_inc(S["edge_hi"], 1)
            act.wait_ge(S["wc_in"], 32)
            nc.scalar.activation(Wch[:], wc_raw[:], ACT.Copy).then_inc(S["edge_hi"], 1)

        @block.vector
        def _(dve):
            c = Count(dve, S["dve_step"])
            c.inc(nc.vector.memset(below[:, 0, :], 0.0))
            c.inc(nc.vector.memset(below[:, BLOCKS, :], 1.0))
            c.inc(nc.vector.memset(tbase[:, 0:1], 0.0))
            dve.wait_ge(S["dst_in"], 16)
            for b in range(1, BLOCKS):
                c.inc(nc.vector.tensor_scalar(below[:, b, :], dst_i[:], float(NB * b), None, ALU.is_lt))
            dve.wait_ge(S["next_in"], 32)
            c.step(nc.vector.tensor_tensor(below[:, BLOCKS + 1, :], next_i[:], dst_i[:], ALU.is_lt))
            nc.vector.tensor_reduce(out=row_cnt[:], in_=below[:], axis=AX_X, op=ALU.add).then_inc(S["cnt_ready"], 1)
            for t in range(BLOCKS):
                if t % 2 == 0:
                    dve.wait_ge(x_in[t // 2], 16)
                c.inc(nc.vector.bn_stats(out=stats[:, t, :], in_=x_raw[0:NB, t, :]))
            c.wait()
            for t in range(BLOCKS):
                ins = nc.vector.bn_aggr(out=mv[:, t, :], in_=stats[:, t, :])
            ins.then_inc(S["var_ready"], 1)
            dve.wait_ge(S["rstd_ready"], 2)
            c.step(nc.vector.tensor_tensor(rs[:, 2, :], rs[:, 1, :], rs[:, 1, :], ALU.mult))
            c.step(nc.vector.scalar_tensor_tensor(out=rs[:, 3, :], in0=mv[:, :, 1], scalar=EPS, in1=rs[:, 2, :], op0=ALU.add, op1=ALU.mult))
            c.step(nc.vector.tensor_scalar(rs[:, 3, :], rs[:, 3, :], -0.5, 1.5, ALU.mult, ALU.add))
            c.step(nc.vector.tensor_tensor(rs[:, 2, :], rs[:, 1, :], rs[:, 3, :], ALU.mult))
            for t in range(BLOCKS):
                nc.vector.tensor_scalar(xn_all[:, t, :], x_raw[0:NB, t, :], mv[:, t, 0:1], rs[:, 2, t:t + 1], ALU.subtract, ALU.mult).then_inc(S["xn_ready"], 1)
            for k in range(2 * KC):
                dve.wait_ge(S["w1_hi"], k + 1)
                nc.vector.tensor_tensor(w1l[:, k, :], w1_raw[:, k, :], f32(w1h[:, k, :]), ALU.subtract).then_inc(S["w1_lo"], 1)
            dve.wait_ge(S["const"], 1)
            dve.wait_ge(S["bias_hi_ready"], 1)
            c.inc(nc.vector.tensor_copy(plus_r[:], ones[0:2, :]))
            c.inc(nc.vector.tensor_scalar(minus_r[:], ones[0:2, :], -1.0, None, ALU.mult))
            c.step(nc.vector.tensor_tensor(bias_raw[:], bias_raw[:], f32(bias_hi[:]), ALU.subtract))
            c.step(nc.vector.tensor_scalar(bias_raw[:], bias_raw[:], row_is1[0:2, 1:2], None, ALU.mult))
            nc.vector.scalar_tensor_tensor(out=bias_r[:], in0=f32(bias_hi[:]), scalar=row_is1[0:2, 0:1], in1=bias_raw[:],
                                           op0=ALU.mult, op1=ALU.add).then_inc(S["bias_ready"], 1)
            dve.wait_ge(S["cnt_sum"], 1)
            c.inc(nc.vector.tensor_copy(first[:], ps_m[:, 0:BLOCKS + 2]))
            c.step(nc.vector.tensor_copy(row_off[:], ps_m[0:EP, 64:64 + BLOCKS + 2]))
            nc.vector.tensor_copy(flag_i[:], first[0:1, BLOCKS + 1:BLOCKS + 2]).then_inc(S["meta_ready"], 1)
            c.step(nc.vector.scalar_tensor_tensor(out=cnt_i[:], in0=first[:, 1:BLOCKS + 1], scalar=float(P - 1), in1=first[:, 0:BLOCKS],
                                                  op0=ALU.add, op1=ALU.subtract))
            c.step(nc.vector.tensor_scalar(cnt_i[:], cnt_i[:], 7, None, ALU.arith_shift_right))
            c.step(nc.vector.tensor_copy(nt[:], cnt_i[:]))
            c.step(nc.vector.tensor_tensor_scan(out=tbase[:, 1:BLOCKS + 1], data0=ones[:, 0:BLOCKS], data1=nt[:], initial=0.0,
                                                op0=ALU.mult, op1=ALU.add))
            c.step(nc.vector.scalar_tensor_tensor(out=off[:], in0=tbase[:], scalar=-float(P), in1=first[:, 0:BLOCKS + 1],
                                                  op0=ALU.mult, op1=ALU.add))
            c.inc(nc.vector.tensor_tensor(doff[:], off[:, 1:BLOCKS + 1], off[:, 0:BLOCKS], ALU.subtract))
            for b in range(BLOCKS):
                c.inc(nc.vector.tensor_scalar(reached[:, b, :], iota_t[:], tbase[:, b + 1:b + 2], None, ALU.is_ge))
            c.wait()
            c.step(nc.vector.tensor_reduce(out=block_f[:], in_=reached[:, 0:BLOCKS - 1, :].rearrange("p b t -> p t b"), axis=AX_X, op=ALU.add))
            for b in range(BLOCKS):
                c.inc(nc.vector.tensor_scalar(reached[:, b, :], reached[:, b, :], doff[:, b:b + 1], None, ALU.mult))
            c.wait()
            c.step(nc.vector.tensor_reduce(out=start_f[:], in_=reached[:].rearrange("p b t -> p t b"), axis=AX_X, op=ALU.add))
            c.step(nc.vector.scalar_tensor_tensor(out=start_f[:], in0=iota_t[:], scalar=float(P), in1=start_f[:], op0=ALU.mult, op1=ALU.add))
            c.inc(nc.vector.tensor_scalar(start_i[:], start_f[:], float(EDGES), None, ALU.min))
            c.inc(nc.vector.tensor_copy(block_i[:], block_f[:]))
            c.inc(nc.vector.tensor_scalar(block_off[:], block_f[:], float(NB), None, ALU.mult))
            c.wait()
            unsorted = dve.value_load(flag_i[0:1, 0:1], min_val=0, max_val=EDGES)
            with dve.If(unsorted > 0):
                for b in range(BLOCKS + 1):
                    ins = nc.vector.tensor_tensor_scan(out=rank[:, b, :], data0=below[:, BLOCKS, :], data1=below[:, b, :],
                                                       initial=row_off[:, b:b + 1], op0=ALU.mult, op1=ALU.add)
                ins.then_inc(S["rank_step"], 1)
                dve.wait_ge(S["rank_step"], 1)
                nc.vector.tensor_tensor(rank[:, 0:BLOCKS, :], rank[:, 1:BLOCKS + 1, :], rank[:, 0:BLOCKS, :], ALU.subtract).then_inc(S["rank_step"], 1)
                nc.vector.tensor_tensor(below[:, 0:BLOCKS, :], below[:, 1:BLOCKS + 1, :], below[:, 0:BLOCKS, :], ALU.subtract).then_inc(S["rank_step"], 1)
                dve.wait_ge(S["rank_step"], 3)
                for b in range(BLOCKS):
                    ins = nc.vector.tensor_scalar(rank[:, b, :], rank[:, b, :], first[0:EP, b:b + 1], -1.0, ALU.add, ALU.add)
                ins.then_inc(S["rank_step"], 1)
                dve.wait_ge(S["rank_step"], 4)
                nc.vector.tensor_tensor(rank[:, 0:BLOCKS, :], rank[:, 0:BLOCKS, :], below[:, 0:BLOCKS, :], ALU.mult).then_inc(S["rank_step"], 1)
                dve.wait_ge(S["rank_step"], 5)
                nc.vector.tensor_reduce(out=pos_f[:], in_=rank[:, 0:BLOCKS, :].rearrange("p b j -> p j b"), axis=AX_X, op=ALU.add).then_inc(S["rank_step"], 1)
                dve.wait_ge(S["rank_step"], 6)
                nc.vector.tensor_copy(pos_i[:], pos_f[:]).then_inc(S["pos_ready"], 1)

            def step(i, c):
                t, k, _ = item(i, c)
                if within(t, BLOCKS):
                    dve.wait_ge(S["xT_hi"], t + 1)
                    nc.vector.tensor_tensor(xTl[:, k, :], ps_t[:, k, 0:KC * NE], f32(xTh[:, k, :]), ALU.subtract).then_inc(S["xT_lo"], 1)
                t, k, used = item(i, c - 1)
                if within(t, BLOCKS):
                    dve.wait_ge(S["b_ready"], t + 1)
                    need(dve, b_stored[k], used * 16)
                    nc.vector.tensor_copy(tabs[:, k, 1, :], ps_b[0:NB, k, :]).then_inc(S["b_out"], 1)

            steps(dve, step, 0, BLOCKS, 4, BLOCKS - 1)
            dve.wait_ge(S["edge_hi"], 2)
            nc.vector.tensor_tensor(W2l[:], w2_raw, f32(W2h[:]), ALU.subtract).then_inc(S["dve_step"], 1)
            nc.vector.tensor_tensor(Wcl[:], wc_raw[:], f32(Wch[:]), ALU.subtract).then_inc(S["dve_step"], 1)

        @block.tensor
        def _(pe):
            pe.wait_ge(S["const"], 1)
            pe.wait_ge(S["cnt_ready"], 1)
            nc.tensor.matmul(ps_m[:, 0:BLOCKS + 2], ones[0:EP, :], row_cnt[:], start=True, stop=True)
            nc.tensor.matmul(ps_m[0:EP, 64:64 + BLOCKS + 2], tri[:], row_cnt[:], start=True, stop=True).then_inc(S["cnt_sum"], 1)
            pe.wait_ge(S["w1_lo"], 2 * KC)
            pe.wait_ge(S["bias_ready"], 1)

            def step(i, c):
                t, k, _ = item(i, c)
                if within(t, BLOCKS):
                    pe.wait_ge(S["op_ready"], t + 1)
                    need(pe, S["xT_lo"], t - 1)
                    for q in range(KC):
                        ins = nc.tensor.transpose(ps_t[:, k, q * NE:(q + 1) * NE], xn_op[:, k, q * P:(q + 1) * P], ident[0:NE, 0:NE])
                    ins.then_inc(S["xt_tr"], 1)
                t, k, _ = item(i, c - 1)
                if within(t, BLOCKS):
                    pe.wait_ge(S["xT_lo"], t + 1)
                    for n, ps, ready, free in ((0, ps_a, "a_ready", "a_out"), (1, ps_b, "b_ready", "b_out")):
                        o = ps[0:NE, k, :]
                        need(pe, S[free], t - 1)
                        if n == 1:
                            nc.tensor.matmul(o, plus_r[:, 0:NE], bias_r[:, 0, :], start=True, stop=False)
                        for q in range(KC):
                            hi, lo = xTh[:, k, q * NE:(q + 1) * NE], xTl[:, k, q * NE:(q + 1) * NE]
                            nc.tensor.matmul(o, hi, w1h[:, n * KC + q, :], start=(q == 0 and n == 0), stop=False)
                            nc.tensor.matmul(o, hi, w1l[:, n * KC + q, :], start=False, stop=False)
                            ins = nc.tensor.matmul(o, lo, w1h[:, n * KC + q, :], start=False, stop=(q == KC - 1))
                        ins.then_inc(S[ready], 1)

            steps(pe, step, 0, BLOCKS, 4, BLOCKS - 1)
    nc.clear_and_free_semaphores(sems)
    nc.all_engine_barrier()


def edge_phase(nc, T):
    W2h, W2l, Wch, Wcl = T["W2h"], T["W2l"], T["Wch"], T["Wcl"]
    ident, minus_r, bias_r, half_col, iota_n = T["ident"], T["minus_r"], T["bias_r"], T["half_col"], T["iota_n"]
    start_i, block_i, block_off, agg = T["start_i"], T["block_i"], T["block_off"], T["agg"]
    src_table, dst_table, ea_scr, idx_scr = T["src_table"], T["dst_table"], T["ea_scr"], T["idx_scr"]

    ctx, sems = ExitStack(), []
    with ctx:
        def sb(name, shape, dt=F32):
            return ctx.enter_context(nc.sbuf_tensor(name, shape, dt))

        def sem(name):
            sems.append(nc.alloc_semaphore(name))
            return sems[-1]

        idx_sl = sb("idx_sl", [P, 2, 2, 3], I32)
        ea_sl = sb("ea_sl", [P, 2, 2, EDIM])
        ea_hl = sb("ea_hl", [P, 2, 2, 2 * EDIM], F32R)
        eaT = sb("eaT", [2 * EDIM, 2, 2, P], F32R)
        gath = sb("gath", [P, 2, 2, HID])
        pre = sb("pre", [P, 2, 2, HID])
        act1 = sb("act1", [P, 2, 2, HID])
        act2 = sb("act2", [P, 2, 2, HID])
        hTh = sb("hTh", [P, 2, 2, HID], F32R)
        hTl = sb("hTl", [P, 2, 2, HID], F32R)
        msg_hi = sb("msg_hi", [P, 2, 2, HID], F32R)
        msg_lo = sb("msg_lo", [P, 2, 2, HID], F32R)
        dloc = sb("dloc", [P, TILES])
        carrier = sb("e_carrier", [1, 2])
        onehot = sb("onehot", [P, 2, 2, NE], F32R)

        ps_1 = ctx.enter_context(nc.psum_tensor("ps_1", [P, 2, HID], F32))
        ps_h = ctx.enter_context(nc.psum_tensor("ps_h", [P, 2, HID], F32))
        ps_2 = ctx.enter_context(nc.psum_tensor("ps_2", [P, 2, 2, HID], F32))

        def slots(name):
            return [sem(f"{name}{k}") for k in range(2)]

        idx_in, ea_in, src_gath, both_gath = slots("idx_in"), slots("ea_in"), slots("src_gath"), slots("both_gath")
        names = ("ea_hi split eaT_ps eaT_ready lin1_ps pre_ready exp1 inc1 sq1 ln1 quot1 h_ready hT_ps hT_hi hT_lo lin2_ps "
                 "exp2 inc2 sq2 ln2 quot2 msg_ready msg_hi_ready msg_lo_ready onehot_ready sum_ps summed carried").split()
        S = {n: sem("e_" + n) for n in names}
        block = ctx.enter_context(nc.Block())

        @block.sync
        def _(sp):
            def step(i, c):
                q, k, used = item(i, c + 3)
                if within(q, PAIRS):
                    need(sp, both_gath[k], used * 32)
                    need(sp, S["split"], q - 1)
                    for j in range(2):
                        first = sp.value_load(start_i[0:1, bass.ds(q * 2 + j, 1)], min_val=0, max_val=EDGES)
                        sp.dma_start(idx_sl[:, k, j, :], idx_scr[bass.ds(first, P), :]).then_inc(idx_in[k], 16)
                        sp.dma_start(ea_sl[:, k, j, :], ea_scr[bass.ds(first, P), :]).then_inc(ea_in[k], 16)

            steps(sp, step, -3, PAIRS + 3, 6, PAIRS - 4)

        @block.gpsimd
        def _(pool):
            nc.gpsimd.memset(carrier[:], 0.0).then_inc(S["carried"], 1)

            def carry(n):
                pool.wait_ge(S["carried"], n + 1)
                nc.gpsimd.tensor_tensor(carrier[0:1, 0:1], carrier[0:1, 1:2], carrier[0:1, 1:2], ALU.add).then_inc(S["carried"], 1)

            def step(i, c):
                g, gk, used = item(i, c + 2)
                if within(g, PAIRS):
                    pool.wait_ge(idx_in[gk], used * 32 + 32)
                    need(pool, S["pre_ready"], g - 1)


                    carry(g * 2)
                    for j in range(2):
                        pool.indirect_dma_start(out=gath[:, gk, j, :], out_offset=None, in_=src_table[:, :],
                                                in_offset=bass.IndirectOffsetOnAxis(ap=idx_sl[:, gk, j, 0:1], axis=0)).then_inc(src_gath[gk], 16)
                q, k, _ = item(i, c - 3)
                if within(q, PAIRS):
                    pool.wait_ge(S["msg_hi_ready"], q + 1)
                    need(pool, S["sum_ps"], q - 1)
                    nc.gpsimd.tensor_tensor(msg_lo[:, k], act2[:, k], f32(msg_hi[:, k]), ALU.subtract).then_inc(S["msg_lo_ready"], 1)
                if within(g, PAIRS):
                    pool.wait_ge(src_gath[gk], used * 32 + 32)
                    carry(g * 2 + 1)
                    for j in range(2):
                        pool.indirect_dma_start(out=gath[:, gk, j, :], out_offset=None, in_=dst_table[:, :],
                                                in_offset=bass.IndirectOffsetOnAxis(ap=idx_sl[:, gk, j, 1:2], axis=0),
                                                compute_op=ALU.add).then_inc(both_gath[gk], 16)

            steps(pool, step, -3, PAIRS + 3, 6, PAIRS - 4)

        @block.scalar
        def _(act):
            nc.scalar.preload_act_table_set(EXP_LN_SET)

            def step(i, c):
                q, k, _ = item(i, c)
                first = within(q, PAIRS)
                q2, k2, _ = item(i, c - 2)
                second = within(q2, PAIRS)
                r, kr, _ = item(i, c - 1)
                if first:
                    act.wait_ge(S["pre_ready"], q + 1)
                    need(act, S["hT_ps"], q - 1)
                    nc.scalar.activation(act1[:, k], pre[:, k], ACT.Exp).then_inc(S["exp1"], 1)
                if within(r, PAIRS):
                    act.wait_ge(S["hT_ps"], r + 1)
                    need(act, S["lin2_ps"], r - 1)
                    nc.scalar.activation(hTh[:, kr], ps_h[:], ACT.Copy).then_inc(S["hT_hi"], 1)
                if second:
                    act.wait_ge(S["lin2_ps"], q2 + 1)
                    need(act, S["msg_lo_ready"], q2 - 1)
                    nc.scalar.activation(act2[:, k2], ps_2[:, k2], ACT.Exp, scale=-1.0).then_inc(S["exp2"], 1)
                if first:
                    act.wait_ge(S["inc1"], q + 1)
                    nc.scalar.activation(act1[:, k], act1[:, k], ACT.Square).then_inc(S["sq1"], 1)
                if second:
                    act.wait_ge(S["inc2"], q2 + 1)
                    nc.scalar.activation(act2[:, k2], act2[:, k2], ACT.Square).then_inc(S["sq2"], 1)
                if first:
                    act.wait_ge(S["sq1"], q + 1)
                    nc.scalar.activation(act1[:, k], act1[:, k], ACT.Ln, bias=half_col[:], scale=0.5).then_inc(S["ln1"], 1)
                if second:
                    act.wait_ge(S["sq2"], q2 + 1)
                    nc.scalar.activation(act2[:, k2], act2[:, k2], ACT.Ln, bias=half_col[:], scale=0.5).then_inc(S["ln2"], 1)
                if first:
                    act.wait_ge(S["ln1"], q + 1)
                    nc.scalar.activation(act1[:, k], act1[:, k], ACT.Exp, scale=-1.0).then_inc(S["quot1"], 1)
                if second:
                    act.wait_ge(S["ln2"], q2 + 1)
                    nc.scalar.activation(act2[:, k2], act2[:, k2], ACT.Exp, scale=-1.0).then_inc(S["quot2"], 1)

            steps(act, step, -3, PAIRS + 3, 6, PAIRS - 4)

        @block.vector
        def _(dve):
            def step(i, c):
                q, k, _ = item(i, c)
                first = within(q, PAIRS)
                q2, k2, _ = item(i, c - 2)
                second = within(q2, PAIRS)
                a, _, _ = item(i, c - 4)
                if within(a, PAIRS):
                    dve.wait_ge(S["sum_ps"], a + 1)
                    for j in range(2):
                        b = dve.value_load(block_i[0:1, bass.ds(a * 2 + j, 1)], min_val=0, max_val=BLOCKS - 1)
                        rows = agg[:, bass.ds(b, 1), :].rearrange("p a d -> p (a d)")
                        need(dve, S["summed"], a * 2 + j)
                        nc.vector.tensor_tensor(rows, rows, ps_1[0:NB, j, :], ALU.add).then_inc(S["summed"], 1)
                n, kn, _ = item(i, c + 1)
                if within(n, PAIRS):
                    dve.wait_ge(S["eaT_ps"], n + 1)
                    need(dve, S["lin1_ps"], n - 1)
                    nc.vector.tensor_copy(eaT[:, kn], ps_1[:, :, 0:P]).then_inc(S["eaT_ready"], 1)
                if first:
                    dve.wait_ge(S["exp1"], q + 1)
                    nc.vector.tensor_scalar(act1[:, k], act1[:, k], EXP_MAX, 1.0, ALU.min, ALU.add).then_inc(S["inc1"], 1)
                r, kr, _ = item(i, c - 1)
                if within(r, PAIRS):
                    dve.wait_ge(S["hT_hi"], r + 1)
                    nc.vector.tensor_tensor(hTl[:, kr], ps_h[:], f32(hTh[:, kr]), ALU.subtract).then_inc(S["hT_lo"], 1)
                if second:
                    dve.wait_ge(S["exp2"], q2 + 1)
                    nc.vector.tensor_scalar(act2[:, k2], act2[:, k2], EXP_MAX, 1.0, ALU.min, ALU.add).then_inc(S["inc2"], 1)
                if within(n, PAIRS):
                    dve.wait_ge(S["lin1_ps"], n + 1)
                    dve.wait_ge(both_gath[kn], item(i, c + 1)[2] * 32 + 32)
                    need(dve, S["h_ready"], n - 1)
                    nc.vector.tensor_tensor(pre[:, kn], ps_1[:], gath[:, kn], ALU.add).then_inc(S["pre_ready"], 1)
                l, kl, used = item(i, c + 2)
                if within(l, PAIRS):
                    dve.wait_ge(ea_in[kl], used * 32 + 32)
                    dve.wait_ge(idx_in[kl], used * 32 + 32)
                    need(dve, S["eaT_ps"], l - 1)
                    nc.vector.tensor_copy(ea_hl[:, kl, :, 0:EDIM], ea_sl[:, kl]).then_inc(S["ea_hi"], 1)
                    nc.vector.tensor_tensor(dloc[:, bass.ds(l * 2, 2)], idx_sl[:, kl, :, 2], block_off[:, bass.ds(l * 2, 2)], ALU.subtract)
                    dve.wait_ge(S["ea_hi"], l + 1)
                    nc.vector.tensor_tensor(ea_hl[:, kl, :, EDIM:2 * EDIM], ea_sl[:, kl], f32(ea_hl[:, kl, :, 0:EDIM]), ALU.subtract).then_inc(S["split"], 1)
                if second:
                    dve.wait_ge(S["split"], q2 + 1)
                    need(dve, S["sum_ps"], q2 - 1)
                    for j in range(2):
                        ins = nc.vector.tensor_scalar(onehot[:, k2, j, :], iota_n[:], dloc[:, bass.ds(q2 * 2 + j, 1)], None, ALU.is_equal)
                    ins.then_inc(S["onehot_ready"], 1)
                if first:
                    dve.wait_ge(S["quot1"], q + 1)
                    nc.vector.scalar_tensor_tensor(out=act1[:, k], in0=act1[:, k], scalar=1.0, in1=pre[:, k],
                                                   op0=ALU.subtract, op1=ALU.mult).then_inc(S["h_ready"], 1)
                if second:
                    dve.wait_ge(S["quot2"], q2 + 1)
                    nc.vector.scalar_tensor_tensor(out=act2[:, k2], in0=act2[:, k2], scalar=1.0, in1=ps_2[:, k2],
                                                   op0=ALU.subtract, op1=ALU.mult).then_inc(S["msg_ready"], 1)
                    dve.wait_ge(S["msg_ready"], q2 + 1)
                    nc.vector.tensor_copy(msg_hi[:, k2], act2[:, k2]).then_inc(S["msg_hi_ready"], 1)

            steps(dve, step, -3, PAIRS + 3, 6, PAIRS - 4)

        @block.tensor
        def _(pe):
            def step(i, c):
                n, kn, _ = item(i, c + 1)
                r, kr, _ = item(i, c - 1)
                if within(n, PAIRS):
                    pe.wait_ge(S["split"], n + 1)
                    need(pe, S["summed"], (n - 4) * 2)
                    for j in range(2):
                        ins = nc.tensor.transpose(ps_1[:, j, 0:P], f32(ea_hl[:, kn, j, :]), ident[:])
                    ins.then_inc(S["eaT_ps"], 1)
                if within(r, PAIRS):
                    pe.wait_ge(S["h_ready"], r + 1)
                    need(pe, S["hT_lo"], r)
                    for j in range(2):
                        for d in range(KC):
                            ins = nc.tensor.transpose(ps_h[:, j, d * P:(d + 1) * P], act1[:, kr, j, d * P:(d + 1) * P], ident[:])
                    ins.then_inc(S["hT_ps"], 1)
                if within(n, PAIRS):
                    pe.wait_ge(S["eaT_ready"], n + 1)
                    for j in range(2):
                        nc.tensor.matmul(ps_1[:, j, :], eaT[:, kn, j, :], Wch[:], start=True, stop=False)
                        ins = nc.tensor.matmul(ps_1[:, j, :], eaT[:, kn, j, :], Wcl[:], start=False, stop=True)
                    ins.then_inc(S["lin1_ps"], 1)
                if within(r, PAIRS):
                    need(pe, S["msg_ready"], r - 1)
                    for j in range(2):
                        nc.tensor.matmul(ps_2[:, kr, j, :], minus_r[:], bias_r[:, 1, :], start=True, stop=False)
                    pe.wait_ge(S["hT_hi"], r + 1)
                    for j in range(2):
                        for d in range(KC):
                            hi = hTh[:, kr, j, d * P:(d + 1) * P]
                            nc.tensor.matmul(ps_2[:, kr, j, :], hi, W2h[:, d, :], start=False, stop=False)
                            nc.tensor.matmul(ps_2[:, kr, j, :], hi, W2l[:, d, :], start=False, stop=False)
                    pe.wait_ge(S["hT_lo"], r + 1)
                    for j in range(2):
                        for d in range(KC):
                            lo = hTl[:, kr, j, d * P:(d + 1) * P]
                            ins = nc.tensor.matmul(ps_2[:, kr, j, :], lo, W2h[:, d, :], start=False, stop=(d == KC - 1))
                    ins.then_inc(S["lin2_ps"], 1)
                m, km, _ = item(i, c - 3)
                if within(m, PAIRS):
                    need(pe, S["summed"], m * 2)
                    pe.wait_ge(S["onehot_ready"], m + 1)
                    pe.wait_ge(S["msg_lo_ready"], m + 1)
                    pe.wait_ge(S["pre_ready"], min(m + 5, PAIRS) if isinstance(m, int) else m + 5)
                    for j in range(2):
                        nc.tensor.matmul(ps_1[0:NE, j, :], onehot[:, km, j, :], msg_hi[:, km, j, :], start=True, stop=False)
                        ins = nc.tensor.matmul(ps_1[0:NE, j, :], onehot[:, km, j, :], msg_lo[:, km, j, :], start=False, stop=True)
                    ins.then_inc(S["sum_ps"], 1)

            steps(pe, step, -3, PAIRS + 3, 6, PAIRS - 4)
    nc.clear_and_free_semaphores(sems)
    nc.all_engine_barrier()


def node_phase(nc, T):
    ident, minus_r, plus_r, bias_r = T["ident"], T["minus_r"], T["plus_r"], T["bias_r"]
    half_col, eps_col, agg, xn_all = T["half_col"], T["eps_col"], T["agg"], T["xn_all"]
    x1_all, xlTh, xlTl = T["x1_all"], T["xlTh"], T["xlTl"]
    KK = 2 * KC

    ctx = ExitStack()
    with ctx:
        def sb(name, shape, dt=F32):
            return ctx.enter_context(nc.sbuf_tensor(name, shape, dt))

        def pb(name, shape):
            return ctx.enter_context(nc.psum_tensor(name, shape, F32))

        def sem(name):
            return ctx.enter_context(nc.semaphore("n_" + name))

        w_raw = sb("w_raw", [P, KK, HID])
        w3h = sb("w3h", [P, KK, HID], F32R)
        w3l = sb("w3l", [P, KK, HID], F32R)
        w4h = sb("w4h", [P, KC, HID], F32R)
        w4l = sb("w4l", [P, KC, HID], F32R)
        gamma_b = sb("gamma_b", [NB, HID])
        beta_b = sb("beta_b", [NB, HID])
        x_sl = sb("x_sl", [NB, 2, HID])
        cat_op = sb("cat_op", [NE, 2, 2 * HID])
        catTh = sb("catTh", [P, 2, KK * NE], F32R)
        catTl = sb("catTl", [P, 2, KK * NE], F32R)
        u = sb("u", [NE, 2, HID])
        uTh = sb("uTh", [P, 2, KC * NE], F32R)
        uTl = sb("uTl", [P, 2, KC * NE], F32R)
        y = sb("y", [NB, 2, HID])
        xl_op = sb("xl_op", [NE, 2, HID])
        stats = sb("n_stats", [NB, 6])
        mv = sb("n_mv", [NB, 2, 2])
        rs = sb("n_rs", [NB, 2, 5])

        ps_c = pb("ps_c", [P, 2, 512])
        ps_u = pb("ps_u", [P, 2, 512])
        ps_v = pb("ps_v", [P, 512])
        ps_o = pb("ps_o", [P, 2, 512])
        ps_x = pb("ps_x", [P, 512])

        names = ("w3_in w4_in gb_in w3_hi w3_lo w4_hi w4_lo zeroed op_ready cat_ps cat_hi cat_lo lin_ps bounded exp sq ln quot "
                 "u_ready uT_ps uT_hi uT_lo out_ps y_ready xb_ready post var_y rstd_y var_x rstd_x xl_ready x1_done xlT_ps xlT_hi xlT_lo").split()
        S = {n: sem(n) for n in names}
        x_in = [sem(f"x_in{k}") for k in range(2)]
        block = ctx.enter_context(nc.Block())
        FIRST, LAST, LO, HI = -1, BLOCKS + 1, 5, BLOCKS - 2

        @block.sync
        def _(sp):
            sp.dma_start(w_raw[:], T["W3"].rearrange("(k p) n -> p k n", p=P)).then_inc(S["w3_in"], 16)
            sp.dma_start(gamma_b[:], T["gamma"].rearrange("(a n) -> a n", a=1).to_broadcast([NB, HID])).then_inc(S["gb_in"], 16)
            sp.dma_start(beta_b[:], T["beta"].rearrange("(a n) -> a n", a=1).to_broadcast([NB, HID])).then_inc(S["gb_in"], 16)
            sp.wait_ge(S["w3_lo"], KC)
            sp.dma_start(w_raw[:, 0:KC, :], T["W4"].rearrange("(k p) n -> p k n", p=P)).then_inc(S["w4_in"], 16)
            x_rows = T["x"].rearrange("(i p) d -> i p d", p=NB)

            def step(i, c):
                t, k, _ = item(i, c + 1)
                if within(t, BLOCKS):
                    need(sp, S["x1_done"], t - 1)
                    sp.dma_start(x_sl[:, k, :], x_rows[bass.ds(t, 1)].rearrange("a p d -> (a p) d")).then_inc(x_in[k], 16)

            steps(sp, step, FIRST, LAST, LO, HI)

        @block.gpsimd
        def _(pool):
            nc.gpsimd.memset(cat_op[:], 0.0).then_inc(S["zeroed"], 1)
            nc.gpsimd.memset(u[:], 0.0).then_inc(S["zeroed"], 1)
            nc.gpsimd.memset(xl_op[:], 0.0).then_inc(S["zeroed"], 1)
            pool.wait_ge(S["zeroed"], 3)

            def step(i, c):
                t, k, _ = item(i, c + 1)
                if within(t, BLOCKS):
                    need(pool, S["cat_ps"], t - 1)
                    nc.gpsimd.tensor_copy(cat_op[0:NB, k, 0:HID], xn_all[:, bass.ds(t, 1), :].rearrange("p a d -> p (a d)"))
                    nc.gpsimd.tensor_copy(cat_op[0:NB, k, HID:2 * HID], agg[:, bass.ds(t, 1), :].rearrange("p a d -> p (a d)")).then_inc(S["op_ready"], 1)

            steps(pool, step, FIRST, LAST, LO, HI)

        @block.scalar
        def _(act):
            nc.scalar.preload_act_table_set(EXP_LN_SET)
            act.wait_ge(S["w3_in"], 16)
            for q in range(KK):
                nc.scalar.activation(w3h[:, q, :], w_raw[:, q, :], ACT.Copy).then_inc(S["w3_hi"], 1)
            act.wait_ge(S["w4_in"], 16)
            for q in range(KC):
                nc.scalar.activation(w4h[:, q, :], w_raw[:, q, :], ACT.Copy).then_inc(S["w4_hi"], 1)

            def rstd(n, t, var, ready):
                act.wait_ge(S[var], t + 1)
                nc.scalar.activation(rs[:, n, 0:1], mv[:, n, 1:2], ACT.Ln, bias=eps_col[0:NB, :]).then_inc(S[ready], 1)
                act.wait_ge(S[ready], t * 2 + 1)
                nc.scalar.activation(rs[:, n, 1:2], rs[:, n, 0:1], ACT.Exp, scale=-0.5).then_inc(S[ready], 1)

            def step(i, c):
                p, kp, _ = item(i, c - 2)
                if within(p, BLOCKS):
                    rstd(0, p, "var_y", "rstd_y")
                    rstd(1, p, "var_x", "rstd_x")
                t, k, _ = item(i, c)
                if within(t, BLOCKS):
                    act.wait_ge(S["bounded"], t + 1)
                    nc.scalar.activation(u[0:NB, k, :], u[0:NB, k, :], ACT.Exp).then_inc(S["exp"], 1)
                v, kv, _ = item(i, c - 1)
                if within(v, BLOCKS):
                    act.wait_ge(S["uT_ps"], v + 1)
                    need(act, S["out_ps"], v - 1)
                    nc.scalar.activation(uTh[:, kv, :], ps_v[:, 0:KC * NE], ACT.Copy).then_inc(S["uT_hi"], 1)
                if within(t, BLOCKS):
                    act.wait_ge(S["exp"], t + 1)
                    nc.scalar.activation(u[0:NB, k, :], u[0:NB, k, :], ACT.Square, bias=1.0).then_inc(S["sq"], 1)
                n, kn, _ = item(i, c + 1)
                if within(n, BLOCKS):
                    act.wait_ge(S["cat_ps"], n + 1)
                    need(act, S["lin_ps"], n - 1)
                    nc.scalar.activation(catTh[:, kn, :].rearrange("p (a n) -> p a n", a=2), ps_c[:, :, 0:KC * NE], ACT.Copy).then_inc(S["cat_hi"], 1)
                if within(t, BLOCKS):
                    act.wait_ge(S["sq"], t + 1)
                    nc.scalar.activation(u[0:NB, k, :], u[0:NB, k, :], ACT.Ln, bias=half_col[0:NB, :], scale=0.5).then_inc(S["ln"], 1)
                    act.wait_ge(S["ln"], t + 1)
                    nc.scalar.activation(u[0:NB, k, :], u[0:NB, k, :], ACT.Exp, scale=-1.0).then_inc(S["quot"], 1)
                if within(p, BLOCKS):
                    act.wait_ge(S["xlT_ps"], p + 1)
                    nc.scalar.activation(xlTh[:, :, bass.ds(p * NE, NE)], ps_x[:, 0:KC * NE].rearrange("p (q n) -> p q n", q=KC), ACT.Copy).then_inc(S["xlT_hi"], 1)

            steps(act, step, FIRST, LAST, LO, HI)

        @block.vector
        def _(dve):
            for q in range(KK):
                dve.wait_ge(S["w3_hi"], q + 1)
                nc.vector.tensor_tensor(w3l[:, q, :], w_raw[:, q, :], f32(w3h[:, q, :]), ALU.subtract).then_inc(S["w3_lo"], 1)
            for q in range(KC):
                dve.wait_ge(S["w4_hi"], q + 1)
                nc.vector.tensor_tensor(w4l[:, q, :], w_raw[:, q, :], f32(w4h[:, q, :]), ALU.subtract).then_inc(S["w4_lo"], 1)
            dve.wait_ge(S["gb_in"], 32)
            dve.wait_ge(S["zeroed"], 3)

            PER = 12

            def step(i, c):
                p, kp, used = item(i, c - 2)
                if within(p, BLOCKS):
                    def link(m, ins):
                        ins.then_inc(S["post"], 1)
                        dve.wait_ge(S["post"], p * PER + m)

                    def newton(n, ready, m):
                        dve.wait_ge(S[ready], p * 2 + 2)
                        link(m, nc.vector.tensor_tensor(rs[:, n, 2:3], rs[:, n, 1:2], rs[:, n, 1:2], ALU.mult))
                        link(m + 1, nc.vector.scalar_tensor_tensor(out=rs[:, n, 3:4], in0=mv[:, n, 1:2], scalar=EPS, in1=rs[:, n, 2:3], op0=ALU.add, op1=ALU.mult))
                        link(m + 2, nc.vector.tensor_scalar(rs[:, n, 4:5], rs[:, n, 3:4], -0.5, 1.5, ALU.mult, ALU.add))
                        link(m + 3, nc.vector.tensor_tensor(rs[:, n, 2:3], rs[:, n, 1:2], rs[:, n, 4:5], ALU.mult))

                    tile = (slice(None), bass.ds(p, 1), slice(None))
                    yk = y[:, kp, :]
                    xk = x_sl[:, kp, :]
                    dve.wait_ge(S["out_ps"], p + 1)
                    nc.vector.tensor_tensor(yk, xn_all[tile].rearrange("p a d -> p (a d)"), ps_o[0:NB, kp, :], ALU.subtract).then_inc(S["y_ready"], 1)
                    dve.wait_ge(S["y_ready"], p + 1)
                    link(1, nc.vector.bn_stats(out=stats[:], in_=yk))
                    dve.wait_ge(x_in[kp], used * 16 + 16)
                    nc.vector.tensor_tensor(xk, xk, beta_b[:], ALU.add).then_inc(S["xb_ready"], 1)
                    nc.vector.bn_aggr(out=mv[:, 0, :], in_=stats[:]).then_inc(S["var_y"], 1)
                    newton(0, "rstd_y", 2)
                    dve.wait_ge(S["xb_ready"], p + 1)
                    link(6, nc.vector.scalar_tensor_tensor(out=yk, in0=yk, scalar=mv[:, 0, 0:1], in1=gamma_b[:], op0=ALU.subtract, op1=ALU.mult))
                    link(7, nc.vector.scalar_tensor_tensor(out=yk, in0=yk, scalar=rs[:, 0, 2:3], in1=xk, op0=ALU.mult, op1=ALU.add))
                    link(8, nc.vector.bn_stats(out=stats[:], in_=yk))
                    nc.vector.tensor_copy(x1_all[tile].rearrange("p a d -> p (a d)"), yk).then_inc(S["x1_done"], 1)
                    nc.vector.bn_aggr(out=mv[:, 1, :], in_=stats[:]).then_inc(S["var_x"], 1)
                    newton(1, "rstd_x", 9)
                    need(dve, S["xlT_ps"], p - 1)
                    nc.vector.tensor_scalar(xl_op[0:NB, kp, :], yk, mv[:, 1, 0:1], rs[:, 1, 2:3], ALU.subtract, ALU.mult).then_inc(S["xl_ready"], 1)
                t, k, _ = item(i, c)
                if within(t, BLOCKS):
                    dve.wait_ge(S["lin_ps"], t + 1)
                    need(dve, S["uT_ps"], t - 1)
                    nc.vector.tensor_scalar(u[0:NB, k, :], ps_u[0:NB, k, :], X_MAX, None, ALU.min).then_inc(S["bounded"], 1)
                v, kv, _ = item(i, c - 1)
                if within(v, BLOCKS):
                    dve.wait_ge(S["uT_hi"], v + 1)
                    nc.vector.tensor_tensor(uTl[:, kv, :], ps_v[:, 0:KC * NE], f32(uTh[:, kv, :]), ALU.subtract).then_inc(S["uT_lo"], 1)
                n, kn, _ = item(i, c + 1)
                if within(n, BLOCKS):
                    dve.wait_ge(S["cat_hi"], n + 1)
                    nc.vector.tensor_tensor(catTl[:, kn, :].rearrange("p (a n) -> p a n", a=2), ps_c[:, :, 0:KC * NE],
                                            f32(catTh[:, kn, :]).rearrange("p (a n) -> p a n", a=2), ALU.subtract).then_inc(S["cat_lo"], 1)
                if within(p, BLOCKS):
                    dve.wait_ge(S["xlT_hi"], p + 1)
                    cols = (slice(None), slice(None), bass.ds(p * NE, NE))
                    nc.vector.tensor_tensor(xlTl[cols], ps_x[:, 0:KC * NE].rearrange("p (q n) -> p q n", q=KC), f32(xlTh[cols]), ALU.subtract).then_inc(S["xlT_lo"], 1)
                if within(t, BLOCKS):
                    dve.wait_ge(S["quot"], t + 1)
                    nc.vector.scalar_tensor_tensor(out=u[0:NB, k, :], in0=u[0:NB, k, :], scalar=1.0, in1=ps_u[0:NB, k, :],
                                                   op0=ALU.subtract, op1=ALU.mult).then_inc(S["u_ready"], 1)

            steps(dve, step, FIRST, LAST, LO, HI)

        @block.tensor
        def _(pe):
            pe.wait_ge(S["w3_lo"], KK)

            def step(i, c):
                t, k, _ = item(i, c)
                if within(t, BLOCKS):
                    pe.wait_ge(S["cat_lo"], t + 1)
                    need(pe, S["u_ready"], t - 1)
                    o = ps_u[0:NE, k, :]
                    nc.tensor.matmul(o, plus_r[:, 0:NE], bias_r[:, 2, :], start=True, stop=False)
                    for q in range(KK):
                        hi, lo = catTh[:, k, q * NE:(q + 1) * NE], catTl[:, k, q * NE:(q + 1) * NE]
                        nc.tensor.matmul(o, hi, w3h[:, q, :], start=False, stop=False)
                        nc.tensor.matmul(o, hi, w3l[:, q, :], start=False, stop=False)
                        ins = nc.tensor.matmul(o, lo, w3h[:, q, :], start=False, stop=(q == KK - 1))
                    ins.then_inc(S["lin_ps"], 1)
                v, kv, _ = item(i, c - 1)
                if within(v, BLOCKS):
                    pe.wait_ge(S["u_ready"], v + 1)
                    need(pe, S["uT_lo"], v)
                    for q in range(KC):
                        ins = nc.tensor.transpose(ps_v[:, q * NE:(q + 1) * NE], u[:, kv, q * P:(q + 1) * P], ident[0:NE, 0:NE])
                    ins.then_inc(S["uT_ps"], 1)
                n, kn, _ = item(i, c + 1)
                if within(n, BLOCKS):
                    pe.wait_ge(S["op_ready"], n + 1)
                    need(pe, S["cat_lo"], n)
                    for q in range(KK):
                        ins = nc.tensor.transpose(ps_c[:, q // KC, (q % KC) * NE:(q % KC + 1) * NE], cat_op[:, kn, q * P:(q + 1) * P], ident[0:NE, 0:NE])
                    ins.then_inc(S["cat_ps"], 1)
                if within(v, BLOCKS):
                    pe.wait_ge(S["w4_lo"], KC)
                    pe.wait_ge(S["uT_lo"], v + 1)
                    need(pe, S["y_ready"], v - 1)
                    o = ps_o[0:NE, kv, :]
                    nc.tensor.matmul(o, minus_r[:, 0:NE], bias_r[:, 3, :], start=True, stop=False)
                    for q in range(KC):
                        hi, lo = uTh[:, kv, q * NE:(q + 1) * NE], uTl[:, kv, q * NE:(q + 1) * NE]
                        nc.tensor.matmul(o, hi, w4h[:, q, :], start=False, stop=False)
                        nc.tensor.matmul(o, hi, w4l[:, q, :], start=False, stop=False)
                        ins = nc.tensor.matmul(o, lo, w4h[:, q, :], start=False, stop=(q == KC - 1))
                    ins.then_inc(S["out_ps"], 1)
                p, kp, _ = item(i, c - 2)
                if within(p, BLOCKS):
                    pe.wait_ge(S["xl_ready"], p + 1)
                    need(pe, S["xlT_lo"], p)
                    for q in range(KC):
                        ins = nc.tensor.transpose(ps_x[:, q * NE:(q + 1) * NE], xl_op[:, kp, q * P:(q + 1) * P], ident[0:NE, 0:NE])
                    ins.then_inc(S["xlT_ps"], 1)

            steps(pe, step, FIRST, LAST, LO, HI)


def ffn_phase(nc, T):
    ident, ones, x1_all, xlTh, xlTl, mask_scr, out = T["ident"], T["ones"], T["x1_all"], T["xlTh"], T["xlTl"], T["mask_scr"], T["out"]
    E, FC = EXPERTS, FFN // P
    TOK = BLOCKS * NE
    NCH = 3
    CW = TOK // NCH

    ctx = ExitStack()
    with ctx:
        def sb(name, shape, dt=F32):
            return ctx.enter_context(nc.sbuf_tensor(name, shape, dt))

        def pb(name, shape):
            return ctx.enter_context(nc.psum_tensor(name, shape, F32))

        def sem(name):
            return ctx.enter_context(nc.semaphore("f_" + name))

        gate = sb("gate", [E, HID])
        gateTh = sb("gateTh", [P, KC, E], F32R)
        gateTl = sb("gateTl", [P, KC, E], F32R)
        logT = sb("logT", [E, TOK])
        row_order = sb("row_order", [NE, E])
        valid = sb("valid", [NE, 1])
        lg = sb("lg", [NE, BLOCKS, E])
        best = sb("best", [NE, 4, BLOCKS])
        hot1 = sb("hot1", [NE, BLOCKS, E])
        hot2 = sb("hot2", [NE, BLOCKS, E])
        rank_a = sb("rank_a", [NE, BLOCKS, E])
        rank_b = sb("rank_b", [NE, BLOCKS, E])
        wt = sb("wt", [NE, 4, BLOCKS])
        mask = sb("mask", [NE, BLOCKS, E])
        gw = sb("gw", [NE, BLOCKS, E])
        msum = sb("msum", [NE, E])
        inv = sb("inv", [P, E])
        maskT = sb("maskT", [E, TOK])
        gwT = sb("gwT", [E, TOK])
        w1_raw = sb("f_w1_raw", [P, 2, FC, HID])
        w2_raw = sb("f_w2_raw", [P, 2, KC, FFN])
        w1Th = sb("w1Th", [P, 2, FC, HID], F32R)
        w1Tl = sb("w1Tl", [P, 2, FC, HID], F32R)
        mask_b = sb("mask_b", [P, 2, TOK])
        hs = sb("hs", [P, FC, TOK])
        junk_h = sb("junk_h", [P, TOK])
        junk_y = sb("junk_y", [P, FFN])
        hsum = sb("hsum", [P, 2, FC])
        hm = sb("hm", [P, 2, FC])
        hm_b = sb("hm_b", [P, 2, FC, P])
        y_col = sb("y_col", [P, 2, KC])
        yT = sb("yT", [P, KC, E])
        y = sb("y_mean", [E, HID])
        res = sb("res", [NB, 2, HID])

        ps_hh = pb("ps_hh", [P, FC, NCH, 512])
        ps_w = pb("ps_w", [P, 512])
        ps_b = pb("ps_b2", [P, 512])

        names = ("gate_in const gateT_ps gate_hi gate_lo log_ps log_out lg_ps step a_step d_step mask_ready maskT_ps maskT_out "
                 "mask_stored gw_ps gw_out cnt_ps w1T_ps w1T_hi w1T_lo h_ps h_act h_sum hm_step y_step hm_ready mean_ps y_done yT_ps y_out res_ps res_done").split()
        S = {n: sem(n) for n in names}
        w1_in, w2_in, mask_in, res_out = ([sem(f"{n}{k}") for k in range(2)] for n in ("w1_in", "w2_in", "mask_in", "res_out"))
        block = ctx.enter_context(nc.Block())
        FIRST, LAST, LO, HI = -1, E, 3, E - 2

        def flat(ap):
            return ap.rearrange("p b e -> p (b e)")

        @block.sync
        def _(sp):
            sp.dma_start(gate[:], T["gate_w"]).then_inc(S["gate_in"], 16)
            w1_rows = T["w1"].rearrange("e (c p) d -> e p c d", p=P)
            w2_rows = T["w2"].rearrange("e (q p) f -> e p q f", p=P)

            def step(i, c):
                e, k, used = item(i, c + 1)
                if within(e, E):
                    need(sp, S["w1T_ps"], (e - 1) * FC)
                    sp.dma_start(w1_raw[:, k], w1_rows[bass.ds(e, 1)].rearrange("a p c d -> (a p) c d")).then_inc(w1_in[k], 16)
                e, k, used = item(i, c)
                if within(e, E):
                    if isinstance(e, int) and e == 0:
                        sp.wait_ge(S["maskT_out"], 1)
                        sp.dma_start(mask_scr, maskT[:]).then_inc(S["mask_stored"], 16)
                        sp.wait_ge(S["mask_stored"], 16)
                    need(sp, S["h_sum"], (e - 1) * FC)
                    sp.dma_start(mask_b[:, k], mask_scr[bass.ds(e, 1), :].to_broadcast([P, TOK])).then_inc(mask_in[k], 16)
                    need(sp, S["y_done"], e - 1)
                    sp.dma_start(w2_raw[:, k], w2_rows[bass.ds(e, 1)].rearrange("a p q f -> (a p) q f")).then_inc(w2_in[k], 16)

            steps(sp, step, FIRST, LAST, LO, HI)
            for t in range(BLOCKS):
                sp.wait_ge(S["res_done"], t + 1)
                sp.dma_start(out[t * NB:(t + 1) * NB, :], res[:, t % 2, :]).then_inc(res_out[t % 2], 16)
            for k in range(2):
                sp.wait_ge(res_out[k], 16 * (BLOCKS // 2))

        @block.gpsimd
        def _(pool):
            nc.gpsimd.iota(row_order[:], [[-1, E]], base=E, channel_multiplier=0, allow_small_or_imprecise_dtypes=True).then_inc(S["const"], 1)
            nc.gpsimd.memset(valid[:], 1.0).then_inc(S["const"], 1)
            pool.wait_ge(S["const"], 2)
            nc.gpsimd.affine_select(out=valid[:], in_=valid[:], compare_op=ALU.not_equal, fill=0.0, base=-NB,
                                    pattern=[[0, 1]], channel_multiplier=1).then_inc(S["const"], 1)

        @block.scalar
        def _(act):
            act.wait_ge(S["gateT_ps"], 1)
            nc.scalar.activation(gateTh[:].rearrange("p q e -> p (q e)"), ps_w[:, 0:KC * E], ACT.Copy).then_inc(S["gate_hi"], 1)
            act.wait_ge(S["log_ps"], 1)
            nc.scalar.activation(logT[:].rearrange("e (n c) -> e n c", n=NCH), ps_hh[0:E, 0, :, 0:CW], ACT.Copy).then_inc(S["log_out"], 1)
            act.wait_ge(S["d_step"], 1)
            nc.scalar.activation(wt[:, 1, :], wt[:, 0, :], ACT.Exp).then_inc(S["a_step"], 1)
            act.wait_ge(S["maskT_ps"], 1)
            nc.scalar.activation(maskT[:].rearrange("e (n c) -> e n c", n=NCH), ps_hh[0:E, 0, :, 0:CW], ACT.Copy).then_inc(S["maskT_out"], 1)
            act.wait_ge(S["gw_ps"], 1)
            nc.scalar.activation(gwT[:].rearrange("e (n c) -> e n c", n=NCH), ps_hh[0:E, 1, :, 0:CW], ACT.Copy).then_inc(S["gw_out"], 1)

            def step(i, c):
                e, k, _ = item(i, c)
                n, kn, _ = item(i, c + 1)
                for f in range(FC):
                    if within(e, E):
                        act.wait_ge(S["h_ps"], e * FC + (f + 1))
                        need(act, S["h_sum"], (e - 1) * FC + (f + 1))
                        nc.scalar.activation(hs[:, f].rearrange("p (n c) -> p n c", n=NCH), ps_hh[:, f, :, 0:CW], ACT.Silu).then_inc(S["h_act"], 1)
                    if within(n, E):
                        act.wait_ge(S["w1T_ps"], n * FC + (f + 1))
                        need(act, S["h_ps"], (n - 2) * FC + (f + 1))
                        nc.scalar.activation(w1Th[:, kn, f, :], ps_w[:], ACT.Copy).then_inc(S["w1T_hi"], 1)

            steps(act, step, FIRST, LAST, LO, HI)
            act.wait_ge(S["yT_ps"], 1)
            nc.scalar.activation(y[:], ps_w[0:E, :], ACT.Copy).then_inc(S["y_out"], 1)

        @block.vector
        def _(dve):
            dve.wait_ge(S["gate_hi"], 1)
            nc.vector.tensor_tensor(gateTl[:].rearrange("p q e -> p (q e)"), ps_w[:, 0:KC * E], f32(gateTh[:]).rearrange("p q e -> p (q e)"), ALU.subtract).then_inc(S["gate_lo"], 1)
            c = Count(dve, S["step"])

            def spread(ap):
                return ap.unsqueeze(2).to_broadcast([NE, BLOCKS, E])

            order = row_order[:].unsqueeze(1).to_broadcast([NE, BLOCKS, E])
            dve.wait_ge(S["const"], 3)
            dve.wait_ge(S["lg_ps"], 1)
            c.step(nc.vector.tensor_copy(flat(lg[:]), ps_b[0:NE, 0:BLOCKS * E]))

            def largest(src, n, hot):
                c.step(nc.vector.tensor_reduce(out=best[:, n, :], in_=src, axis=AX_X, op=ALU.max))
                c.step(nc.vector.tensor_tensor(rank_a[:], src, spread(best[:, n, :]), ALU.is_equal))
                c.step(nc.vector.tensor_tensor(rank_a[:], rank_a[:], order, ALU.mult))
                c.step(nc.vector.tensor_reduce(out=best[:, 2 + n, :], in_=rank_a[:], axis=AX_X, op=ALU.max))
                c.step(nc.vector.tensor_tensor(hot, order, spread(best[:, 2 + n, :]), ALU.is_equal))

            largest(lg[:], 0, hot1[:])
            c.step(nc.vector.scalar_tensor_tensor(out=flat(rank_b[:]), in0=flat(hot1[:]), scalar=-1e30, in1=flat(lg[:]), op0=ALU.mult, op1=ALU.add))
            largest(rank_b[:], 1, hot2[:])
            nc.vector.tensor_tensor(wt[:, 0, :], best[:, 1, :], best[:, 0, :], ALU.subtract).then_inc(S["d_step"], 1)
            c.step(nc.vector.tensor_tensor(mask[:], hot1[:], hot2[:], ALU.add))
            nc.vector.tensor_scalar(flat(mask[:]), flat(mask[:]), valid[:, 0:1], None, ALU.mult).then_inc(S["mask_ready"], 1)
            dve.wait_ge(S["mask_ready"], 1)
            nc.vector.tensor_reduce(out=msum[:], in_=mask[:].rearrange("p b e -> p e b"), axis=AX_X, op=ALU.add).then_inc(S["mask_ready"], 1)
            dve.wait_ge(S["a_step"], 1)
            c.step(nc.vector.tensor_scalar(wt[:, 2, :], wt[:, 1, :], 1.0, None, ALU.add))
            c.step(nc.vector.reciprocal(wt[:, 3, :], wt[:, 2, :]))
            c.step(nc.vector.tensor_tensor(wt[:, 2, :], wt[:, 3, :], wt[:, 1, :], ALU.mult))
            c.inc(nc.vector.tensor_tensor(hot1[:], hot1[:], spread(wt[:, 3, :]), ALU.mult))
            c.step(nc.vector.tensor_tensor(hot2[:], hot2[:], spread(wt[:, 2, :]), ALU.mult))
            nc.vector.tensor_tensor(gw[:], hot1[:], hot2[:], ALU.add).then_inc(S["mask_ready"], 1)
            dve.wait_ge(S["cnt_ps"], 1)
            c.step(nc.vector.tensor_scalar(inv[:], ps_b[:, 256:256 + E], 1.0, None, ALU.max))
            c.step(nc.vector.reciprocal(inv[:], inv[:]))

            def step(i, c):
                e, k, used = item(i, c)
                n, kn, _ = item(i, c + 1)
                o, ko, oused = item(i, c - 1)
                for f in range(FC):
                    if within(n, E):
                        dve.wait_ge(S["w1T_hi"], n * FC + (f + 1))
                        nc.vector.tensor_tensor(w1Tl[:, kn, f, :], ps_w[:], f32(w1Th[:, kn, f, :]), ALU.subtract).then_inc(S["w1T_lo"], 1)
                    if f == 0 and within(o, E):
                        dve.wait_ge(S["mean_ps"], o + 1)
                        dve.wait_ge(w2_in[ko], oused * 16 + 16)
                        for q in range(KC):
                            need(dve, S["y_step"], o * KC + q)
                            ins = nc.vector.tensor_tensor_reduce(out=junk_y[:], in0=w2_raw[:, ko, q, :], in1=ps_b[:, 0:FFN], scale=1.0, scalar=0.0,
                                                                 op0=ALU.mult, op1=ALU.add, accum_out=y_col[:, ko, q:q + 1])
                            ins.then_inc(S["y_step"], 1)
                        dve.wait_ge(S["y_step"], o * KC + KC)
                        nc.vector.tensor_copy(yT[:, :, bass.ds(o, 1)].rearrange("p q a -> p (q a)"), y_col[:, ko, :]).then_inc(S["y_done"], 1)
                    if within(e, E):
                        dve.wait_ge(S["h_act"], e * FC + (f + 1))
                        dve.wait_ge(mask_in[k], used * 16 + 16)
                        need(dve, S["h_sum"], e * FC + f)
                        nc.vector.tensor_tensor_reduce(out=junk_h[:], in0=hs[:, f, :], in1=mask_b[:, k, :], scale=1.0, scalar=0.0,
                                                       op0=ALU.mult, op1=ALU.add, accum_out=hsum[:, k, f:f + 1]).then_inc(S["h_sum"], 1)
                if within(e, E):
                    dve.wait_ge(S["h_sum"], e * FC + FC)
                    nc.vector.tensor_scalar(hm[:, k, :], hsum[:, k, :], inv[:, bass.ds(e, 1)], None, ALU.mult).then_inc(S["hm_step"], 1)
                    dve.wait_ge(S["hm_step"], e + 1)
                    for f in range(FC):
                        ins = nc.vector.tensor_scalar(hm_b[:, k, f, :], ones[:], hm[:, k, f:f + 1], None, ALU.mult)
                    ins.then_inc(S["hm_ready"], 1)

            steps(dve, step, FIRST, LAST, LO, HI)
            for t in range(BLOCKS):
                dve.wait_ge(S["res_ps"], t + 1)
                need(dve, res_out[t % 2], 16 * (t // 2))
                nc.vector.tensor_tensor(res[:, t % 2, :], x1_all[:, t, :], ps_hh[0:NB, t % 2, 0, :], ALU.add).then_inc(S["res_done"], 1)

        @block.tensor
        def _(pe):
            pe.wait_ge(S["gate_in"], 16)
            for q in range(KC):
                ins = nc.tensor.transpose(ps_w[:, q * E:(q + 1) * E], gate[:, q * P:(q + 1) * P], ident[0:E, 0:E])
            ins.then_inc(S["gateT_ps"], 1)
            pe.wait_ge(S["gate_lo"], 1)
            for n in range(NCH):
                cols = slice(n * CW, (n + 1) * CW)
                for q in range(KC):
                    o = ps_hh[0:E, 0, n, 0:CW]
                    nc.tensor.matmul(o, gateTh[:, q, :], xlTh[:, q, cols], start=(q == 0), stop=False)
                    nc.tensor.matmul(o, gateTl[:, q, :], xlTh[:, q, cols], start=False, stop=False)
                    ins = nc.tensor.matmul(o, gateTh[:, q, :], xlTl[:, q, cols], start=False, stop=(q == KC - 1))
            ins.then_inc(S["log_ps"], 1)
            pe.wait_ge(S["log_out"], 1)
            for b in range(BLOCKS):
                ins = nc.tensor.transpose(ps_b[0:NE, b * E:(b + 1) * E], logT[:, b * NE:(b + 1) * NE], ident[0:E, 0:E])
            ins.then_inc(S["lg_ps"], 1)
            pe.wait_ge(S["mask_ready"], 2)
            nc.tensor.matmul(ps_b[:, 256:256 + E], ones[0:NE, :], msum[:], start=True, stop=True).then_inc(S["cnt_ps"], 1)

            def rows_of(src, f, signal):
                for b in range(BLOCKS):
                    n0, n1 = b * NE // CW, ((b + 1) * NE - 1) // CW
                    for n in range(n0, n1 + 1):
                        lo, hi = max(b * NE, n * CW), min((b + 1) * NE, (n + 1) * CW)
                        ins = nc.tensor.matmul(ps_hh[0:E, f, n, lo - n * CW:hi - n * CW], src[:, b, :],
                                               ident[0:NE, lo - b * NE:hi - b * NE], start=True, stop=True)
                ins.then_inc(S[signal], 1)

            rows_of(mask, 0, "maskT_ps")
            pe.wait_ge(S["mask_ready"], 3)
            rows_of(gw, 1, "gw_ps")
            pe.wait_ge(S["maskT_out"], 1)
            pe.wait_ge(S["gw_out"], 1)

            def step(i, c):
                e, k, _ = item(i, c)
                n, kn, nused = item(i, c + 1)
                o, ko, _ = item(i, c - 1)
                for f in range(FC):
                    if within(e, E):
                        pe.wait_ge(S["w1T_lo"], e * FC + (f + 1))
                        need(pe, S["h_act"], (e - 1) * FC + (f + 1))
                        for q in range(KC):
                            hi, lo = w1Th[:, k, f, q * P:(q + 1) * P], w1Tl[:, k, f, q * P:(q + 1) * P]
                            for w, xs in ((hi, xlTh), (hi, xlTl), (lo, xlTh)):
                                for m in range(NCH):
                                    ins = nc.tensor.matmul(ps_hh[:, f, m, 0:CW], w, xs[:, q, m * CW:(m + 1) * CW],
                                                           start=(q == 0 and w is hi and xs is xlTh), stop=(q == KC - 1 and w is lo))
                        ins.then_inc(S["h_ps"], 1)
                    if within(n, E):
                        if f == 0:
                            pe.wait_ge(w1_in[kn], nused * 16 + 16)
                        need(pe, S["w1T_lo"], n * FC + f)
                        for q in range(KC):
                            ins = nc.tensor.transpose(ps_w[:, q * P:(q + 1) * P], w1_raw[:, kn, f, q * P:(q + 1) * P], ident[:])
                        ins.then_inc(S["w1T_ps"], 1)
                    if f == 0 and within(o, E):
                        pe.wait_ge(S["hm_ready"], o + 1)
                        need(pe, S["y_done"], o)
                        for g in range(FC):
                            ins = nc.tensor.matmul(ps_b[:, g * P:(g + 1) * P], hm_b[:, ko, g, :], ident[:], start=True, stop=True)
                        ins.then_inc(S["mean_ps"], 1)

            steps(pe, step, FIRST, LAST, LO, HI)
            pe.wait_ge(S["y_done"], E)
            for q in range(KC):
                ins = nc.tensor.transpose(ps_w[0:E, q * P:(q + 1) * P], yT[:, q, :], ident[:])
            ins.then_inc(S["yT_ps"], 1)
            pe.wait_ge(S["y_out"], 1)
            for t in range(BLOCKS):
                need(pe, S["res_done"], t - 1)
                nc.tensor.matmul(ps_hh[0:NB, t % 2, 0, :], gwT[:, t * NE:t * NE + NB], y[:], start=True, stop=True).then_inc(S["res_ps"], 1)


_INS = ["x", "src", "dst", "edge_attr_64", "L0_gnn_W1", "L0_gnn_b1", "L0_gnn_W2", "L0_gnn_b2", "L0_gnn_W3", "L0_gnn_b3",
        "L0_gnn_W4", "L0_gnn_b4", "L0_gnn_gamma", "L0_gnn_beta", "L0_ffn_gate_weight", "L0_ffn_w1", "L0_ffn_w2"]
_OUTS = [((NODES, HID), "float32")]


def kernel(**inputs):
    import numpy as _np
    import concourse.bacc as _bacc
    from concourse import mybir as _mybir
    from concourse.bass_utils import run_bass_kernel_spmd as _run

    nc = _bacc.Bacc("TRN2", target_bir_lowering=False, num_devices=1)
    arrays, args = {}, []
    for name in _INS:
        a = _np.ascontiguousarray(inputs[name])
        arrays[f"in_{name}_dram"] = a
        args.append(nc.dram_tensor(f"in_{name}_dram", a.shape, _mybir.dt.from_np(a.dtype), kind="ExternalInput").ap())
    for i, (shape, dtype) in enumerate(_OUTS):
        dt = _mybir.dt.from_np(_np.dtype(dtype))
        args.append(nc.dram_tensor(f"out_{i}_dram", shape, dt, kind="ExternalOutput").ap())
    gnn_ffn_kernel(nc, *args)
    r = _run(nc, [arrays], core_ids=[0])
    return r.results[0]["out_0_dram"]
```

```python
from contextlib import ExitStack

import concourse.bass as bass
from concourse import mybir

F32 = mybir.dt.float32
F32R = mybir.dt.float32r
I32 = mybir.dt.int32
ALU = mybir.AluOpType
ACT = mybir.ActivationFunctionType
AX_X = mybir.AxisListType.X

NODES, HID, EDGES, EDIM = 1250, 512, 20000, 64
EXPERTS, FFN = 16, 256
P = 128
NB = 125
NE = NB + 1
BLOCKS = NODES // NB
KC = HID // P
EP = 125
EJ = EDGES // EP
TILES = (EDGES + BLOCKS * (P - 1)) // P
PAIRS = TILES // 2
EPS = 1e-5
EXP_MAX = float(2 ** 30)
X_MAX = 20.75
EXP_LN_SET = "natural_log_exp_and_others"
NO_NODE = 1 << 20
assert TILES % 2 == 0 and PAIRS % 2 == 1


class Count:

    def __init__(self, eng, sem):
        self.eng, self.sem, self.n = eng, sem, 0

    def inc(self, ins):
        self.n += 1
        ins.then_inc(self.sem, 1)

    def wait(self):
        self.eng.wait_ge(self.sem, self.n)

    def step(self, ins):
        self.inc(ins)
        self.wait()


def f32(ap):
    return ap.bitcast(F32)


def need(eng, sem, n):
    if not isinstance(n, int) or n > 0:
        eng.wait_ge(sem, n)


def item(i, c):
    return i * 2 + c, c % 2, i + c // 2


def within(n, count):
    return not isinstance(n, int) or 0 <= n < count


def steps(eng, step, first, last, lo, hi):
    for s in range(first, lo):
        step(0, s)
    with eng.Fori(0, (hi - lo + 1) // 2) as i:
        for a in range(2):
            step(i, lo + a)
    for s in range(hi + 1, last + 1):
        step(0, s)


def gnn_ffn_kernel(nc, x, src, dst, edge_attr, W1, b1, W2, b2, W3, b3, W4, b4, gamma, beta, gate_w, w1, w2, out):
    top = ExitStack()
    with top:
        def dram(name, shape, dt):
            return nc.dram_tensor(name, shape, dt).ap()

        src_table = dram("src_table", (NODES, HID), F32)
        dst_table = dram("dst_table", (NODES, HID), F32)
        ea_scr = dram("ea_scr", (EDGES + P, EDIM), F32)
        idx_scr = dram("idx_scr", (EDGES + P, 3), I32)
        mask_scr = dram("mask_scr", (EXPERTS, BLOCKS * NE), F32)

        def sb(name, shape, dt, ctx=top):
            return ctx.enter_context(nc.sbuf_tensor(name, shape, dt))

        ident = sb("ident", [P, P], F32)
        ones = sb("ones", [P, P], F32)
        minus_r = sb("minus_r", [2, P], F32R)
        plus_r = sb("plus_r", [2, P], F32R)
        bias_r = sb("bias_r", [2, 4, HID], F32R)
        eps_col = sb("eps_col", [P, 1], F32)
        half_col = sb("half_col", [P, 1], F32)
        agg = sb("agg", [NB, BLOCKS, HID], F32)
        xn_all = sb("xn_all", [NB, BLOCKS, HID], F32)

        edge_ctx = ExitStack()
        W2h = sb("W2h", [P, KC, HID], F32R, edge_ctx)
        W2l = sb("W2l", [P, KC, HID], F32R, edge_ctx)
        Wch = sb("Wch", [P, HID], F32R, edge_ctx)
        Wcl = sb("Wcl", [P, HID], F32R, edge_ctx)
        start_i = sb("start_i", [P, TILES], I32, edge_ctx)
        block_i = sb("block_i", [P, TILES], I32, edge_ctx)
        block_off = sb("block_off", [P, TILES], F32, edge_ctx)
        iota_n = sb("iota_n", [P, NE], F32, edge_ctx)

        prologue(nc, locals())
        edge_phase(nc, locals())
        edge_ctx.close()

        x1_all = agg
        xlTh = sb("xlTh", [P, KC, BLOCKS * NE], F32R)
        xlTl = sb("xlTl", [P, KC, BLOCKS * NE], F32R)
        node_phase(nc, locals())
        ffn_phase(nc, locals())


def prologue(nc, T):
    x, src, dst, edge_attr = T["x"], T["src"], T["dst"], T["edge_attr"]
    W1, W2 = T["W1"], T["W2"]
    ident, ones, minus_r, plus_r, bias_r = T["ident"], T["ones"], T["minus_r"], T["plus_r"], T["bias_r"]
    eps_col, half_col, agg = T["eps_col"], T["half_col"], T["agg"]
    W2h, W2l, Wch, Wcl = T["W2h"], T["W2l"], T["Wch"], T["Wcl"]
    start_i, block_i, block_off, iota_n = T["start_i"], T["block_i"], T["block_off"], T["iota_n"]
    xn_all, src_table, dst_table = T["xn_all"], T["src_table"], T["dst_table"]
    ea_scr, idx_scr = T["ea_scr"], T["idx_scr"]

    ctx, sems = ExitStack(), []
    with ctx:
        def sb(name, shape, dt):
            return ctx.enter_context(nc.sbuf_tensor(name, shape, dt))

        def pb(name, shape, dt=F32):
            return ctx.enter_context(nc.psum_tensor(name, shape, dt))

        def sem(name):
            sems.append(nc.alloc_semaphore(name))
            return sems[-1]

        w1_raw = sb("w1_raw", [P, 2 * KC, HID], F32)
        w1h = sb("w1h", [P, 2 * KC, HID], F32R)
        w1l = sb("w1l", [P, 2 * KC, HID], F32R)
        wc_raw = sb("wc_raw", [P, HID], F32)
        bias_raw = sb("bias_raw", [2, 4, HID], F32)
        bias_hi = sb("bias_hi", [2, 4, HID], F32R)
        row_is1 = sb("row_is1", [P, 2], F32)
        x_raw = sb("x_raw", [P, BLOCKS, HID], F32)
        w2_raw = x_raw[:, 0:KC, :]
        rank = x_raw[0:EP, KC:2 * KC, :].rearrange("p a d -> p (a d)")[:, 0:(BLOCKS + 1) * EJ].rearrange("p (b j) -> p b j", j=EJ)
        xn_op = sb("xn_op", [NE, 2, HID], F32)
        xTh = sb("xTh", [P, 2, KC * NE], F32R)
        xTl = sb("xTl", [P, 2, KC * NE], F32R)
        tabs = sb("tabs", [NB, 2, 2, HID], F32)
        stats = sb("stats", [NB, BLOCKS, 6], F32)
        mv = sb("mv", [NB, BLOCKS, 2], F32)
        rs = sb("rs", [NB, 4, BLOCKS], F32)

        dst_i = sb("dst_i", [EP, EJ], I32)
        src_i = sb("src_i", [EP, EJ], I32)
        next_i = sb("next_i", [EP, EJ], I32)
        rec_i = sb("rec_i", [EP, EJ, 3], I32)
        tail_i = sb("tail_i", [P, 3], I32)
        tail_ea = sb("tail_ea", [P, EDIM], F32)
        below = sb("below", [EP, BLOCKS + 2, EJ], F32)
        row_cnt = sb("row_cnt", [EP, BLOCKS + 2], F32)
        tri = sb("tri", [EP, EP], F32)
        first = sb("first", [P, BLOCKS + 2], F32)
        row_off = sb("row_off", [EP, BLOCKS + 2], F32)
        cnt_i = sb("cnt_i", [P, BLOCKS], I32)
        nt = sb("nt", [P, BLOCKS], F32)
        tbase = sb("tbase", [P, BLOCKS + 1], F32)
        off = sb("off", [P, BLOCKS + 1], F32)
        doff = sb("doff", [P, BLOCKS], F32)
        iota_t = sb("iota_t", [P, TILES], F32)
        reached = sb("reached", [P, BLOCKS, TILES], F32)
        start_f = sb("start_f", [P, TILES], F32)
        block_f = sb("block_f", [P, TILES], F32)
        flag_i = sb("flag_i", [1, 1], I32)
        pos_f = sb("pos_f", [EP, EJ], F32)
        pos_i = sb("pos_i", [EP, EJ], I32)
        carrier = sb("carrier", [1, 2], F32)
        ea_row = sb("ea_row", [EP, EDIM], F32)
        rec_row = sb("rec_row", [EP, 3], I32)
        pos_row = sb("pos_row", [EP, 1], I32)

        ps_t = pb("ps_t", [P, 2, 512])
        ps_a = pb("ps_a", [P, 2, 512])
        ps_b = pb("ps_b", [P, 2, 512])
        ps_m = pb("ps_m", [P, 512])

        names = ("w1_in w2_in wc_in bias_in dst_in src_in next_in rec_out tail_out ea_out next_set const pool_step dve_step "
                 "w1_hi w1_lo w1_dst_lo edge_hi bias_hi_ready bias_ready cnt_ready cnt_sum var_ready rstd_ready xn_ready op_zero op_ready "
                 "xt_tr xT_hi xT_lo a_ready b_ready a_out b_out meta_ready rank_step pos_ready scat_in scat_out row_ready carried").split()
        S = {n: sem(n) for n in names}
        x_in = [sem(f"x_in{k}") for k in range(BLOCKS // 2)]
        a_stored = [sem(f"a_stored{k}") for k in range(2)]
        b_stored = [sem(f"b_stored{k}") for k in range(2)]
        block = ctx.enter_context(nc.Block())

        src_rows = src_table.rearrange("(i p) d -> i p d", p=NB)
        dst_rows = dst_table.rearrange("(i p) d -> i p d", p=NB)

        @block.sync
        def _(sp):
            x_rows = x.rearrange("(i p) d -> p i d", p=NB)
            for k in range(BLOCKS // 2):
                sp.dma_start(x_raw[0:NB, 2 * k:2 * k + 2, :], x_rows[:, 2 * k:2 * k + 2, :]).then_inc(x_in[k], 16)
            sp.dma_start(w1_raw[:], W1[0:2 * HID, :].rearrange("(k p) n -> p k n", p=P)).then_inc(S["w1_in"], 16)
            sp.dma_start(dst_i[:], dst.rearrange("(p j) -> p j", p=EP)).then_inc(S["dst_in"], 16)
            sp.wait_ge(S["next_set"], 1)
            sp.dma_start(next_i[0:EP - 1, :], dst[1:1 + (EP - 1) * EJ].rearrange("(p j) -> p j", j=EJ)).then_inc(S["next_in"], 16)
            sp.dma_start(next_i[EP - 1:EP, 0:EJ - 1], dst[1 + (EP - 1) * EJ:EDGES].rearrange("(p j) -> p j", p=1)).then_inc(S["next_in"], 16)
            sp.dma_start(src_i[:], src.rearrange("(p j) -> p j", p=EP)).then_inc(S["src_in"], 16)
            for k in range(2):
                sp.dma_start(wc_raw[k * EDIM:(k + 1) * EDIM, :], W1[2 * HID:2 * HID + EDIM, :]).then_inc(S["wc_in"], 16)
            sp.wait_ge(S["xn_ready"], BLOCKS)
            sp.dma_start(w2_raw, W2.rearrange("(k p) n -> p k n", p=P)).then_inc(S["w2_in"], 16)

            def step(i, c):
                t, k, _ = item(i, c - 1)
                if within(t, BLOCKS):
                    sp.wait_ge(S["a_out"], t + 1)
                    sp.dma_start(src_rows[bass.ds(t, 1)].rearrange("a p d -> (a p) d"), tabs[:, k, 0, :]).then_inc(a_stored[k], 16)
                    sp.wait_ge(S["b_out"], t + 1)
                    sp.dma_start(dst_rows[bass.ds(t, 1)].rearrange("a p d -> (a p) d"), tabs[:, k, 1, :]).then_inc(b_stored[k], 16)

            steps(sp, step, 0, BLOCKS, 4, BLOCKS - 1)
            for k in range(2):
                sp.wait_ge(a_stored[k], 16 * (BLOCKS // 2))
                sp.wait_ge(b_stored[k], 16 * (BLOCKS // 2))

        @block.gpsimd
        def _(pool):
            nc.gpsimd.memset(next_i[:], NO_NODE).then_inc(S["next_set"], 1)
            c = Count(pool, S["pool_step"])
            c.inc(nc.gpsimd.memset(ident[:], 0.0))
            c.inc(nc.gpsimd.memset(ones[:], 1.0))
            c.inc(nc.gpsimd.memset(tri[:], 1.0))
            c.inc(nc.gpsimd.memset(row_is1[:], 0.0))
            c.inc(nc.gpsimd.memset(tail_i[:], 0))
            c.inc(nc.gpsimd.memset(tail_ea[:], 0.0))
            c.step(nc.gpsimd.iota(iota_t[:], [[1, TILES]], base=0, channel_multiplier=0, allow_small_or_imprecise_dtypes=True))
            c.inc(nc.gpsimd.iota(iota_n[:], [[1, NE]], base=0, channel_multiplier=0, allow_small_or_imprecise_dtypes=True))
            c.inc(nc.gpsimd.affine_select(out=ident[:], in_=ident[:], compare_op=ALU.not_equal, fill=1.0, base=0,
                                          pattern=[[-1, P]], channel_multiplier=1))
            c.inc(nc.gpsimd.affine_select(out=tri[:], in_=tri[:], compare_op=ALU.is_gt, fill=0.0, base=0,
                                          pattern=[[1, EP]], channel_multiplier=-1))
            c.inc(nc.gpsimd.affine_select(out=row_is1[:], in_=row_is1[:], compare_op=ALU.not_equal, fill=1.0, base=0,
                                          pattern=[[-1, 2]], channel_multiplier=1))
            c.inc(nc.gpsimd.memset(tail_i[:, 2:3], NO_NODE))
            c.inc(nc.gpsimd.memset(eps_col[:], EPS))
            c.step(nc.gpsimd.memset(half_col[:], 0.5))
            nc.gpsimd.memset(xn_op[:], 0.0).then_inc(S["const"], 1)
            for k in range(KC, 2 * KC):
                pool.wait_ge(S["w1_hi"], k + 1)
                nc.gpsimd.tensor_tensor(w1l[:, k, :], w1_raw[:, k, :], f32(w1h[:, k, :]), ALU.subtract).then_inc(S["w1_dst_lo"], 1)
            pool.dma_start(idx_scr[EDGES:EDGES + P, :], tail_i[:]).then_inc(S["tail_out"], 16)
            pool.dma_start(ea_scr[EDGES:EDGES + P, :], tail_ea[:]).then_inc(S["tail_out"], 16)
            pool.wait_ge(S["const"], 1)

            def grouped():
                pool.wait_ge(S["dst_in"], 16)
                pool.wait_ge(S["src_in"], 16)
                c.inc(nc.gpsimd.tensor_copy(rec_i[:, :, 0], src_i[:]))
                c.inc(nc.gpsimd.tensor_copy(rec_i[:, :, 1], dst_i[:]))
                c.inc(nc.gpsimd.tensor_copy(rec_i[:, :, 2], dst_i[:]))
                c.wait()
                pool.wait_ge(S["meta_ready"], 1)
                unsorted = pool.value_load(flag_i[0:1, 0:1], min_val=0, max_val=EDGES)
                nc.gpsimd.memset(carrier[:], 0.0).then_inc(S["carried"], 1)
                with pool.If(unsorted > 0):
                    pool.wait_ge(S["pos_ready"], 1)
                    ea_cols = edge_attr.rearrange("(p j) d -> j p d", p=EP)
                    with pool.Fori(0, EJ) as j:
                        pool.dma_start(ea_row[:], ea_cols[bass.ds(j, 1)].rearrange("a p d -> (a p) d")).then_inc(S["scat_in"], 16)
                        nc.gpsimd.tensor_copy(rec_row[:], rec_i[:, bass.ds(j, 1), :].rearrange("p a r -> p (a r)")).then_inc(S["row_ready"], 1)
                        nc.gpsimd.tensor_copy(pos_row[:], pos_i[:, bass.ds(j, 1)]).then_inc(S["row_ready"], 1)
                        pool.wait_ge(S["row_ready"], j * 2 + 2)
                        pool.wait_ge(S["scat_in"], j * 16 + 16)
                        pool.wait_ge(S["carried"], j + 1)
                        nc.gpsimd.tensor_tensor(carrier[0:1, 0:1], carrier[0:1, 1:2], carrier[0:1, 1:2], ALU.add).then_inc(S["carried"], 1)
                        pool.indirect_dma_start(out=ea_scr[:, :], out_offset=bass.IndirectOffsetOnAxis(ap=pos_row[:, 0:1], axis=0),
                                                in_=ea_row[:], in_offset=None).then_inc(S["scat_out"], 16)
                        pool.indirect_dma_start(out=idx_scr[:, :], out_offset=bass.IndirectOffsetOnAxis(ap=pos_row[:, 0:1], axis=0),
                                                in_=rec_row[:], in_offset=None).then_inc(S["scat_out"], 16)
                        pool.wait_ge(S["scat_out"], j * 32 + 32)
                with pool.Else():
                    pool.dma_start(ea_scr[0:EDGES, :].rearrange("(p j) d -> p (j d)", p=P - 3), edge_attr.rearrange("(p j) d -> p (j d)", p=P - 3)).then_inc(S["ea_out"], 16)
                    pool.dma_start(idx_scr[0:EDGES, :].rearrange("(p j) r -> p (j r)", p=EP), rec_i[:].rearrange("p j r -> p (j r)")).then_inc(S["rec_out"], 16)

            def step(i, c):
                t, k, _ = item(i, c)
                if within(t, BLOCKS):
                    pool.wait_ge(S["xn_ready"], t + 1)
                    need(pool, S["xt_tr"], t - 1)
                    nc.gpsimd.tensor_copy(xn_op[0:NB, k, :], xn_all[:, bass.ds(t, 1), :].rearrange("p a d -> p (a d)")).then_inc(S["op_ready"], 1)
                if isinstance(i, int) and c == 3:
                    grouped()

            steps(pool, step, 0, BLOCKS - 1, 4, BLOCKS - 1)
            nc.gpsimd.memset(agg[:], 0.0).then_inc(S["pool_step"], 1)
            c.n += 1
            unsorted = pool.value_load(flag_i[0:1, 0:1], min_val=0, max_val=EDGES)
            with pool.If(unsorted < 1):
                pool.wait_ge(S["ea_out"], 16)
                pool.wait_ge(S["rec_out"], 16)
            pool.wait_ge(S["tail_out"], 32)
            c.wait()

        @block.scalar
        def _(act):
            for n, b in enumerate(("b1", "b2", "b3", "b4")):
                for r in range(2):
                    act.dma_start(bias_raw[r:r + 1, n, :], T[b].rearrange("(a n) -> a n", a=1)).then_inc(S["bias_in"], 16)
            nc.scalar.preload_act_table_set(EXP_LN_SET)
            act.wait_ge(S["const"], 1)
            act.wait_ge(S["var_ready"], 1)
            nc.scalar.activation(rs[:, 0, :], mv[:, :, 1], ACT.Ln, bias=eps_col[0:NB, :]).then_inc(S["rstd_ready"], 1)
            act.wait_ge(S["rstd_ready"], 1)
            nc.scalar.activation(rs[:, 1, :], rs[:, 0, :], ACT.Exp, scale=-0.5).then_inc(S["rstd_ready"], 1)
            act.wait_ge(S["bias_in"], 128)
            nc.scalar.activation(bias_hi[:], bias_raw[:], ACT.Copy).then_inc(S["bias_hi_ready"], 1)
            act.wait_ge(S["w1_in"], 16)
            for k in range(2 * KC):
                nc.scalar.activation(w1h[:, k, :], w1_raw[:, k, :], ACT.Copy).then_inc(S["w1_hi"], 1)

            def step(i, c):
                t, k, _ = item(i, c)
                if within(t, BLOCKS):
                    act.wait_ge(S["xt_tr"], t + 1)
                    need(act, S["b_ready"], t - 1)
                    nc.scalar.activation(xTh[:, k, :], ps_t[:, k, 0:KC * NE], ACT.Copy).then_inc(S["xT_hi"], 1)
                t, k, used = item(i, c - 1)
                if within(t, BLOCKS):
                    act.wait_ge(S["a_ready"], t + 1)
                    need(act, a_stored[k], used * 16)
                    nc.scalar.activation(tabs[:, k, 0, :], ps_a[0:NB, k, :], ACT.Copy).then_inc(S["a_out"], 1)
                if isinstance(i, int) and c == 3:
                    act.wait_ge(S["w2_in"], 16)
                    nc.scalar.activation(W2h[:], w2_raw, ACT.Copy).then_inc(S["edge_hi"], 1)
                    act.wait_ge(S["wc_in"], 32)
                    nc.scalar.activation(Wch[:], wc_raw[:], ACT.Copy).then_inc(S["edge_hi"], 1)

            steps(act, step, 0, BLOCKS, 4, BLOCKS - 1)

        @block.vector
        def _(dve):
            c = Count(dve, S["dve_step"])
            for t in range(BLOCKS):
                if t % 2 == 0:
                    dve.wait_ge(x_in[t // 2], 16)
                c.inc(nc.vector.bn_stats(out=stats[:, t, :], in_=x_raw[0:NB, t, :]))
            c.wait()
            for t in range(BLOCKS):
                ins = nc.vector.bn_aggr(out=mv[:, t, :], in_=stats[:, t, :])
            ins.then_inc(S["var_ready"], 1)
            dve.wait_ge(S["rstd_ready"], 2)
            c.step(nc.vector.tensor_tensor(rs[:, 2, :], rs[:, 1, :], rs[:, 1, :], ALU.mult))
            c.step(nc.vector.scalar_tensor_tensor(out=rs[:, 3, :], in0=mv[:, :, 1], scalar=EPS, in1=rs[:, 2, :], op0=ALU.add, op1=ALU.mult))
            c.step(nc.vector.tensor_scalar(rs[:, 3, :], rs[:, 3, :], -0.5, 1.5, ALU.mult, ALU.add))
            c.step(nc.vector.tensor_tensor(rs[:, 2, :], rs[:, 1, :], rs[:, 3, :], ALU.mult))

            def normalised(first, end):
                for t in range(first, end):
                    nc.vector.tensor_scalar(xn_all[:, t, :], x_raw[0:NB, t, :], mv[:, t, 0:1], rs[:, 2, t:t + 1], ALU.subtract, ALU.mult).then_inc(S["xn_ready"], 1)

            normalised(0, 2)
            for k in range(KC):
                dve.wait_ge(S["w1_hi"], k + 1)
                nc.vector.tensor_tensor(w1l[:, k, :], w1_raw[:, k, :], f32(w1h[:, k, :]), ALU.subtract).then_inc(S["w1_lo"], 1)
            dve.wait_ge(S["const"], 1)
            dve.wait_ge(S["bias_hi_ready"], 1)
            c.inc(nc.vector.tensor_copy(plus_r[:], ones[0:2, :]))
            c.inc(nc.vector.tensor_scalar(minus_r[:], ones[0:2, :], -1.0, None, ALU.mult))
            c.step(nc.vector.tensor_tensor(bias_raw[:], bias_raw[:], f32(bias_hi[:]), ALU.subtract))
            c.step(nc.vector.tensor_scalar(bias_raw[:], bias_raw[:], row_is1[0:2, 1:2], None, ALU.mult))
            nc.vector.scalar_tensor_tensor(out=bias_r[:], in0=f32(bias_hi[:]), scalar=row_is1[0:2, 0:1], in1=bias_raw[:],
                                           op0=ALU.mult, op1=ALU.add).then_inc(S["bias_ready"], 1)
            def edges_below():
                c.inc(nc.vector.memset(below[:, 0, :], 0.0))
                c.inc(nc.vector.memset(below[:, BLOCKS, :], 1.0))
                c.inc(nc.vector.memset(tbase[:, 0:1], 0.0))
                dve.wait_ge(S["dst_in"], 16)
                for b in range(1, BLOCKS):
                    c.inc(nc.vector.tensor_scalar(below[:, b, :], dst_i[:], float(NB * b), None, ALU.is_lt))
                dve.wait_ge(S["next_in"], 32)
                c.step(nc.vector.tensor_tensor(below[:, BLOCKS + 1, :], next_i[:], dst_i[:], ALU.is_lt))
                nc.vector.tensor_reduce(out=row_cnt[:], in_=below[:], axis=AX_X, op=ALU.add).then_inc(S["cnt_ready"], 1)

            def first_edges():
                dve.wait_ge(S["cnt_sum"], 1)
                c.inc(nc.vector.tensor_copy(first[:], ps_m[:, 0:BLOCKS + 2]))
                c.step(nc.vector.tensor_copy(row_off[:], ps_m[0:EP, 64:64 + BLOCKS + 2]))
                nc.vector.tensor_copy(flag_i[:], first[0:1, BLOCKS + 1:BLOCKS + 2]).then_inc(S["meta_ready"], 1)
                c.step(nc.vector.scalar_tensor_tensor(out=cnt_i[:], in0=first[:, 1:BLOCKS + 1], scalar=float(P - 1), in1=first[:, 0:BLOCKS],
                                                      op0=ALU.add, op1=ALU.subtract))
                c.step(nc.vector.tensor_scalar(cnt_i[:], cnt_i[:], 7, None, ALU.arith_shift_right))
                c.step(nc.vector.tensor_copy(nt[:], cnt_i[:]))
                c.step(nc.vector.tensor_tensor_scan(out=tbase[:, 1:BLOCKS + 1], data0=ones[:, 0:BLOCKS], data1=nt[:], initial=0.0,
                                                    op0=ALU.mult, op1=ALU.add))
                c.step(nc.vector.scalar_tensor_tensor(out=off[:], in0=tbase[:], scalar=-float(P), in1=first[:, 0:BLOCKS + 1],
                                                      op0=ALU.mult, op1=ALU.add))
                c.inc(nc.vector.tensor_tensor(doff[:], off[:, 1:BLOCKS + 1], off[:, 0:BLOCKS], ALU.subtract))

            def tiles_reached():
                for b in range(BLOCKS):
                    c.inc(nc.vector.tensor_scalar(reached[:, b, :], iota_t[:], tbase[:, b + 1:b + 2], None, ALU.is_ge))
                c.wait()

            def tile_blocks():
                c.step(nc.vector.tensor_reduce(out=block_f[:], in_=reached[:, 0:BLOCKS - 1, :].rearrange("p b t -> p t b"), axis=AX_X, op=ALU.add))
                for b in range(BLOCKS):
                    c.inc(nc.vector.tensor_scalar(reached[:, b, :], reached[:, b, :], doff[:, b:b + 1], None, ALU.mult))
                c.wait()

            def tile_starts():
                c.step(nc.vector.tensor_reduce(out=start_f[:], in_=reached[:].rearrange("p b t -> p t b"), axis=AX_X, op=ALU.add))
                c.step(nc.vector.scalar_tensor_tensor(out=start_f[:], in0=iota_t[:], scalar=float(P), in1=start_f[:], op0=ALU.mult, op1=ALU.add))
                c.inc(nc.vector.tensor_scalar(start_i[:], start_f[:], float(EDGES), None, ALU.min))
                c.inc(nc.vector.tensor_copy(block_i[:], block_f[:]))
                c.inc(nc.vector.tensor_scalar(block_off[:], block_f[:], float(NB), None, ALU.mult))
                c.wait()

            def places():
                unsorted = dve.value_load(flag_i[0:1, 0:1], min_val=0, max_val=EDGES)
                with dve.If(unsorted > 0):
                    for b in range(BLOCKS + 1):
                        ins = nc.vector.tensor_tensor_scan(out=rank[:, b, :], data0=below[:, BLOCKS, :], data1=below[:, b, :],
                                                           initial=row_off[:, b:b + 1], op0=ALU.mult, op1=ALU.add)
                    ins.then_inc(S["rank_step"], 1)
                    dve.wait_ge(S["rank_step"], 1)
                    nc.vector.tensor_tensor(rank[:, 0:BLOCKS, :], rank[:, 1:BLOCKS + 1, :], rank[:, 0:BLOCKS, :], ALU.subtract).then_inc(S["rank_step"], 1)
                    nc.vector.tensor_tensor(below[:, 0:BLOCKS, :], below[:, 1:BLOCKS + 1, :], below[:, 0:BLOCKS, :], ALU.subtract).then_inc(S["rank_step"], 1)
                    dve.wait_ge(S["rank_step"], 3)
                    for b in range(BLOCKS):
                        ins = nc.vector.tensor_scalar(rank[:, b, :], rank[:, b, :], first[0:EP, b:b + 1], -1.0, ALU.add, ALU.add)
                    ins.then_inc(S["rank_step"], 1)
                    dve.wait_ge(S["rank_step"], 4)
                    nc.vector.tensor_tensor(rank[:, 0:BLOCKS, :], rank[:, 0:BLOCKS, :], below[:, 0:BLOCKS, :], ALU.mult).then_inc(S["rank_step"], 1)
                    dve.wait_ge(S["rank_step"], 5)
                    nc.vector.tensor_reduce(out=pos_f[:], in_=rank[:, 0:BLOCKS, :].rearrange("p b j -> p j b"), axis=AX_X, op=ALU.add).then_inc(S["rank_step"], 1)
                    dve.wait_ge(S["rank_step"], 6)
                    nc.vector.tensor_copy(pos_i[:], pos_f[:]).then_inc(S["pos_ready"], 1)

            def lo_weights():
                dve.wait_ge(S["edge_hi"], 2)
                nc.vector.tensor_tensor(W2l[:], w2_raw, f32(W2h[:]), ALU.subtract).then_inc(S["dve_step"], 1)
                nc.vector.tensor_tensor(Wcl[:], wc_raw[:], f32(Wch[:]), ALU.subtract).then_inc(S["dve_step"], 1)

            def step(i, c):
                t, k, _ = item(i, c)
                if within(t, BLOCKS):
                    dve.wait_ge(S["xT_hi"], t + 1)
                    nc.vector.tensor_tensor(xTl[:, k, :], ps_t[:, k, 0:KC * NE], f32(xTh[:, k, :]), ALU.subtract).then_inc(S["xT_lo"], 1)
                if isinstance(i, int) and c == BLOCKS:
                    tile_starts()
                    lo_weights()
                t, k, used = item(i, c - 1)
                if within(t, BLOCKS):
                    dve.wait_ge(S["b_ready"], t + 1)
                    need(dve, b_stored[k], used * 16)
                    nc.vector.tensor_copy(tabs[:, k, 1, :], ps_b[0:NB, k, :]).then_inc(S["b_out"], 1)
                if isinstance(i, int) and c == 0:
                    normalised(2, BLOCKS)
                if isinstance(i, int) and c == 1:
                    edges_below()
                if isinstance(i, int) and c == 2:
                    first_edges()
                    tiles_reached()
                if isinstance(i, int) and c == 3:
                    tile_blocks()
                    places()

            steps(dve, step, 0, BLOCKS, 4, BLOCKS - 1)

        @block.tensor
        def _(pe):
            pe.wait_ge(S["const"], 1)

            def step(i, c):
                t, k, _ = item(i, c)
                if within(t, BLOCKS):
                    pe.wait_ge(S["op_ready"], t + 1)
                    need(pe, S["xT_lo"], t - 1)
                    for q in range(KC):
                        ins = nc.tensor.transpose(ps_t[:, k, q * NE:(q + 1) * NE], xn_op[:, k, q * P:(q + 1) * P], ident[0:NE, 0:NE])
                    ins.then_inc(S["xt_tr"], 1)
                t, k, _ = item(i, c - 1)
                if within(t, BLOCKS):
                    pe.wait_ge(S["xT_lo"], t + 1)
                    if isinstance(t, int) and t == 0:
                        pe.wait_ge(S["w1_lo"], KC)
                    for n, ps, ready, free in ((0, ps_a, "a_ready", "a_out"), (1, ps_b, "b_ready", "b_out")):
                        o = ps[0:NE, k, :]
                        need(pe, S[free], t - 1)
                        if n == 1:
                            if isinstance(t, int) and t == 0:
                                pe.wait_ge(S["w1_dst_lo"], KC)
                                pe.wait_ge(S["bias_ready"], 1)
                            nc.tensor.matmul(o, plus_r[:, 0:NE], bias_r[:, 0, :], start=True, stop=False)
                        for q in range(KC):
                            hi, lo = xTh[:, k, q * NE:(q + 1) * NE], xTl[:, k, q * NE:(q + 1) * NE]
                            nc.tensor.matmul(o, hi, w1h[:, n * KC + q, :], start=(q == 0 and n == 0), stop=False)
                            nc.tensor.matmul(o, hi, w1l[:, n * KC + q, :], start=False, stop=False)
                            ins = nc.tensor.matmul(o, lo, w1h[:, n * KC + q, :], start=False, stop=(q == KC - 1))
                        ins.then_inc(S[ready], 1)
                if isinstance(i, int) and c == 2:
                    pe.wait_ge(S["cnt_ready"], 1)
                    nc.tensor.matmul(ps_m[:, 0:BLOCKS + 2], ones[0:EP, :], row_cnt[:], start=True, stop=True)
                    nc.tensor.matmul(ps_m[0:EP, 64:64 + BLOCKS + 2], tri[:], row_cnt[:], start=True, stop=True).then_inc(S["cnt_sum"], 1)

            steps(pe, step, 0, BLOCKS, 4, BLOCKS - 1)
    nc.clear_and_free_semaphores(sems)
    nc.all_engine_barrier()


def edge_phase(nc, T):
    W2h, W2l, Wch, Wcl = T["W2h"], T["W2l"], T["Wch"], T["Wcl"]
    ident, minus_r, bias_r, half_col, iota_n = T["ident"], T["minus_r"], T["bias_r"], T["half_col"], T["iota_n"]
    start_i, block_i, block_off, agg = T["start_i"], T["block_i"], T["block_off"], T["agg"]
    src_table, dst_table, ea_scr, idx_scr = T["src_table"], T["dst_table"], T["ea_scr"], T["idx_scr"]

    ctx, sems = ExitStack(), []
    with ctx:
        def sb(name, shape, dt=F32):
            return ctx.enter_context(nc.sbuf_tensor(name, shape, dt))

        def sem(name):
            sems.append(nc.alloc_semaphore(name))
            return sems[-1]

        idx_sl = sb("idx_sl", [P, 2, 2, 3], I32)
        ea_sl = sb("ea_sl", [P, 2, 2, EDIM])
        ea_hl = sb("ea_hl", [P, 2, 2, 2 * EDIM], F32R)
        eaT = sb("eaT", [2 * EDIM, 2, 2, P], F32R)
        gath = sb("gath", [P, 2, 2, HID])
        pre = sb("pre", [P, 2, 2, HID])
        act1 = sb("act1", [P, 2, 2, HID])
        act2 = sb("act2", [P, 2, 2, HID])
        hTh = sb("hTh", [P, 2, 2, HID], F32R)
        hTl = sb("hTl", [P, 2, 2, HID], F32R)
        msg_hi = sb("msg_hi", [P, 2, 2, HID], F32R)
        msg_lo = sb("msg_lo", [P, 2, 2, HID], F32R)
        dloc = sb("dloc", [P, TILES])
        carrier = sb("e_carrier", [1, 3, 2])
        onehot = sb("onehot", [P, 2, 2, NE], F32R)

        ps_1 = ctx.enter_context(nc.psum_tensor("ps_1", [P, 2, HID], F32))
        ps_h = ctx.enter_context(nc.psum_tensor("ps_h", [P, 2, HID], F32))
        ps_2 = ctx.enter_context(nc.psum_tensor("ps_2", [P, 2, 2, HID], F32))

        def slots(name):
            return [sem(f"{name}{k}") for k in range(2)]

        idx_in, ea_in, src_gath, both_gath = slots("idx_in"), slots("ea_in"), slots("src_gath"), slots("both_gath")
        names = ("ea_hi split dst_ready eaT_ps eaT_ready lin1_ps pre_ready exp1 inc1 sq1 ln1 quot1 h_ready hT_ps hT_hi hT_lo lin2_ps "
                 "exp2 inc2 sq2 ln2 quot2 msg_ready msg_hi_ready msg_lo_ready onehot_ready sum_ps summed src_free dst_free ea_free").split()
        S = {n: sem("e_" + n) for n in names}
        block = ctx.enter_context(nc.Block())

        FIRST, LAST, LO, HI = -4, PAIRS + 3, 7, PAIRS - 5

        @block.sync
        def _(sp):
            def step(i, c):
                q, k, used = item(i, c + 4)
                if within(q, PAIRS):
                    need(sp, both_gath[k], used * 32)
                    need(sp, S["split"], q - 1)
                    need(sp, S["dst_ready"], q - 1)
                    for j in range(2):
                        first = sp.value_load(start_i[0:1, bass.ds(q * 2 + j, 1)], min_val=0, max_val=EDGES)
                        sp.dma_start(idx_sl[:, k, j, :], idx_scr[bass.ds(first, P), :]).then_inc(idx_in[k], 16)
                        sp.dma_start(ea_sl[:, k, j, :], ea_scr[bass.ds(first, P), :]).then_inc(ea_in[k], 16)

            steps(sp, step, FIRST, LAST, LO, HI)

        @block.gpsimd
        def _(pool):
            nc.gpsimd.memset(carrier[:, 0, :], 0.0).then_inc(S["src_free"], 1)
            nc.gpsimd.memset(carrier[:, 1, :], 0.0).then_inc(S["dst_free"], 1)
            nc.gpsimd.memset(carrier[:, 2, :], 0.0).then_inc(S["ea_free"], 1)

            def carry(n, row, passed):
                pool.wait_ge(passed, n + 1)
                nc.gpsimd.tensor_tensor(carrier[:, row, 0:1], carrier[:, row, 1:2], carrier[:, row, 1:2], ALU.add).then_inc(passed, 1)

            def step(i, c):
                b, kb, used = item(i, c + 2)
                if within(b, PAIRS):
                    pool.wait_ge(src_gath[kb], used * 32 + 32)
                    carry(b, 1, S["dst_free"])
                    for j in range(2):
                        pool.indirect_dma_start(out=gath[:, kb, j, :], out_offset=None, in_=dst_table[:, :],
                                                in_offset=bass.IndirectOffsetOnAxis(ap=idx_sl[:, kb, j, 1:2], axis=0),
                                                compute_op=ALU.add).then_inc(both_gath[kb], 16)
                if within(b, PAIRS):
                    pool.wait_ge(ea_in[kb], used * 32 + 32)
                    need(pool, S["eaT_ps"], b - 1)
                    carry(b, 2, S["ea_free"])
                    nc.gpsimd.tensor_copy(ea_hl[:, kb, :, 0:EDIM], ea_sl[:, kb]).then_inc(S["ea_hi"], 1)
                    pool.wait_ge(S["ea_hi"], b + 1)
                    nc.gpsimd.tensor_tensor(ea_hl[:, kb, :, EDIM:2 * EDIM], ea_sl[:, kb], f32(ea_hl[:, kb, :, 0:EDIM]), ALU.subtract).then_inc(S["split"], 1)
                g, kg, used = item(i, c + 3)
                if within(g, PAIRS):
                    pool.wait_ge(idx_in[kg], used * 32 + 32)
                    need(pool, S["pre_ready"], g - 1)
                    carry(g, 0, S["src_free"])
                    for j in range(2):
                        pool.indirect_dma_start(out=gath[:, kg, j, :], out_offset=None, in_=src_table[:, :],
                                                in_offset=bass.IndirectOffsetOnAxis(ap=idx_sl[:, kg, j, 0:1], axis=0)).then_inc(src_gath[kg], 16)
                q, k, _ = item(i, c - 3)
                if within(q, PAIRS):
                    pool.wait_ge(S["msg_hi_ready"], q + 1)
                    need(pool, S["sum_ps"], q - 1)
                    nc.gpsimd.tensor_tensor(msg_lo[:, k], act2[:, k], f32(msg_hi[:, k]), ALU.subtract).then_inc(S["msg_lo_ready"], 1)

            steps(pool, step, FIRST, LAST, LO, HI)

        @block.scalar
        def _(act):
            nc.scalar.preload_act_table_set(EXP_LN_SET)

            def step(i, c):
                q, k, _ = item(i, c)
                first = within(q, PAIRS)
                q2, k2, _ = item(i, c - 2)
                second = within(q2, PAIRS)
                if second:
                    act.wait_ge(S["lin2_ps"], q2 + 1)
                    need(act, S["msg_lo_ready"], q2 - 1)
                    nc.scalar.activation(act2[:, k2], ps_2[:, k2], ACT.Exp, scale=-1.0).then_inc(S["exp2"], 1)
                r, kr, _ = item(i, c - 1)
                if within(r, PAIRS):
                    act.wait_ge(S["hT_ps"], r + 1)
                    need(act, S["lin2_ps"], r - 1)
                    nc.scalar.activation(hTh[:, kr], ps_h[:], ACT.Copy).then_inc(S["hT_hi"], 1)
                if first:
                    act.wait_ge(S["inc1"], q + 1)
                    nc.scalar.activation(act1[:, k], act1[:, k], ACT.Square).then_inc(S["sq1"], 1)
                if second:
                    act.wait_ge(S["inc2"], q2 + 1)
                    nc.scalar.activation(act2[:, k2], act2[:, k2], ACT.Square).then_inc(S["sq2"], 1)
                if first:
                    act.wait_ge(S["sq1"], q + 1)
                    nc.scalar.activation(act1[:, k], act1[:, k], ACT.Ln, bias=half_col[:], scale=0.5).then_inc(S["ln1"], 1)
                if second:
                    act.wait_ge(S["sq2"], q2 + 1)
                    nc.scalar.activation(act2[:, k2], act2[:, k2], ACT.Ln, bias=half_col[:], scale=0.5).then_inc(S["ln2"], 1)
                if first:
                    act.wait_ge(S["ln1"], q + 1)
                    nc.scalar.activation(act1[:, k], act1[:, k], ACT.Exp, scale=-1.0).then_inc(S["quot1"], 1)
                n, kn, _ = item(i, c + 1)
                if within(n, PAIRS):
                    act.wait_ge(S["pre_ready"], n + 1)
                    need(act, S["hT_ps"], n - 1)
                    nc.scalar.activation(act1[:, kn], pre[:, kn], ACT.Exp).then_inc(S["exp1"], 1)
                if second:
                    act.wait_ge(S["ln2"], q2 + 1)
                    nc.scalar.activation(act2[:, k2], act2[:, k2], ACT.Exp, scale=-1.0).then_inc(S["quot2"], 1)

            steps(act, step, FIRST, LAST, LO, HI)

        @block.vector
        def _(dve):
            def step(i, c):
                q, k, _ = item(i, c)
                first = within(q, PAIRS)
                q2, k2, _ = item(i, c - 2)
                n, kn, used = item(i, c + 1)
                if within(n, PAIRS):
                    dve.wait_ge(S["eaT_ps"], n + 1)
                    need(dve, S["lin1_ps"], n - 1)
                    nc.vector.tensor_copy(eaT[:, kn], ps_1[:, :, 0:P]).then_inc(S["eaT_ready"], 1)
                g, kg, _ = item(i, c - 3)
                if within(g, PAIRS):
                    dve.wait_ge(S["quot2"], g + 1)
                    nc.vector.scalar_tensor_tensor(out=act2[:, kg], in0=act2[:, kg], scalar=1.0, in1=ps_2[:, kg],
                                                   op0=ALU.subtract, op1=ALU.mult).then_inc(S["msg_ready"], 1)
                if within(q2, PAIRS):
                    dve.wait_ge(S["exp2"], q2 + 1)
                    nc.vector.tensor_scalar(act2[:, k2], act2[:, k2], EXP_MAX, 1.0, ALU.min, ALU.add).then_inc(S["inc2"], 1)
                if within(g, PAIRS):
                    need(dve, S["sum_ps"], g - 1)
                    dve.wait_ge(S["msg_ready"], g + 1)
                    nc.vector.tensor_copy(msg_hi[:, kg], act2[:, kg]).then_inc(S["msg_hi_ready"], 1)
                if within(n, PAIRS):
                    dve.wait_ge(S["lin1_ps"], n + 1)
                    dve.wait_ge(both_gath[kn], used * 32 + 32)
                    need(dve, S["h_ready"], n - 1)
                    nc.vector.tensor_tensor(pre[:, kn], ps_1[:], gath[:, kn], ALU.add).then_inc(S["pre_ready"], 1)
                a, ka, _ = item(i, c - 4)
                if within(a, PAIRS):
                    rows = []
                    for j in range(2):
                        b = dve.value_load(block_i[0:1, bass.ds(a * 2 + j, 1)], min_val=0, max_val=BLOCKS - 1)
                        rows.append(agg[:, bass.ds(b, 1), :].rearrange("p a d -> p (a d)"))
                r, kr, _ = item(i, c - 1)
                if within(r, PAIRS):
                    dve.wait_ge(S["hT_hi"], r + 1)
                    nc.vector.tensor_tensor(hTl[:, kr], ps_h[:], f32(hTh[:, kr]), ALU.subtract).then_inc(S["hT_lo"], 1)
                for j in range(2):
                    if within(a, PAIRS):
                        dve.wait_ge(S["sum_ps"], a + 1)
                        need(dve, S["summed"], a * 2 + j)
                        nc.vector.tensor_tensor(rows[j], rows[j], ps_1[0:NB, j, :], ALU.add).then_inc(S["summed"], 1)
                    if within(g, PAIRS):
                        dve.wait_ge(S["dst_ready"], g + 1)
                        nc.vector.tensor_scalar(onehot[:, kg, j, :], iota_n[:], dloc[:, bass.ds(g * 2 + j, 1)], None, ALU.is_equal).then_inc(S["onehot_ready"], 1)
                if first:
                    dve.wait_ge(S["quot1"], q + 1)
                    nc.vector.scalar_tensor_tensor(out=act1[:, k], in0=act1[:, k], scalar=1.0, in1=pre[:, k],
                                                   op0=ALU.subtract, op1=ALU.mult).then_inc(S["h_ready"], 1)
                l, kl, lused = item(i, c + 2)
                if within(l, PAIRS):
                    dve.wait_ge(idx_in[kl], lused * 32 + 32)
                    nc.vector.tensor_tensor(dloc[:, bass.ds(l * 2, 2)], idx_sl[:, kl, :, 2], block_off[:, bass.ds(l * 2, 2)], ALU.subtract).then_inc(S["dst_ready"], 1)
                if within(n, PAIRS):
                    dve.wait_ge(S["exp1"], n + 1)
                    nc.vector.tensor_scalar(act1[:, kn], act1[:, kn], EXP_MAX, 1.0, ALU.min, ALU.add).then_inc(S["inc1"], 1)

            steps(dve, step, FIRST, LAST, LO, HI)

        @block.tensor
        def _(pe):
            def step(i, c):
                n, kn, _ = item(i, c + 1)
                r, kr, _ = item(i, c - 1)
                m, km, _ = item(i, c - 4)

                def lin2(j, d, part, weights, last=False):
                    return nc.tensor.matmul(ps_2[:, kr, j, :], part[:, kr, j, d * P:(d + 1) * P], weights[:, d, :], start=False, stop=last)

                if within(n, PAIRS):
                    pe.wait_ge(S["split"], n + 1)
                    need(pe, S["pre_ready"], n)
                    need(pe, S["summed"], (n - 5) * 2)
                    for j in range(2):
                        ins = nc.tensor.transpose(ps_1[:, j, 0:P], f32(ea_hl[:, kn, j, :]), ident[:])
                    ins.then_inc(S["eaT_ps"], 1)
                if within(r, PAIRS):
                    pe.wait_ge(S["h_ready"], r + 1)
                    need(pe, S["hT_lo"], r)
                    for j in range(2):
                        for d in range(KC):
                            ins = nc.tensor.transpose(ps_h[:, j, d * P:(d + 1) * P], act1[:, kr, j, d * P:(d + 1) * P], ident[:])
                    ins.then_inc(S["hT_ps"], 1)
                if within(n, PAIRS):
                    pe.wait_ge(S["eaT_ready"], n + 1)
                    for j in range(2):
                        nc.tensor.matmul(ps_1[:, j, :], eaT[:, kn, j, :], Wch[:], start=True, stop=False)
                        ins = nc.tensor.matmul(ps_1[:, j, :], eaT[:, kn, j, :], Wcl[:], start=False, stop=True)
                    ins.then_inc(S["lin1_ps"], 1)
                if within(r, PAIRS):
                    need(pe, S["msg_ready"], r - 1)
                    for j in range(2):
                        nc.tensor.matmul(ps_2[:, kr, j, :], minus_r[:], bias_r[:, 1, :], start=True, stop=False)
                    pe.wait_ge(S["hT_hi"], r + 1)
                    for d in range(KC):
                        lin2(0, d, hTh, W2h)
                        lin2(0, d, hTh, W2l)
                if within(m, PAIRS):
                    need(pe, S["summed"], m * 2)
                    pe.wait_ge(S["onehot_ready"], m * 2 + 2)
                    pe.wait_ge(S["msg_lo_ready"], m + 1)
                    pe.wait_ge(S["pre_ready"], min(m + 6, PAIRS) if isinstance(m, int) else m + 6)
                    for j in range(2):
                        nc.tensor.matmul(ps_1[0:NE, j, :], onehot[:, km, j, :], msg_hi[:, km, j, :], start=True, stop=False)
                        ins = nc.tensor.matmul(ps_1[0:NE, j, :], onehot[:, km, j, :], msg_lo[:, km, j, :], start=False, stop=True)
                    ins.then_inc(S["sum_ps"], 1)
                if within(r, PAIRS):
                    for d in range(KC):
                        lin2(1, d, hTh, W2h)
                        lin2(1, d, hTh, W2l)
                    pe.wait_ge(S["hT_lo"], r + 1)
                    for j in range(2):
                        for d in range(KC):
                            ins = lin2(j, d, hTl, W2h, d == KC - 1)
                    ins.then_inc(S["lin2_ps"], 1)

            steps(pe, step, FIRST, LAST, LO, HI)
    nc.clear_and_free_semaphores(sems)
    nc.all_engine_barrier()


def node_phase(nc, T):
    ident, minus_r, plus_r, bias_r = T["ident"], T["minus_r"], T["plus_r"], T["bias_r"]
    half_col, eps_col, agg, xn_all = T["half_col"], T["eps_col"], T["agg"], T["xn_all"]
    x1_all, xlTh, xlTl = T["x1_all"], T["xlTh"], T["xlTl"]
    KK = 2 * KC

    ctx = ExitStack()
    with ctx:
        def sb(name, shape, dt=F32):
            return ctx.enter_context(nc.sbuf_tensor(name, shape, dt))

        def pb(name, shape):
            return ctx.enter_context(nc.psum_tensor(name, shape, F32))

        def sem(name):
            return ctx.enter_context(nc.semaphore("n_" + name))

        w_raw = sb("w_raw", [P, KK, HID])
        w3h = sb("w3h", [P, KK, HID], F32R)
        w3l = sb("w3l", [P, KK, HID], F32R)
        w4h = sb("w4h", [P, KC, HID], F32R)
        w4l = sb("w4l", [P, KC, HID], F32R)
        gamma_b = sb("gamma_b", [NB, HID])
        beta_b = sb("beta_b", [NB, HID])
        x_sl = sb("x_sl", [NB, 2, HID])
        cat_op = sb("cat_op", [NE, 2, 2 * HID])
        catTh = sb("catTh", [P, 2, KK * NE], F32R)
        catTl = sb("catTl", [P, 2, KK * NE], F32R)
        u = sb("u", [NE, 2, HID])
        uTh = sb("uTh", [P, 2, KC * NE], F32R)
        uTl = sb("uTl", [P, 2, KC * NE], F32R)
        y = sb("y", [NB, 2, HID])
        xl_op = sb("xl_op", [NE, 2, HID])
        stats = sb("n_stats", [NB, 2, 6])
        mv = sb("n_mv", [NB, 2, 2])
        rs = sb("n_rs", [NB, 2, 5])

        ps_c = pb("ps_c", [P, 2, 512])
        ps_u = pb("ps_u", [P, 2, 512])
        ps_v = pb("ps_v", [P, 512])
        ps_o = pb("ps_o", [P, 2, 512])
        ps_x = pb("ps_x", [P, 512])

        names = ("w3_in w4_in gb_in w3_hi w3_lo w4_hi w4_lo zeroed op_ready cat_ps cat_hi cat_lo lin_ps bounded exp sq ln quot "
                 "u_ready uT_ps uT_hi uT_lo out_ps y_ready xb_ready x1_ready x1_stats post var_y rstd_y var_x rstd_x xl_ready x1_done xlT_ps xlT_hi xlT_lo").split()
        S = {n: sem(n) for n in names}
        x_in = [sem(f"x_in{k}") for k in range(2)]
        block = ctx.enter_context(nc.Block())
        FIRST, LAST, LO, HI = -1, BLOCKS + 2, 5, BLOCKS - 2

        @block.sync
        def _(sp):
            sp.dma_start(w_raw[:], T["W3"].rearrange("(k p) n -> p k n", p=P)).then_inc(S["w3_in"], 16)
            sp.dma_start(gamma_b[:], T["gamma"].rearrange("(a n) -> a n", a=1).to_broadcast([NB, HID])).then_inc(S["gb_in"], 16)
            sp.dma_start(beta_b[:], T["beta"].rearrange("(a n) -> a n", a=1).to_broadcast([NB, HID])).then_inc(S["gb_in"], 16)
            sp.wait_ge(S["w3_lo"], KC)
            sp.dma_start(w_raw[:, 0:KC, :], T["W4"].rearrange("(k p) n -> p k n", p=P)).then_inc(S["w4_in"], 16)
            x_rows = T["x"].rearrange("(i p) d -> i p d", p=NB)

            def step(i, c):
                t, k, _ = item(i, c + 1)
                if within(t, BLOCKS):
                    need(sp, S["x1_done"], t - 1)
                    sp.dma_start(x_sl[:, k, :], x_rows[bass.ds(t, 1)].rearrange("a p d -> (a p) d")).then_inc(x_in[k], 16)

            steps(sp, step, FIRST, LAST, LO, HI)

        @block.gpsimd
        def _(pool):
            nc.gpsimd.memset(cat_op[:], 0.0).then_inc(S["zeroed"], 1)
            nc.gpsimd.memset(u[:], 0.0).then_inc(S["zeroed"], 1)
            nc.gpsimd.memset(xl_op[:], 0.0).then_inc(S["zeroed"], 1)
            pool.wait_ge(S["zeroed"], 3)
            pool.wait_ge(S["gb_in"], 32)

            def step(i, c):
                t, k, _ = item(i, c + 1)
                if within(t, BLOCKS):
                    need(pool, S["cat_ps"], t - 1)
                    nc.gpsimd.tensor_copy(cat_op[0:NB, k, 0:HID], xn_all[:, bass.ds(t, 1), :].rearrange("p a d -> p (a d)"))
                    nc.gpsimd.tensor_copy(cat_op[0:NB, k, HID:2 * HID], agg[:, bass.ds(t, 1), :].rearrange("p a d -> p (a d)")).then_inc(S["op_ready"], 1)
                p, kp, used = item(i, c - 1)
                if within(p, BLOCKS):
                    pool.wait_ge(x_in[kp], used * 16 + 16)
                    nc.gpsimd.tensor_tensor(x_sl[:, kp, :], x_sl[:, kp, :], beta_b[:], ALU.add).then_inc(S["xb_ready"], 1)

            steps(pool, step, FIRST, LAST, LO, HI)

        @block.scalar
        def _(act):
            nc.scalar.preload_act_table_set(EXP_LN_SET)
            act.wait_ge(S["w3_in"], 16)
            for q in range(KK):
                nc.scalar.activation(w3h[:, q, :], w_raw[:, q, :], ACT.Copy).then_inc(S["w3_hi"], 1)
            act.wait_ge(S["w4_in"], 16)
            for q in range(KC):
                nc.scalar.activation(w4h[:, q, :], w_raw[:, q, :], ACT.Copy).then_inc(S["w4_hi"], 1)

            def rstd(n, t, var, ready):
                act.wait_ge(S[var], t + 1)
                nc.scalar.activation(rs[:, n, 0:1], mv[:, n, 1:2], ACT.Ln, bias=eps_col[0:NB, :]).then_inc(S[ready], 1)
                act.wait_ge(S[ready], t * 2 + 1)
                nc.scalar.activation(rs[:, n, 1:2], rs[:, n, 0:1], ACT.Exp, scale=-0.5).then_inc(S[ready], 1)

            def step(i, c):
                v, kv, _ = item(i, c - 1)
                if within(v, BLOCKS):
                    act.wait_ge(S["uT_ps"], v + 1)
                    need(act, S["out_ps"], v - 1)
                    nc.scalar.activation(uTh[:, kv, :], ps_v[:, 0:KC * NE], ACT.Copy).then_inc(S["uT_hi"], 1)
                t, k, _ = item(i, c)
                p, kp, _ = item(i, c - 2)
                if within(p, BLOCKS):
                    rstd(0, p, "var_y", "rstd_y")
                z, _, _ = item(i, c - 3)
                if within(z, BLOCKS):
                    act.wait_ge(S["xlT_ps"], z + 1)
                    nc.scalar.activation(xlTh[:, :, bass.ds(z * NE, NE)], ps_x[:, 0:KC * NE].rearrange("p (q n) -> p q n", q=KC), ACT.Copy).then_inc(S["xlT_hi"], 1)
                if within(t, BLOCKS):
                    act.wait_ge(S["bounded"], t + 1)
                    nc.scalar.activation(u[0:NB, k, :], u[0:NB, k, :], ACT.Exp).then_inc(S["exp"], 1)
                n, kn, _ = item(i, c + 1)
                if within(n, BLOCKS):
                    act.wait_ge(S["cat_ps"], n + 1)
                    need(act, S["lin_ps"], n - 1)
                    nc.scalar.activation(catTh[:, kn, :].rearrange("p (a n) -> p a n", a=2), ps_c[:, :, 0:KC * NE], ACT.Copy).then_inc(S["cat_hi"], 1)
                if within(t, BLOCKS):
                    act.wait_ge(S["exp"], t + 1)
                    nc.scalar.activation(u[0:NB, k, :], u[0:NB, k, :], ACT.Square, bias=1.0).then_inc(S["sq"], 1)
                if within(t, BLOCKS):
                    act.wait_ge(S["sq"], t + 1)
                    nc.scalar.activation(u[0:NB, k, :], u[0:NB, k, :], ACT.Ln, bias=half_col[0:NB, :], scale=0.5).then_inc(S["ln"], 1)
                    act.wait_ge(S["ln"], t + 1)
                    nc.scalar.activation(u[0:NB, k, :], u[0:NB, k, :], ACT.Exp, scale=-1.0).then_inc(S["quot"], 1)
                if within(p, BLOCKS):
                    act.wait_ge(S["x1_ready"], p + 1)
                    nc.scalar.activation(x1_all[:, bass.ds(p, 1), :].rearrange("p a d -> p (a d)"), y[:, kp, :], ACT.Copy).then_inc(S["x1_done"], 1)
                    rstd(1, p, "var_x", "rstd_x")

            steps(act, step, FIRST, LAST, LO, HI)

        @block.vector
        def _(dve):
            for q in range(KK):
                dve.wait_ge(S["w3_hi"], q + 1)
                nc.vector.tensor_tensor(w3l[:, q, :], w_raw[:, q, :], f32(w3h[:, q, :]), ALU.subtract).then_inc(S["w3_lo"], 1)
            for q in range(KC):
                dve.wait_ge(S["w4_hi"], q + 1)
                nc.vector.tensor_tensor(w4l[:, q, :], w_raw[:, q, :], f32(w4h[:, q, :]), ALU.subtract).then_inc(S["w4_lo"], 1)
            dve.wait_ge(S["gb_in"], 32)
            dve.wait_ge(S["zeroed"], 3)

            PER = 10

            def step(i, c):
                p, kp, _ = item(i, c - 2)
                yk = y[:, kp, :]

                def link(m, ins):
                    ins.then_inc(S["post"], 1)
                    dve.wait_ge(S["post"], p * PER + m)

                def newton(n, ready, m):
                    dve.wait_ge(S[ready], p * 2 + 2)
                    link(m, nc.vector.tensor_tensor(rs[:, n, 2:3], rs[:, n, 1:2], rs[:, n, 1:2], ALU.mult))
                    link(m + 1, nc.vector.scalar_tensor_tensor(out=rs[:, n, 3:4], in0=mv[:, n, 1:2], scalar=EPS, in1=rs[:, n, 2:3], op0=ALU.add, op1=ALU.mult))
                    link(m + 2, nc.vector.tensor_scalar(rs[:, n, 4:5], rs[:, n, 3:4], -0.5, 1.5, ALU.mult, ALU.add))
                    link(m + 3, nc.vector.tensor_tensor(rs[:, n, 2:3], rs[:, n, 1:2], rs[:, n, 4:5], ALU.mult))

                v, kv, _ = item(i, c - 1)
                if within(v, BLOCKS):
                    dve.wait_ge(S["uT_hi"], v + 1)
                    nc.vector.tensor_tensor(uTl[:, kv, :], ps_v[:, 0:KC * NE], f32(uTh[:, kv, :]), ALU.subtract).then_inc(S["uT_lo"], 1)
                if within(p, BLOCKS):
                    dve.wait_ge(S["out_ps"], p + 1)
                    nc.vector.tensor_tensor(yk, xn_all[:, bass.ds(p, 1), :].rearrange("p a d -> p (a d)"), ps_o[0:NB, kp, :], ALU.subtract).then_inc(S["y_ready"], 1)
                    dve.wait_ge(S["y_ready"], p + 1)
                    link(1, nc.vector.bn_stats(out=stats[:, 0, :], in_=yk))
                    nc.vector.tensor_copy(rs[:, 0, 4:5], eps_col[0:NB, :])
                    nc.vector.bn_aggr(out=mv[:, 0, :], in_=stats[:, 0, :]).then_inc(S["var_y"], 1)
                if within(p, BLOCKS):
                    newton(0, "rstd_y", 2)
                t, k, _ = item(i, c)
                if within(t, BLOCKS):
                    dve.wait_ge(S["lin_ps"], t + 1)
                    need(dve, S["uT_ps"], t - 1)
                    nc.vector.tensor_scalar(u[0:NB, k, :], ps_u[0:NB, k, :], X_MAX, None, ALU.min).then_inc(S["bounded"], 1)
                n, kn, _ = item(i, c + 1)
                if within(n, BLOCKS):
                    dve.wait_ge(S["cat_hi"], n + 1)
                    nc.vector.tensor_tensor(catTl[:, kn, :].rearrange("p (a n) -> p a n", a=2), ps_c[:, :, 0:KC * NE],
                                            f32(catTh[:, kn, :]).rearrange("p (a n) -> p a n", a=2), ALU.subtract).then_inc(S["cat_lo"], 1)
                if within(p, BLOCKS):
                    link(6, nc.vector.scalar_tensor_tensor(out=yk, in0=yk, scalar=mv[:, 0, 0:1], in1=gamma_b[:], op0=ALU.subtract, op1=ALU.mult))
                    dve.wait_ge(S["xb_ready"], p + 1)
                    nc.vector.scalar_tensor_tensor(out=yk, in0=yk, scalar=rs[:, 0, 2:3], in1=x_sl[:, kp, :], op0=ALU.mult, op1=ALU.add).then_inc(S["x1_ready"], 1)
                z, _, _ = item(i, c - 3)
                if within(z, BLOCKS):
                    dve.wait_ge(S["xlT_hi"], z + 1)
                    cols = (slice(None), slice(None), bass.ds(z * NE, NE))
                    nc.vector.tensor_tensor(xlTl[cols], ps_x[:, 0:KC * NE].rearrange("p (q n) -> p q n", q=KC), f32(xlTh[cols]), ALU.subtract).then_inc(S["xlT_lo"], 1)
                if within(p, BLOCKS):
                    dve.wait_ge(S["x1_ready"], p + 1)
                    nc.vector.bn_stats(out=stats[:, 1, :], in_=yk).then_inc(S["x1_stats"], 1)
                if within(t, BLOCKS):
                    dve.wait_ge(S["quot"], t + 1)
                    nc.vector.scalar_tensor_tensor(out=u[0:NB, k, :], in0=u[0:NB, k, :], scalar=1.0, in1=ps_u[0:NB, k, :],
                                                   op0=ALU.subtract, op1=ALU.mult).then_inc(S["u_ready"], 1)
                if within(p, BLOCKS):
                    dve.wait_ge(S["x1_stats"], p + 1)
                    nc.vector.tensor_copy(rs[:, 1, 4:5], eps_col[0:NB, :])
                    nc.vector.bn_aggr(out=mv[:, 1, :], in_=stats[:, 1, :]).then_inc(S["var_x"], 1)
                    newton(1, "rstd_x", 7)
                    need(dve, S["xlT_ps"], p - 1)
                    nc.vector.tensor_scalar(xl_op[0:NB, kp, :], yk, mv[:, 1, 0:1], rs[:, 1, 2:3], ALU.subtract, ALU.mult).then_inc(S["xl_ready"], 1)

            steps(dve, step, FIRST, LAST, LO, HI)

        @block.tensor
        def _(pe):
            pe.wait_ge(S["w3_lo"], KK)

            def step(i, c):
                t, k, _ = item(i, c)
                o = ps_u[0:NE, k, :]

                def lin(first, end):
                    for q in range(first, end):
                        hi, lo = catTh[:, k, q * NE:(q + 1) * NE], catTl[:, k, q * NE:(q + 1) * NE]
                        nc.tensor.matmul(o, hi, w3h[:, q, :], start=False, stop=False)
                        nc.tensor.matmul(o, hi, w3l[:, q, :], start=False, stop=False)
                        ins = nc.tensor.matmul(o, lo, w3h[:, q, :], start=False, stop=(q == KK - 1))
                    return ins

                if within(t, BLOCKS):
                    pe.wait_ge(S["cat_lo"], t + 1)
                    need(pe, S["u_ready"], t - 1)
                    nc.tensor.matmul(o, plus_r[:, 0:NE], bias_r[:, 2, :], start=True, stop=False)
                    lin(0, KC)
                v, kv, _ = item(i, c - 1)
                if within(v, BLOCKS):
                    pe.wait_ge(S["u_ready"], v + 1)
                    need(pe, S["uT_lo"], v)
                    for q in range(KC):
                        ins = nc.tensor.transpose(ps_v[:, q * NE:(q + 1) * NE], u[:, kv, q * P:(q + 1) * P], ident[0:NE, 0:NE])
                    ins.then_inc(S["uT_ps"], 1)
                if within(t, BLOCKS):
                    lin(KC, KK).then_inc(S["lin_ps"], 1)
                z, kz, _ = item(i, c - 3)
                if within(z, BLOCKS):
                    pe.wait_ge(S["xl_ready"], z + 1)
                    need(pe, S["xlT_lo"], z)
                    for q in range(KC):
                        ins = nc.tensor.transpose(ps_x[:, q * NE:(q + 1) * NE], xl_op[:, kz, q * P:(q + 1) * P], ident[0:NE, 0:NE])
                    ins.then_inc(S["xlT_ps"], 1)
                n, kn, _ = item(i, c + 1)
                if within(n, BLOCKS):
                    pe.wait_ge(S["op_ready"], n + 1)
                    need(pe, S["cat_lo"], n)
                    for q in range(KK):
                        ins = nc.tensor.transpose(ps_c[:, q // KC, (q % KC) * NE:(q % KC + 1) * NE], cat_op[:, kn, q * P:(q + 1) * P], ident[0:NE, 0:NE])
                    ins.then_inc(S["cat_ps"], 1)
                if within(v, BLOCKS):
                    pe.wait_ge(S["w4_lo"], KC)
                    pe.wait_ge(S["uT_lo"], v + 1)
                    need(pe, S["y_ready"], v - 1)
                    out2 = ps_o[0:NE, kv, :]
                    nc.tensor.matmul(out2, minus_r[:, 0:NE], bias_r[:, 3, :], start=True, stop=False)
                    for q in range(KC):
                        hi, lo = uTh[:, kv, q * NE:(q + 1) * NE], uTl[:, kv, q * NE:(q + 1) * NE]
                        nc.tensor.matmul(out2, hi, w4h[:, q, :], start=False, stop=False)
                        nc.tensor.matmul(out2, hi, w4l[:, q, :], start=False, stop=False)
                        ins = nc.tensor.matmul(out2, lo, w4h[:, q, :], start=False, stop=(q == KC - 1))
                    ins.then_inc(S["out_ps"], 1)

            steps(pe, step, FIRST, LAST, LO, HI)


def ffn_phase(nc, T):
    ident, ones, x1_all, xlTh, xlTl, mask_scr, out = T["ident"], T["ones"], T["x1_all"], T["xlTh"], T["xlTl"], T["mask_scr"], T["out"]
    E, FC = EXPERTS, FFN // P
    TOK = BLOCKS * NE
    NCH = 3
    CW = TOK // NCH

    ctx = ExitStack()
    with ctx:
        def sb(name, shape, dt=F32):
            return ctx.enter_context(nc.sbuf_tensor(name, shape, dt))

        def pb(name, shape):
            return ctx.enter_context(nc.psum_tensor(name, shape, F32))

        def sem(name):
            return ctx.enter_context(nc.semaphore("f_" + name))

        gate = sb("gate", [E, HID])
        gateTh = sb("gateTh", [P, KC, E], F32R)
        gateTl = sb("gateTl", [P, KC, E], F32R)
        logT = sb("logT", [E, TOK])
        row_order = sb("row_order", [NE, E])
        valid = sb("valid", [NE, 1])
        lg = sb("lg", [NE, BLOCKS, E])
        best = sb("best", [NE, 4, BLOCKS])
        hot1 = sb("hot1", [NE, BLOCKS, E])
        hot2 = sb("hot2", [NE, BLOCKS, E])
        rank_a = sb("rank_a", [NE, BLOCKS, E])
        rank_b = sb("rank_b", [NE, BLOCKS, E])
        wt = sb("wt", [NE, 4, BLOCKS])
        mask = sb("mask", [NE, BLOCKS, E])
        gw = sb("gw", [NE, BLOCKS, E])
        msum = sb("msum", [NE, E])
        inv = sb("inv", [P, E])
        maskT = sb("maskT", [E, TOK])
        gwT = sb("gwT", [E, TOK])
        w1_raw = sb("f_w1_raw", [P, 2, FC, HID])
        w2_raw = sb("f_w2_raw", [P, 2, KC, FFN])
        w1Th = sb("w1Th", [P, 2, FC, HID], F32R)
        w1Tl = sb("w1Tl", [P, 2, FC, HID], F32R)
        mask_b = sb("mask_b", [P, 2, TOK])
        hs = sb("hs", [P, FC, TOK])
        junk_h = sb("junk_h", [P, TOK])
        junk_y = sb("junk_y", [P, FFN])
        hsum = sb("hsum", [P, 2, FC])
        hm = sb("hm", [P, 2, FC])
        hm_b = sb("hm_b", [P, 2, FC, P])
        y_col = sb("y_col", [P, 2, KC])
        yT = sb("yT", [P, KC, E])
        y = sb("y_mean", [E, HID])
        res = sb("res", [NB, 2, HID])

        ps_hh = pb("ps_hh", [P, FC, NCH, 512])
        ps_w = pb("ps_w", [P, 512])
        ps_b = pb("ps_b2", [P, 512])

        names = ("gate_in const gateT_ps gate_hi gate_lo log_ps log_out lg_ps step a_step d_step mask_ready maskT_ps maskT_out "
                 "mask_stored gw_ps gw_out cnt_ps w1T_ps w1T_hi w1T_lo h_ps h_act h_sum hm_step y_step hm_ready mean_ps y_done yT_ps y_out res_ps res_done").split()
        S = {n: sem(n) for n in names}
        w1_in, w2_in, mask_in, res_out = ([sem(f"{n}{k}") for k in range(2)] for n in ("w1_in", "w2_in", "mask_in", "res_out"))
        block = ctx.enter_context(nc.Block())
        FIRST, LAST, LO, HI = -1, E, 3, E - 2

        def flat(ap):
            return ap.rearrange("p b e -> p (b e)")

        @block.sync
        def _(sp):
            sp.dma_start(gate[:], T["gate_w"]).then_inc(S["gate_in"], 16)
            w1_rows = T["w1"].rearrange("e (c p) d -> e p c d", p=P)
            w2_rows = T["w2"].rearrange("e (q p) f -> e p q f", p=P)

            def step(i, c):
                e, k, used = item(i, c + 1)
                if within(e, E):
                    need(sp, S["w1T_ps"], (e - 1) * FC)
                    sp.dma_start(w1_raw[:, k], w1_rows[bass.ds(e, 1)].rearrange("a p c d -> (a p) c d")).then_inc(w1_in[k], 16)
                e, k, used = item(i, c)
                if within(e, E):
                    if isinstance(e, int) and e == 0:
                        sp.wait_ge(S["maskT_out"], 1)
                        sp.dma_start(mask_scr, maskT[:]).then_inc(S["mask_stored"], 16)
                        sp.wait_ge(S["mask_stored"], 16)
                    need(sp, S["h_sum"], (e - 1) * FC)
                    sp.dma_start(mask_b[:, k], mask_scr[bass.ds(e, 1), :].to_broadcast([P, TOK])).then_inc(mask_in[k], 16)
                    need(sp, S["y_done"], e - 1)
                    sp.dma_start(w2_raw[:, k], w2_rows[bass.ds(e, 1)].rearrange("a p q f -> (a p) q f")).then_inc(w2_in[k], 16)

            steps(sp, step, FIRST, LAST, LO, HI)
            for t in range(BLOCKS):
                sp.wait_ge(S["res_done"], t + 1)
                sp.dma_start(out[t * NB:(t + 1) * NB, :], res[:, t % 2, :]).then_inc(res_out[t % 2], 16)
            for k in range(2):
                sp.wait_ge(res_out[k], 16 * (BLOCKS // 2))

        @block.gpsimd
        def _(pool):
            nc.gpsimd.iota(row_order[:], [[-1, E]], base=E, channel_multiplier=0, allow_small_or_imprecise_dtypes=True).then_inc(S["const"], 1)
            nc.gpsimd.memset(valid[:], 1.0).then_inc(S["const"], 1)
            pool.wait_ge(S["const"], 2)
            nc.gpsimd.affine_select(out=valid[:], in_=valid[:], compare_op=ALU.not_equal, fill=0.0, base=-NB,
                                    pattern=[[0, 1]], channel_multiplier=1).then_inc(S["const"], 1)

        @block.scalar
        def _(act):
            act.wait_ge(S["gateT_ps"], 1)
            nc.scalar.activation(gateTh[:].rearrange("p q e -> p (q e)"), ps_w[:, 0:KC * E], ACT.Copy).then_inc(S["gate_hi"], 1)
            act.wait_ge(S["log_ps"], 1)
            nc.scalar.activation(logT[:].rearrange("e (n c) -> e n c", n=NCH), ps_hh[0:E, 0, :, 0:CW], ACT.Copy).then_inc(S["log_out"], 1)
            act.wait_ge(S["d_step"], 1)
            nc.scalar.activation(wt[:, 1, :], wt[:, 0, :], ACT.Exp).then_inc(S["a_step"], 1)
            act.wait_ge(S["maskT_ps"], 1)
            nc.scalar.activation(maskT[:].rearrange("e (n c) -> e n c", n=NCH), ps_hh[0:E, 0, :, 0:CW], ACT.Copy).then_inc(S["maskT_out"], 1)
            act.wait_ge(S["gw_ps"], 1)
            nc.scalar.activation(gwT[:].rearrange("e (n c) -> e n c", n=NCH), ps_hh[0:E, 1, :, 0:CW], ACT.Copy).then_inc(S["gw_out"], 1)

            def step(i, c):
                e, k, _ = item(i, c)
                n, kn, _ = item(i, c + 1)
                for f in range(FC):
                    if within(e, E):
                        act.wait_ge(S["h_ps"], e * FC + (f + 1))
                        need(act, S["h_sum"], (e - 1) * FC + (f + 1))
                        nc.scalar.activation(hs[:, f].rearrange("p (n c) -> p n c", n=NCH), ps_hh[:, f, :, 0:CW], ACT.Silu).then_inc(S["h_act"], 1)
                    if within(n, E):
                        act.wait_ge(S["w1T_ps"], n * FC + (f + 1))
                        need(act, S["h_ps"], (n - 2) * FC + (f + 1))
                        nc.scalar.activation(w1Th[:, kn, f, :], ps_w[:], ACT.Copy).then_inc(S["w1T_hi"], 1)

            steps(act, step, FIRST, LAST, LO, HI)
            act.wait_ge(S["yT_ps"], 1)
            nc.scalar.activation(y[:], ps_w[0:E, :], ACT.Copy).then_inc(S["y_out"], 1)

        @block.vector
        def _(dve):
            dve.wait_ge(S["gate_hi"], 1)
            nc.vector.tensor_tensor(gateTl[:].rearrange("p q e -> p (q e)"), ps_w[:, 0:KC * E], f32(gateTh[:]).rearrange("p q e -> p (q e)"), ALU.subtract).then_inc(S["gate_lo"], 1)
            c = Count(dve, S["step"])

            def spread(ap):
                return ap.unsqueeze(2).to_broadcast([NE, BLOCKS, E])

            order = row_order[:].unsqueeze(1).to_broadcast([NE, BLOCKS, E])
            dve.wait_ge(S["const"], 3)
            dve.wait_ge(S["lg_ps"], 1)
            c.step(nc.vector.tensor_copy(flat(lg[:]), ps_b[0:NE, 0:BLOCKS * E]))

            def largest(src, n, hot):
                c.step(nc.vector.tensor_reduce(out=best[:, n, :], in_=src, axis=AX_X, op=ALU.max))
                c.step(nc.vector.tensor_tensor(rank_a[:], src, spread(best[:, n, :]), ALU.is_equal))
                c.step(nc.vector.tensor_tensor(rank_a[:], rank_a[:], order, ALU.mult))
                c.step(nc.vector.tensor_reduce(out=best[:, 2 + n, :], in_=rank_a[:], axis=AX_X, op=ALU.max))
                c.step(nc.vector.tensor_tensor(hot, order, spread(best[:, 2 + n, :]), ALU.is_equal))

            largest(lg[:], 0, hot1[:])
            c.step(nc.vector.scalar_tensor_tensor(out=flat(rank_b[:]), in0=flat(hot1[:]), scalar=-1e30, in1=flat(lg[:]), op0=ALU.mult, op1=ALU.add))
            largest(rank_b[:], 1, hot2[:])
            nc.vector.tensor_tensor(wt[:, 0, :], best[:, 1, :], best[:, 0, :], ALU.subtract).then_inc(S["d_step"], 1)
            c.step(nc.vector.tensor_tensor(mask[:], hot1[:], hot2[:], ALU.add))
            nc.vector.tensor_scalar(flat(mask[:]), flat(mask[:]), valid[:, 0:1], None, ALU.mult).then_inc(S["mask_ready"], 1)
            dve.wait_ge(S["mask_ready"], 1)
            nc.vector.tensor_reduce(out=msum[:], in_=mask[:].rearrange("p b e -> p e b"), axis=AX_X, op=ALU.add).then_inc(S["mask_ready"], 1)
            dve.wait_ge(S["a_step"], 1)
            c.step(nc.vector.tensor_scalar(wt[:, 2, :], wt[:, 1, :], 1.0, None, ALU.add))
            c.step(nc.vector.reciprocal(wt[:, 3, :], wt[:, 2, :]))
            c.step(nc.vector.tensor_tensor(wt[:, 2, :], wt[:, 3, :], wt[:, 1, :], ALU.mult))
            c.inc(nc.vector.tensor_tensor(hot1[:], hot1[:], spread(wt[:, 3, :]), ALU.mult))
            c.step(nc.vector.tensor_tensor(hot2[:], hot2[:], spread(wt[:, 2, :]), ALU.mult))
            nc.vector.tensor_tensor(gw[:], hot1[:], hot2[:], ALU.add).then_inc(S["mask_ready"], 1)
            dve.wait_ge(S["cnt_ps"], 1)
            c.step(nc.vector.tensor_scalar(inv[:], ps_b[:, 256:256 + E], 1.0, None, ALU.max))
            c.step(nc.vector.reciprocal(inv[:], inv[:]))

            def step(i, c):
                e, k, used = item(i, c)
                n, kn, _ = item(i, c + 1)
                o, ko, oused = item(i, c - 1)
                for f in range(FC):
                    if within(n, E):
                        dve.wait_ge(S["w1T_hi"], n * FC + (f + 1))
                        nc.vector.tensor_tensor(w1Tl[:, kn, f, :], ps_w[:], f32(w1Th[:, kn, f, :]), ALU.subtract).then_inc(S["w1T_lo"], 1)
                    if f == 0 and within(o, E):
                        dve.wait_ge(S["mean_ps"], o + 1)
                        dve.wait_ge(w2_in[ko], oused * 16 + 16)
                        for q in range(KC):
                            need(dve, S["y_step"], o * KC + q)
                            ins = nc.vector.tensor_tensor_reduce(out=junk_y[:], in0=w2_raw[:, ko, q, :], in1=ps_b[:, 0:FFN], scale=1.0, scalar=0.0,
                                                                 op0=ALU.mult, op1=ALU.add, accum_out=y_col[:, ko, q:q + 1])
                            ins.then_inc(S["y_step"], 1)
                        dve.wait_ge(S["y_step"], o * KC + KC)
                        nc.vector.tensor_copy(yT[:, :, bass.ds(o, 1)].rearrange("p q a -> p (q a)"), y_col[:, ko, :]).then_inc(S["y_done"], 1)
                    if within(e, E):
                        dve.wait_ge(S["h_act"], e * FC + (f + 1))
                        dve.wait_ge(mask_in[k], used * 16 + 16)
                        need(dve, S["h_sum"], e * FC + f)
                        nc.vector.tensor_tensor_reduce(out=junk_h[:], in0=hs[:, f, :], in1=mask_b[:, k, :], scale=1.0, scalar=0.0,
                                                       op0=ALU.mult, op1=ALU.add, accum_out=hsum[:, k, f:f + 1]).then_inc(S["h_sum"], 1)
                if within(e, E):
                    dve.wait_ge(S["h_sum"], e * FC + FC)
                    nc.vector.tensor_scalar(hm[:, k, :], hsum[:, k, :], inv[:, bass.ds(e, 1)], None, ALU.mult).then_inc(S["hm_step"], 1)
                    dve.wait_ge(S["hm_step"], e + 1)
                    for f in range(FC):
                        ins = nc.vector.tensor_scalar(hm_b[:, k, f, :], ones[:], hm[:, k, f:f + 1], None, ALU.mult)
                    ins.then_inc(S["hm_ready"], 1)

            steps(dve, step, FIRST, LAST, LO, HI)
            for t in range(BLOCKS):
                dve.wait_ge(S["res_ps"], t + 1)
                need(dve, res_out[t % 2], 16 * (t // 2))
                nc.vector.tensor_tensor(res[:, t % 2, :], x1_all[:, t, :], ps_hh[0:NB, t % 2, 0, :], ALU.add).then_inc(S["res_done"], 1)

        @block.tensor
        def _(pe):
            pe.wait_ge(S["gate_in"], 16)
            for q in range(KC):
                ins = nc.tensor.transpose(ps_w[:, q * E:(q + 1) * E], gate[:, q * P:(q + 1) * P], ident[0:E, 0:E])
            ins.then_inc(S["gateT_ps"], 1)
            pe.wait_ge(S["gate_lo"], 1)
            for n in range(NCH):
                cols = slice(n * CW, (n + 1) * CW)
                for q in range(KC):
                    o = ps_hh[0:E, 0, n, 0:CW]
                    nc.tensor.matmul(o, gateTh[:, q, :], xlTh[:, q, cols], start=(q == 0), stop=False)
                    nc.tensor.matmul(o, gateTl[:, q, :], xlTh[:, q, cols], start=False, stop=False)
                    ins = nc.tensor.matmul(o, gateTh[:, q, :], xlTl[:, q, cols], start=False, stop=(q == KC - 1))
            ins.then_inc(S["log_ps"], 1)
            pe.wait_ge(S["log_out"], 1)
            for b in range(BLOCKS):
                ins = nc.tensor.transpose(ps_b[0:NE, b * E:(b + 1) * E], logT[:, b * NE:(b + 1) * NE], ident[0:E, 0:E])
            ins.then_inc(S["lg_ps"], 1)
            pe.wait_ge(S["mask_ready"], 2)
            nc.tensor.matmul(ps_b[:, 256:256 + E], ones[0:NE, :], msum[:], start=True, stop=True).then_inc(S["cnt_ps"], 1)

            def rows_of(src, f, signal):
                for b in range(BLOCKS):
                    n0, n1 = b * NE // CW, ((b + 1) * NE - 1) // CW
                    for n in range(n0, n1 + 1):
                        lo, hi = max(b * NE, n * CW), min((b + 1) * NE, (n + 1) * CW)
                        ins = nc.tensor.matmul(ps_hh[0:E, f, n, lo - n * CW:hi - n * CW], src[:, b, :],
                                               ident[0:NE, lo - b * NE:hi - b * NE], start=True, stop=True)
                ins.then_inc(S[signal], 1)

            rows_of(mask, 0, "maskT_ps")
            pe.wait_ge(S["mask_ready"], 3)
            rows_of(gw, 1, "gw_ps")
            pe.wait_ge(S["maskT_out"], 1)
            pe.wait_ge(S["gw_out"], 1)

            def step(i, c):
                e, k, _ = item(i, c)
                n, kn, nused = item(i, c + 1)
                o, ko, _ = item(i, c - 1)
                for f in range(FC):
                    if within(e, E):
                        pe.wait_ge(S["w1T_lo"], e * FC + (f + 1))
                        need(pe, S["h_act"], (e - 1) * FC + (f + 1))
                        for q in range(KC):
                            hi, lo = w1Th[:, k, f, q * P:(q + 1) * P], w1Tl[:, k, f, q * P:(q + 1) * P]
                            for w, xs in ((hi, xlTh), (hi, xlTl), (lo, xlTh)):
                                for m in range(NCH):
                                    ins = nc.tensor.matmul(ps_hh[:, f, m, 0:CW], w, xs[:, q, m * CW:(m + 1) * CW],
                                                           start=(q == 0 and w is hi and xs is xlTh), stop=(q == KC - 1 and w is lo))
                        ins.then_inc(S["h_ps"], 1)
                    if within(n, E):
                        if f == 0:
                            pe.wait_ge(w1_in[kn], nused * 16 + 16)
                        need(pe, S["w1T_lo"], n * FC + f)
                        for q in range(KC):
                            ins = nc.tensor.transpose(ps_w[:, q * P:(q + 1) * P], w1_raw[:, kn, f, q * P:(q + 1) * P], ident[:])
                        ins.then_inc(S["w1T_ps"], 1)
                    if f == 0 and within(o, E):
                        pe.wait_ge(S["hm_ready"], o + 1)
                        need(pe, S["y_done"], o)
                        for g in range(FC):
                            ins = nc.tensor.matmul(ps_b[:, g * P:(g + 1) * P], hm_b[:, ko, g, :], ident[:], start=True, stop=True)
                        ins.then_inc(S["mean_ps"], 1)

            steps(pe, step, FIRST, LAST, LO, HI)
            pe.wait_ge(S["y_done"], E)
            for q in range(KC):
                ins = nc.tensor.transpose(ps_w[0:E, q * P:(q + 1) * P], yT[:, q, :], ident[:])
            ins.then_inc(S["yT_ps"], 1)
            pe.wait_ge(S["y_out"], 1)
            for t in range(BLOCKS):
                need(pe, S["res_done"], t - 1)
                nc.tensor.matmul(ps_hh[0:NB, t % 2, 0, :], gwT[:, t * NE:t * NE + NB], y[:], start=True, stop=True).then_inc(S["res_ps"], 1)


_INS = ["x", "src", "dst", "edge_attr_64", "L0_gnn_W1", "L0_gnn_b1", "L0_gnn_W2", "L0_gnn_b2", "L0_gnn_W3", "L0_gnn_b3",
        "L0_gnn_W4", "L0_gnn_b4", "L0_gnn_gamma", "L0_gnn_beta", "L0_ffn_gate_weight", "L0_ffn_w1", "L0_ffn_w2"]
_OUTS = [((NODES, HID), "float32")]


def kernel(**inputs):
    import numpy as _np
    import concourse.bacc as _bacc
    from concourse import mybir as _mybir
    from concourse.bass_utils import run_bass_kernel_spmd as _run

    nc = _bacc.Bacc("TRN2", target_bir_lowering=False, num_devices=1)
    arrays, args = {}, []
    for name in _INS:
        a = _np.ascontiguousarray(inputs[name])
        arrays[f"in_{name}_dram"] = a
        args.append(nc.dram_tensor(f"in_{name}_dram", a.shape, _mybir.dt.from_np(a.dtype), kind="ExternalInput").ap())
    for i, (shape, dtype) in enumerate(_OUTS):
        dt = _mybir.dt.from_np(_np.dtype(dtype))
        args.append(nc.dram_tensor(f"out_{i}_dram", shape, dt, kind="ExternalOutput").ap())
    gnn_ffn_kernel(nc, *args)
    r = _run(nc, [arrays], core_ids=[0])
    return r.results[0]["out_0_dram"]
```

```python
from contextlib import ExitStack

import concourse.bass as bass
from concourse import mybir

F32 = mybir.dt.float32
F32R = mybir.dt.float32r
I32 = mybir.dt.int32
ALU = mybir.AluOpType
ACT = mybir.ActivationFunctionType
AX_X = mybir.AxisListType.X

NODES, HID, EDGES, EDIM = 1250, 512, 20000, 64
EXPERTS, FFN = 16, 256
P = 128
NB = 125
NE = NB + 1
BLOCKS = NODES // NB
KC = HID // P
EP = 125
EJ = EDGES // EP
TILES = (EDGES + BLOCKS * (P - 1)) // P
PAIRS = TILES // 2
EPS = 1e-5
EXP_MAX = float(2 ** 30)
X_MAX = 20.75
EXP_LN_SET = "natural_log_exp_and_others"
NO_NODE = 1 << 20
TOP_K = 2
ROUTE_TILES = (TOP_K * NODES + EXPERTS * (P - 1)) // P
assert EP == NB
assert TILES % 2 == 0 and PAIRS % 2 == 1


class Count:

    def __init__(self, eng, sem):
        self.eng, self.sem, self.n = eng, sem, 0

    def inc(self, ins):
        self.n += 1
        ins.then_inc(self.sem, 1)

    def wait(self):
        self.eng.wait_ge(self.sem, self.n)

    def step(self, ins):
        self.inc(ins)
        self.wait()


def f32(ap):
    return ap.bitcast(F32)


def need(eng, sem, n):
    if not isinstance(n, int) or n > 0:
        eng.wait_ge(sem, n)


def item(i, c, slots=2, unroll=None):
    unroll = unroll or slots
    return i * unroll + c, c % slots, i * (unroll // slots) + c // slots


def within(n, count):
    return not isinstance(n, int) or 0 <= n < count


def steps(eng, step, first, last, lo, hi, unroll=2):
    for s in range(first, lo):
        step(0, s)
    with eng.Fori(0, (hi - lo + 1) // unroll) as i:
        for a in range(unroll):
            step(i, lo + a)
    for s in range(hi + 1, last + 1):
        step(0, s)


def gnn_ffn_kernel(nc, x, src, dst, edge_attr, W1, b1, W2, b2, W3, b3, W4, b4, gamma, beta, gate_w, w1, w2, out):
    top = ExitStack()
    with top:
        def dram(name, shape, dt):
            return nc.dram_tensor(name, shape, dt).ap()

        src_table = dram("src_table", (NODES, HID), F32)
        dst_table = dram("dst_table", (NODES, HID), F32)
        ea_scr = dram("ea_scr", (EDGES + P, EDIM), F32)
        idx_scr = dram("idx_scr", (EDGES + P, 3), I32)
        xl_scr = dram("xl_scr", (NODES, HID), F32)
        route_scr = dram("route_scr", (ROUTE_TILES * P, 1), I32)

        def sb(name, shape, dt, ctx=top):
            return ctx.enter_context(nc.sbuf_tensor(name, shape, dt))

        ident = sb("ident", [P, P], F32)
        ones = sb("ones", [P, P], F32)
        minus_r = sb("minus_r", [2, P], F32R)
        plus_r = sb("plus_r", [2, P], F32R)
        bias_r = sb("bias_r", [2, 4, HID], F32R)
        eps_col = sb("eps_col", [P, 1], F32)
        half_col = sb("half_col", [P, 1], F32)
        agg = sb("agg", [NB, BLOCKS, HID], F32)
        tri = sb("tri", [NB, NB], F32)
        lg = sb("lg", [NB, BLOCKS, 2 * EXPERTS], F32)

        node_ctx = ExitStack()
        xn_all = sb("xn_all", [NB, BLOCKS, HID], F32, node_ctx)
        w_raw = sb("w_raw", [P, 2 * KC, HID], F32, node_ctx)
        w1h = w3h = sb("w1h_w3h", [P, 2 * KC, HID], F32R, node_ctx)
        w1l = w3l = sb("w1l_w3l", [P, 2 * KC, HID], F32R, node_ctx)
        edge_ctx = ExitStack()
        W2h = sb("W2h", [P, KC, HID], F32R, edge_ctx)
        W2l = sb("W2l", [P, KC, HID], F32R, edge_ctx)
        Wch = sb("Wch", [P, HID], F32R, edge_ctx)
        Wcl = sb("Wcl", [P, HID], F32R, edge_ctx)
        start_i = sb("start_i", [P, TILES], I32, edge_ctx)
        block_i = sb("block_i", [P, TILES], I32, edge_ctx)
        block_off = sb("block_off", [P, TILES], F32, edge_ctx)
        iota_n = sb("iota_n", [P, NE], F32, edge_ctx)

        prologue(nc, locals())
        edge_phase(nc, locals())
        edge_ctx.close()

        x1_all = agg
        node_phase(nc, locals())
        node_ctx.close()
        ffn_phase(nc, locals())


def prologue(nc, T):
    x, src, dst, edge_attr = T["x"], T["src"], T["dst"], T["edge_attr"]
    W1, W2 = T["W1"], T["W2"]
    ident, ones, minus_r, plus_r, bias_r = T["ident"], T["ones"], T["minus_r"], T["plus_r"], T["bias_r"]
    eps_col, half_col, agg, tri = T["eps_col"], T["half_col"], T["agg"], T["tri"]
    W2h, W2l, Wch, Wcl = T["W2h"], T["W2l"], T["Wch"], T["Wcl"]
    start_i, block_i, block_off, iota_n = T["start_i"], T["block_i"], T["block_off"], T["iota_n"]
    w1_raw, w1h, w1l = T["w_raw"], T["w1h"], T["w1l"]
    xn_all, src_table, dst_table = T["xn_all"], T["src_table"], T["dst_table"]
    ea_scr, idx_scr = T["ea_scr"], T["idx_scr"]

    ctx, sems = ExitStack(), []
    with ctx:
        def sb(name, shape, dt):
            return ctx.enter_context(nc.sbuf_tensor(name, shape, dt))

        def pb(name, shape, dt=F32):
            return ctx.enter_context(nc.psum_tensor(name, shape, dt))

        def sem(name):
            sems.append(nc.alloc_semaphore(name))
            return sems[-1]

        wc_raw = sb("wc_raw", [P, HID], F32)
        bias_raw = sb("bias_raw", [2, 4, HID], F32)
        bias_hi = sb("bias_hi", [2, 4, HID], F32R)
        row_is1 = sb("row_is1", [P, 2], F32)
        x_raw = sb("x_raw", [P, BLOCKS, HID], F32)
        w2_raw = x_raw[:, 0:KC, :]
        rank = x_raw[0:EP, KC:2 * KC, :].rearrange("p a d -> p (a d)")[:, 0:(BLOCKS + 1) * EJ].rearrange("p (b j) -> p b j", j=EJ)
        xn_op = sb("xn_op", [NE, 2, HID], F32)
        xTh = sb("xTh", [P, 2, KC * NE], F32R)
        xTl = sb("xTl", [P, 2, KC * NE], F32R)
        tabs = sb("tabs", [NB, 2, 2, HID], F32)
        stats = sb("stats", [NB, BLOCKS, 6], F32)
        mv = sb("mv", [NB, BLOCKS, 2], F32)
        rs = sb("rs", [NB, 4, BLOCKS], F32)

        dst_i = sb("dst_i", [EP, EJ], I32)
        src_i = sb("src_i", [EP, EJ], I32)
        next_i = sb("next_i", [EP, EJ], I32)
        rec_i = sb("rec_i", [EP, EJ, 3], I32)
        tail_i = sb("tail_i", [P, 3], I32)
        tail_ea = sb("tail_ea", [P, EDIM], F32)
        below = sb("below", [EP, BLOCKS + 2, EJ], F32)
        row_cnt = sb("row_cnt", [EP, BLOCKS + 2], F32)
        first = sb("first", [P, BLOCKS + 2], F32)
        row_off = sb("row_off", [EP, BLOCKS + 2], F32)
        cnt_i = sb("cnt_i", [P, BLOCKS], I32)
        nt = sb("nt", [P, BLOCKS], F32)
        tbase = sb("tbase", [P, BLOCKS + 1], F32)
        off = sb("off", [P, BLOCKS + 1], F32)
        doff = sb("doff", [P, BLOCKS], F32)
        iota_t = sb("iota_t", [P, TILES], F32)
        reached = sb("reached", [P, BLOCKS, TILES], F32)
        start_f = sb("start_f", [P, TILES], F32)
        block_f = sb("block_f", [P, TILES], F32)
        flag_i = sb("flag_i", [1, 1], I32)
        pos_f = sb("pos_f", [EP, EJ], F32)
        pos_i = sb("pos_i", [EP, EJ], I32)
        carrier = sb("carrier", [1, 2], F32)
        ea_row = sb("ea_row", [EP, EDIM], F32)
        rec_row = sb("rec_row", [EP, 3], I32)
        pos_row = sb("pos_row", [EP, 1], I32)

        ps_t = pb("ps_t", [P, 2, 512])
        ps_a = pb("ps_a", [P, 2, 512])
        ps_b = pb("ps_b", [P, 2, 512])
        ps_m = pb("ps_m", [P, 512])

        names = ("w2_in wc_in bias_in dst_in src_in next_in rec_out tail_out ea_out next_set const pool_step dve_step "
                 "w1_hi w1_lo w1_dst_lo edge_hi bias_hi_ready bias_ready cnt_ready cnt_sum var_ready rstd_ready xn_ready op_ready "
                 "xt_tr xT_hi xT_lo a_ready b_ready a_out b_out meta_ready rank_step pos_ready scat_in scat_out row_ready carried").split()
        S = {n: sem(n) for n in names}
        x_in = [sem(f"x_in{k}") for k in range(BLOCKS // 2)]
        w1_in = [sem(f"w1_in{k}") for k in range(2)]
        a_stored = [sem(f"a_stored{k}") for k in range(2)]
        b_stored = [sem(f"b_stored{k}") for k in range(2)]
        block = ctx.enter_context(nc.Block())

        src_rows = src_table.rearrange("(i p) d -> i p d", p=NB)
        dst_rows = dst_table.rearrange("(i p) d -> i p d", p=NB)

        def first_tiles(t):
            return isinstance(t, int) and t < 2

        @block.sync
        def _(sp):
            x_rows = x.rearrange("(i p) d -> p i d", p=NB)
            for k in range(BLOCKS // 2):
                sp.dma_start(x_raw[0:NB, 2 * k:2 * k + 2, :], x_rows[:, 2 * k:2 * k + 2, :]).then_inc(x_in[k], 16)
            for k in range(0, 2 * KC, KC):
                sp.dma_start(w1_raw[:, k:k + KC, :], W1[k * P:(k + KC) * P, :].rearrange("(k p) n -> p k n", p=P)).then_inc(w1_in[k // KC], 16)
            sp.dma_start(dst_i[:], dst.rearrange("(p j) -> p j", p=EP)).then_inc(S["dst_in"], 16)
            sp.wait_ge(S["next_set"], 1)
            sp.dma_start(next_i[0:EP - 1, :], dst[1:1 + (EP - 1) * EJ].rearrange("(p j) -> p j", j=EJ)).then_inc(S["next_in"], 16)
            sp.dma_start(next_i[EP - 1:EP, 0:EJ - 1], dst[1 + (EP - 1) * EJ:EDGES].rearrange("(p j) -> p j", p=1)).then_inc(S["next_in"], 16)
            sp.dma_start(src_i[:], src.rearrange("(p j) -> p j", p=EP)).then_inc(S["src_in"], 16)
            for k in range(2):
                sp.dma_start(wc_raw[k * EDIM:(k + 1) * EDIM, :], W1[2 * HID:2 * HID + EDIM, :]).then_inc(S["wc_in"], 16)
            sp.wait_ge(S["xn_ready"], BLOCKS)
            sp.dma_start(w2_raw, W2.rearrange("(k p) n -> p k n", p=P)).then_inc(S["w2_in"], 16)

            def step(i, c):
                t, k, _ = item(i, c - 1)
                if within(t, BLOCKS):
                    sp.wait_ge(S["a_out"], t + 1)
                    sp.dma_start(src_rows[bass.ds(t, 1)].rearrange("a p d -> (a p) d"), tabs[:, k, 0, :]).then_inc(a_stored[k], 16)
                    sp.wait_ge(S["b_out"], t + 1)
                    sp.dma_start(dst_rows[bass.ds(t, 1)].rearrange("a p d -> (a p) d"), tabs[:, k, 1, :]).then_inc(b_stored[k], 16)

            steps(sp, step, 0, BLOCKS, 4, BLOCKS - 1)
            for k in range(2):
                sp.wait_ge(a_stored[k], 16 * (BLOCKS // 2))
                sp.wait_ge(b_stored[k], 16 * (BLOCKS // 2))

        @block.gpsimd
        def _(pool):
            nc.gpsimd.memset(next_i[:], NO_NODE).then_inc(S["next_set"], 1)
            c = Count(pool, S["pool_step"])
            c.inc(nc.gpsimd.memset(ident[:], 0.0))
            c.inc(nc.gpsimd.memset(ones[:], 1.0))
            c.inc(nc.gpsimd.memset(tri[:], 1.0))
            c.inc(nc.gpsimd.memset(row_is1[:], 0.0))
            c.inc(nc.gpsimd.memset(tail_i[:], 0))
            c.inc(nc.gpsimd.memset(tail_ea[:], 0.0))
            c.step(nc.gpsimd.iota(iota_t[:], [[1, TILES]], base=0, channel_multiplier=0, allow_small_or_imprecise_dtypes=True))
            c.inc(nc.gpsimd.iota(iota_n[:], [[1, NE]], base=0, channel_multiplier=0, allow_small_or_imprecise_dtypes=True))
            c.inc(nc.gpsimd.affine_select(out=ident[:], in_=ident[:], compare_op=ALU.not_equal, fill=1.0, base=0,
                                          pattern=[[-1, P]], channel_multiplier=1))
            c.inc(nc.gpsimd.affine_select(out=tri[:], in_=tri[:], compare_op=ALU.is_gt, fill=0.0, base=0,
                                          pattern=[[1, EP]], channel_multiplier=-1))
            c.inc(nc.gpsimd.affine_select(out=row_is1[:], in_=row_is1[:], compare_op=ALU.not_equal, fill=1.0, base=0,
                                          pattern=[[-1, 2]], channel_multiplier=1))
            c.inc(nc.gpsimd.memset(tail_i[:, 2:3], NO_NODE))
            c.inc(nc.gpsimd.memset(eps_col[:], EPS))
            c.step(nc.gpsimd.memset(half_col[:], 0.5))
            nc.gpsimd.memset(xn_op[:], 0.0).then_inc(S["const"], 1)
            for k in range(KC + KC // 2, 2 * KC):
                pool.wait_ge(S["w1_hi"], k + 1)
                nc.gpsimd.tensor_tensor(w1l[:, k, :], w1_raw[:, k, :], f32(w1h[:, k, :]), ALU.subtract).then_inc(S["w1_dst_lo"], 1)
            pool.dma_start(idx_scr[EDGES:EDGES + P, :], tail_i[:]).then_inc(S["tail_out"], 16)
            pool.dma_start(ea_scr[EDGES:EDGES + P, :], tail_ea[:]).then_inc(S["tail_out"], 16)
            pool.wait_ge(S["const"], 1)

            def grouped():
                pool.wait_ge(S["dst_in"], 16)
                pool.wait_ge(S["src_in"], 16)
                c.inc(nc.gpsimd.tensor_copy(rec_i[:, :, 0], src_i[:]))
                c.inc(nc.gpsimd.tensor_copy(rec_i[:, :, 1], dst_i[:]))
                c.inc(nc.gpsimd.tensor_copy(rec_i[:, :, 2], dst_i[:]))
                c.wait()
                pool.wait_ge(S["meta_ready"], 1)
                unsorted = pool.value_load(flag_i[0:1, 0:1], min_val=0, max_val=EDGES)
                nc.gpsimd.memset(carrier[:], 0.0).then_inc(S["carried"], 1)
                with pool.If(unsorted > 0):
                    pool.wait_ge(S["pos_ready"], 1)
                    ea_cols = edge_attr.rearrange("(p j) d -> j p d", p=EP)
                    with pool.Fori(0, EJ) as j:
                        pool.dma_start(ea_row[:], ea_cols[bass.ds(j, 1)].rearrange("a p d -> (a p) d")).then_inc(S["scat_in"], 16)
                        nc.gpsimd.tensor_copy(rec_row[:], rec_i[:, bass.ds(j, 1), :].rearrange("p a r -> p (a r)")).then_inc(S["row_ready"], 1)
                        nc.gpsimd.tensor_copy(pos_row[:], pos_i[:, bass.ds(j, 1)]).then_inc(S["row_ready"], 1)
                        pool.wait_ge(S["row_ready"], j * 2 + 2)
                        pool.wait_ge(S["scat_in"], j * 16 + 16)
                        pool.wait_ge(S["carried"], j + 1)
                        nc.gpsimd.tensor_tensor(carrier[0:1, 0:1], carrier[0:1, 1:2], carrier[0:1, 1:2], ALU.add).then_inc(S["carried"], 1)
                        pool.indirect_dma_start(out=ea_scr[:, :], out_offset=bass.IndirectOffsetOnAxis(ap=pos_row[:, 0:1], axis=0),
                                                in_=ea_row[:], in_offset=None).then_inc(S["scat_out"], 16)
                        pool.indirect_dma_start(out=idx_scr[:, :], out_offset=bass.IndirectOffsetOnAxis(ap=pos_row[:, 0:1], axis=0),
                                                in_=rec_row[:], in_offset=None).then_inc(S["scat_out"], 16)
                        pool.wait_ge(S["scat_out"], j * 32 + 32)
                with pool.Else():
                    pool.dma_start(ea_scr[0:EDGES, :].rearrange("(p j) d -> p (j d)", p=P - 3), edge_attr.rearrange("(p j) d -> p (j d)", p=P - 3)).then_inc(S["ea_out"], 16)
                    pool.dma_start(idx_scr[0:EDGES, :].rearrange("(p j) r -> p (j r)", p=EP), rec_i[:].rearrange("p j r -> p (j r)")).then_inc(S["rec_out"], 16)

            def step(i, c):
                t, k, _ = item(i, c)
                if within(t, BLOCKS) and not first_tiles(t):
                    pool.wait_ge(S["xn_ready"], t + 1)
                    need(pool, S["xt_tr"], t - 1)
                    nc.gpsimd.tensor_copy(xn_op[0:NB, k, :], xn_all[:, bass.ds(t, 1), :].rearrange("p a d -> p (a d)")).then_inc(S["op_ready"], 1)
                if isinstance(i, int) and c == 3:
                    grouped()

            steps(pool, step, 0, BLOCKS - 1, 4, BLOCKS - 1)
            pool.wait_ge(S["edge_hi"], 2)
            c.inc(nc.gpsimd.tensor_tensor(W2l[:], w2_raw, f32(W2h[:]), ALU.subtract))
            c.inc(nc.gpsimd.tensor_tensor(Wcl[:], wc_raw[:], f32(Wch[:]), ALU.subtract))
            nc.gpsimd.memset(agg[:], 0.0).then_inc(S["pool_step"], 1)
            c.n += 1
            unsorted = pool.value_load(flag_i[0:1, 0:1], min_val=0, max_val=EDGES)
            with pool.If(unsorted < 1):
                pool.wait_ge(S["ea_out"], 16)
                pool.wait_ge(S["rec_out"], 16)
            pool.wait_ge(S["tail_out"], 32)
            c.wait()

        @block.scalar
        def _(act):
            for n, b in enumerate(("b1", "b2", "b3", "b4")):
                act.dma_start(bias_raw[:, n, :], T[b].rearrange("(a n) -> a n", a=1).to_broadcast([2, HID])).then_inc(S["bias_in"], 16)
            nc.scalar.preload_act_table_set(EXP_LN_SET)
            act.wait_ge(S["const"], 1)
            act.wait_ge(S["var_ready"], 1)
            nc.scalar.activation(rs[:, 0, :], mv[:, :, 1], ACT.Ln, bias=eps_col[0:NB, :]).then_inc(S["rstd_ready"], 1)
            act.wait_ge(S["rstd_ready"], 1)
            nc.scalar.activation(rs[:, 1, :], rs[:, 0, :], ACT.Exp, scale=-0.5).then_inc(S["rstd_ready"], 1)

            def w1_hi(half):
                act.wait_ge(w1_in[half], 16)
                for k in range(half * KC, (half + 1) * KC):
                    nc.scalar.activation(w1h[:, k, :], w1_raw[:, k, :], ACT.Copy).then_inc(S["w1_hi"], 1)

            w1_hi(0)

            def step(i, c):
                t, k, _ = item(i, c)
                if within(t, BLOCKS):
                    act.wait_ge(S["xt_tr"], t + 1)
                    need(act, S["b_ready"], t - 1)
                    nc.scalar.activation(xTh[:, k, :], ps_t[:, k, 0:KC * NE], ACT.Copy).then_inc(S["xT_hi"], 1)
                if isinstance(i, int) and c == 0:
                    act.wait_ge(S["bias_in"], 64)
                    nc.scalar.activation(bias_hi[:, 0, :], bias_raw[:, 0, :], ACT.Copy).then_inc(S["bias_hi_ready"], 1)
                    w1_hi(1)
                if isinstance(i, int) and c == 1:
                    nc.scalar.activation(bias_hi[:, 1:, :], bias_raw[:, 1:, :], ACT.Copy).then_inc(S["bias_hi_ready"], 1)
                t, k, used = item(i, c - 1)
                if within(t, BLOCKS):
                    act.wait_ge(S["a_ready"], t + 1)
                    need(act, a_stored[k], used * 16)
                    nc.scalar.activation(tabs[:, k, 0, :], ps_a[0:NB, k, :], ACT.Copy).then_inc(S["a_out"], 1)
                if isinstance(i, int) and c == 3:
                    act.wait_ge(S["w2_in"], 16)
                    nc.scalar.activation(W2h[:], w2_raw, ACT.Copy).then_inc(S["edge_hi"], 1)
                    act.wait_ge(S["wc_in"], 32)
                    nc.scalar.activation(Wch[:], wc_raw[:], ACT.Copy).then_inc(S["edge_hi"], 1)

            steps(act, step, 0, BLOCKS, 4, BLOCKS - 1)

        @block.vector
        def _(dve):
            c = Count(dve, S["dve_step"])
            for t in range(BLOCKS):
                if t % 2 == 0:
                    dve.wait_ge(x_in[t // 2], 16)
                c.inc(nc.vector.bn_stats(out=stats[:, t, :], in_=x_raw[0:NB, t, :]))
            c.wait()
            for t in range(BLOCKS):
                ins = nc.vector.bn_aggr(out=mv[:, t, :], in_=stats[:, t, :])
            ins.then_inc(S["var_ready"], 1)
            dve.wait_ge(S["rstd_ready"], 2)
            c.step(nc.vector.tensor_tensor(rs[:, 2, :], rs[:, 1, :], rs[:, 1, :], ALU.mult))
            c.step(nc.vector.scalar_tensor_tensor(out=rs[:, 3, :], in0=mv[:, :, 1], scalar=EPS, in1=rs[:, 2, :], op0=ALU.add, op1=ALU.mult))
            c.step(nc.vector.tensor_scalar(rs[:, 3, :], rs[:, 3, :], -0.5, 1.5, ALU.mult, ALU.add))
            c.step(nc.vector.tensor_tensor(rs[:, 2, :], rs[:, 1, :], rs[:, 3, :], ALU.mult))

            def normalised(first, end):
                for t in range(first, end):
                    nc.vector.tensor_scalar(xn_all[:, t, :], x_raw[0:NB, t, :], mv[:, t, 0:1], rs[:, 2, t:t + 1], ALU.subtract, ALU.mult).then_inc(S["xn_ready"], 1)

            normalised(0, 2)
            dve.wait_ge(S["const"], 1)
            for t in range(2):
                nc.vector.tensor_scalar(xn_op[0:NB, t, :], x_raw[0:NB, t, :], mv[:, t, 0:1], rs[:, 2, t:t + 1], ALU.subtract, ALU.mult).then_inc(S["op_ready"], 1)
            c.inc(nc.vector.tensor_copy(plus_r[:], ones[0:2, :]))
            c.inc(nc.vector.tensor_scalar(minus_r[:], ones[0:2, :], -1.0, None, ALU.mult))
            for k in range(KC):
                dve.wait_ge(S["w1_hi"], k + 1)
                nc.vector.tensor_tensor(w1l[:, k, :], w1_raw[:, k, :], f32(w1h[:, k, :]), ALU.subtract).then_inc(S["w1_lo"], 1)

            def bias_rows(first, end, ready):
                raw, hi = bias_raw[:, first:end, :], f32(bias_hi[:, first:end, :])
                dve.wait_ge(S["bias_hi_ready"], ready)
                c.step(nc.vector.tensor_tensor(raw, raw, hi, ALU.subtract))
                c.step(nc.vector.tensor_scalar(raw, raw, row_is1[0:2, 1:2], None, ALU.mult))
                nc.vector.scalar_tensor_tensor(out=bias_r[:, first:end, :], in0=hi, scalar=row_is1[0:2, 0:1], in1=raw,
                                               op0=ALU.mult, op1=ALU.add).then_inc(S["bias_ready"], 1)

            def edges_below():
                c.inc(nc.vector.memset(below[:, 0, :], 0.0))
                c.inc(nc.vector.memset(below[:, BLOCKS, :], 1.0))
                c.inc(nc.vector.memset(tbase[:, 0:1], 0.0))
                dve.wait_ge(S["dst_in"], 16)
                for b in range(1, BLOCKS):
                    c.inc(nc.vector.tensor_scalar(below[:, b, :], dst_i[:], float(NB * b), None, ALU.is_lt))
                dve.wait_ge(S["next_in"], 32)
                c.step(nc.vector.tensor_tensor(below[:, BLOCKS + 1, :], next_i[:], dst_i[:], ALU.is_lt))
                nc.vector.tensor_reduce(out=row_cnt[:], in_=below[:], axis=AX_X, op=ALU.add).then_inc(S["cnt_ready"], 1)

            def first_edges():
                dve.wait_ge(S["cnt_sum"], 1)
                c.inc(nc.vector.tensor_copy(first[:], ps_m[:, 0:BLOCKS + 2]))
                c.step(nc.vector.tensor_copy(row_off[:], ps_m[0:EP, 64:64 + BLOCKS + 2]))
                nc.vector.tensor_copy(flag_i[:], first[0:1, BLOCKS + 1:BLOCKS + 2]).then_inc(S["meta_ready"], 1)
                c.step(nc.vector.scalar_tensor_tensor(out=cnt_i[:], in0=first[:, 1:BLOCKS + 1], scalar=float(P - 1), in1=first[:, 0:BLOCKS],
                                                      op0=ALU.add, op1=ALU.subtract))
                c.step(nc.vector.tensor_scalar(cnt_i[:], cnt_i[:], 7, None, ALU.arith_shift_right))
                c.step(nc.vector.tensor_copy(nt[:], cnt_i[:]))
                c.step(nc.vector.tensor_tensor_scan(out=tbase[:, 1:BLOCKS + 1], data0=ones[:, 0:BLOCKS], data1=nt[:], initial=0.0,
                                                    op0=ALU.mult, op1=ALU.add))
                c.step(nc.vector.scalar_tensor_tensor(out=off[:], in0=tbase[:], scalar=-float(P), in1=first[:, 0:BLOCKS + 1],
                                                      op0=ALU.mult, op1=ALU.add))
                c.inc(nc.vector.tensor_tensor(doff[:], off[:, 1:BLOCKS + 1], off[:, 0:BLOCKS], ALU.subtract))

            def tiles_reached():
                for b in range(BLOCKS):
                    c.inc(nc.vector.tensor_scalar(reached[:, b, :], iota_t[:], tbase[:, b + 1:b + 2], None, ALU.is_ge))
                c.wait()

            def tile_blocks():
                c.step(nc.vector.tensor_reduce(out=block_f[:], in_=reached[:, 0:BLOCKS - 1, :].rearrange("p b t -> p t b"), axis=AX_X, op=ALU.add))
                for b in range(BLOCKS):
                    c.inc(nc.vector.tensor_scalar(reached[:, b, :], reached[:, b, :], doff[:, b:b + 1], None, ALU.mult))
                c.wait()

            def tile_starts():
                c.step(nc.vector.tensor_reduce(out=start_f[:], in_=reached[:].rearrange("p b t -> p t b"), axis=AX_X, op=ALU.add))
                c.step(nc.vector.scalar_tensor_tensor(out=start_f[:], in0=iota_t[:], scalar=float(P), in1=start_f[:], op0=ALU.mult, op1=ALU.add))
                c.inc(nc.vector.tensor_scalar(start_i[:], start_f[:], float(EDGES), None, ALU.min))
                c.inc(nc.vector.tensor_copy(block_i[:], block_f[:]))
                c.inc(nc.vector.tensor_scalar(block_off[:], block_f[:], float(NB), None, ALU.mult))
                c.wait()

            def places():
                unsorted = dve.value_load(flag_i[0:1, 0:1], min_val=0, max_val=EDGES)
                with dve.If(unsorted > 0):
                    for b in range(BLOCKS + 1):
                        ins = nc.vector.tensor_tensor_scan(out=rank[:, b, :], data0=below[:, BLOCKS, :], data1=below[:, b, :],
                                                           initial=row_off[:, b:b + 1], op0=ALU.mult, op1=ALU.add)
                    ins.then_inc(S["rank_step"], 1)
                    dve.wait_ge(S["rank_step"], 1)
                    nc.vector.tensor_tensor(rank[:, 0:BLOCKS, :], rank[:, 1:BLOCKS + 1, :], rank[:, 0:BLOCKS, :], ALU.subtract).then_inc(S["rank_step"], 1)
                    nc.vector.tensor_tensor(below[:, 0:BLOCKS, :], below[:, 1:BLOCKS + 1, :], below[:, 0:BLOCKS, :], ALU.subtract).then_inc(S["rank_step"], 1)
                    dve.wait_ge(S["rank_step"], 3)
                    for b in range(BLOCKS):
                        ins = nc.vector.tensor_scalar(rank[:, b, :], rank[:, b, :], first[0:EP, b:b + 1], -1.0, ALU.add, ALU.add)
                    ins.then_inc(S["rank_step"], 1)
                    dve.wait_ge(S["rank_step"], 4)
                    nc.vector.tensor_tensor(rank[:, 0:BLOCKS, :], rank[:, 0:BLOCKS, :], below[:, 0:BLOCKS, :], ALU.mult).then_inc(S["rank_step"], 1)
                    dve.wait_ge(S["rank_step"], 5)
                    nc.vector.tensor_reduce(out=pos_f[:], in_=rank[:, 0:BLOCKS, :].rearrange("p b j -> p j b"), axis=AX_X, op=ALU.add).then_inc(S["rank_step"], 1)
                    dve.wait_ge(S["rank_step"], 6)
                    nc.vector.tensor_copy(pos_i[:], pos_f[:]).then_inc(S["pos_ready"], 1)

            def step(i, c):
                t, k, _ = item(i, c)
                if within(t, BLOCKS):
                    dve.wait_ge(S["xT_hi"], t + 1)
                    nc.vector.tensor_tensor(xTl[:, k, :], ps_t[:, k, 0:KC * NE], f32(xTh[:, k, :]), ALU.subtract).then_inc(S["xT_lo"], 1)
                if isinstance(i, int) and c == 0:
                    bias_rows(0, 1, 1)
                    for w in range(KC, KC + KC // 2):
                        dve.wait_ge(S["w1_hi"], w + 1)
                        nc.vector.tensor_tensor(w1l[:, w, :], w1_raw[:, w, :], f32(w1h[:, w, :]), ALU.subtract).then_inc(S["w1_dst_lo"], 1)
                if isinstance(i, int) and c == 1:
                    normalised(4, BLOCKS)
                    edges_below()
                if isinstance(i, int) and c == BLOCKS - 2:
                    tile_starts()
                if isinstance(i, int) and c == BLOCKS - 1:
                    bias_rows(1, 4, 2)
                t, k, used = item(i, c - 1)
                if within(t, BLOCKS):
                    dve.wait_ge(S["b_ready"], t + 1)
                    need(dve, b_stored[k], used * 16)
                    nc.vector.tensor_copy(tabs[:, k, 1, :], ps_b[0:NB, k, :]).then_inc(S["b_out"], 1)
                if isinstance(i, int) and c == 0:
                    normalised(2, 4)
                if isinstance(i, int) and c == 2:
                    first_edges()
                    tiles_reached()
                if isinstance(i, int) and c == 3:
                    tile_blocks()
                    places()

            steps(dve, step, 0, BLOCKS, 4, BLOCKS - 3)

        @block.tensor
        def _(pe):
            pe.wait_ge(S["const"], 1)

            def step(i, c):
                t, k, _ = item(i, c)
                if within(t, BLOCKS):
                    pe.wait_ge(S["op_ready"], t + 1)
                    need(pe, S["xT_lo"], t - 1)
                    for q in range(KC):
                        ins = nc.tensor.transpose(ps_t[:, k, q * NE:(q + 1) * NE], xn_op[:, k, q * P:(q + 1) * P], ident[0:NE, 0:NE])
                    ins.then_inc(S["xt_tr"], 1)
                t, k, _ = item(i, c - 1)
                if within(t, BLOCKS):
                    pe.wait_ge(S["xT_lo"], t + 1)
                    if isinstance(t, int) and t == 0:
                        pe.wait_ge(S["w1_lo"], KC)
                    for n, ps, ready, free in ((0, ps_a, "a_ready", "a_out"), (1, ps_b, "b_ready", "b_out")):
                        o = ps[0:NE, k, :]
                        need(pe, S[free], t - 1)
                        if n == 1:
                            if isinstance(t, int) and t == 0:
                                pe.wait_ge(S["w1_dst_lo"], KC)
                                pe.wait_ge(S["bias_ready"], 1)
                            nc.tensor.matmul(o, plus_r[:, 0:NE], bias_r[:, 0, :], start=True, stop=False)
                        for q in range(KC):
                            hi, lo = xTh[:, k, q * NE:(q + 1) * NE], xTl[:, k, q * NE:(q + 1) * NE]
                            nc.tensor.matmul(o, hi, w1h[:, n * KC + q, :], start=(q == 0 and n == 0), stop=False)
                            nc.tensor.matmul(o, hi, w1l[:, n * KC + q, :], start=False, stop=False)
                            ins = nc.tensor.matmul(o, lo, w1h[:, n * KC + q, :], start=False, stop=(q == KC - 1))
                        ins.then_inc(S[ready], 1)
                if isinstance(i, int) and c == 2:
                    pe.wait_ge(S["cnt_ready"], 1)
                    nc.tensor.matmul(ps_m[:, 0:BLOCKS + 2], ones[0:EP, :], row_cnt[:], start=True, stop=True)
                    nc.tensor.matmul(ps_m[0:EP, 64:64 + BLOCKS + 2], tri[:], row_cnt[:], start=True, stop=True).then_inc(S["cnt_sum"], 1)

            steps(pe, step, 0, BLOCKS, 4, BLOCKS - 1)
    nc.clear_and_free_semaphores(sems)
    nc.all_engine_barrier()


def edge_phase(nc, T):
    W2h, W2l, Wch, Wcl = T["W2h"], T["W2l"], T["Wch"], T["Wcl"]
    ident, minus_r, bias_r, half_col, iota_n = T["ident"], T["minus_r"], T["bias_r"], T["half_col"], T["iota_n"]
    start_i, block_i, block_off, agg = T["start_i"], T["block_i"], T["block_off"], T["agg"]
    w_raw, w3h, w3l = T["w_raw"], T["w3h"], T["w3l"]
    src_table, dst_table, ea_scr, idx_scr = T["src_table"], T["dst_table"], T["ea_scr"], T["idx_scr"]

    ctx, sems = ExitStack(), []
    with ctx:
        def sb(name, shape, dt=F32):
            return ctx.enter_context(nc.sbuf_tensor(name, shape, dt))

        def sem(name):
            sems.append(nc.alloc_semaphore(name))
            return sems[-1]

        idx_sl = sb("idx_sl", [P, 2, 2, 3], I32)
        ea_sl = sb("ea_sl", [P, 2, 2, EDIM])
        ea_hl = sb("ea_hl", [P, 2, 2, 2 * EDIM], F32R)
        eaT = sb("eaT", [2 * EDIM, 2, 2, P], F32R)
        gath = sb("gath", [P, 2, 2, HID])
        pre = sb("pre", [P, 2, 2, HID])
        act1 = sb("act1", [P, 2, 2, HID])
        act2 = sb("act2", [P, 2, 2, HID])
        hTh = sb("hTh", [P, 2, 2, HID], F32R)
        hTl = sb("hTl", [P, 2, 2, HID], F32R)
        msg_hi = sb("msg_hi", [P, 2, 2, HID], F32R)
        msg_lo = sb("msg_lo", [P, 2, 2, HID], F32R)
        dloc = sb("dloc", [P, TILES])
        carrier = sb("e_carrier", [1, 3, 2])
        onehot = sb("onehot", [P, 2, 2, NE], F32R)

        ps_1 = ctx.enter_context(nc.psum_tensor("ps_1", [P, 2, HID], F32))
        ps_h = ctx.enter_context(nc.psum_tensor("ps_h", [P, 2, HID], F32))
        ps_2 = ctx.enter_context(nc.psum_tensor("ps_2", [P, 2, 2, HID], F32))

        def slots(name):
            return [sem(f"{name}{k}") for k in range(2)]

        idx_in, ea_in, src_gath, both_gath = slots("idx_in"), slots("ea_in"), slots("src_gath"), slots("both_gath")
        names = ("ea_hi split dst_ready eaT_ps eaT_ready lin1_ps pre_ready exp1 inc1 sq1 ln1 quot1 h_ready hT_ps hT_hi hT_lo lin2_ps "
                 "exp2 inc2 sq2 ln2 quot2 msg_ready msg_hi_ready msg_lo_ready onehot_ready sum_ps summed src_free dst_free ea_free w3_in w3_hi w3_lo").split()
        S = {n: sem("e_" + n) for n in names}
        block = ctx.enter_context(nc.Block())

        FIRST, LAST, LO, HI, UNROLL = -4, PAIRS + 3, 7, PAIRS - 5, 6

        def pair(i, c):
            return item(i, c, unroll=UNROLL)

        act_parts = {PAIRS: (7, 0, 1, 2), PAIRS + 1: (3, 4, 5, 6)}
        dve_parts = {PAIRS + 1: (0, 1), PAIRS + 2: (2,), PAIRS + 3: (3, 4, 5, 6)}
        pool_parts = {PAIRS + 1: (7,)}
        hi_order = act_parts[PAIRS] + act_parts[PAIRS + 1]

        def of_step(parts, i, c):
            return parts.get(c, ()) if isinstance(i, int) else ()

        @block.sync
        def _(sp):
            def step(i, c):
                q, k, used = pair(i, c + 4)
                if within(q, PAIRS):
                    need(sp, both_gath[k], used * 32)
                    need(sp, S["split"], q - 1)
                    need(sp, S["dst_ready"], q - 1)
                    for j in range(2):
                        first = sp.value_load(start_i[0:1, bass.ds(q * 2 + j, 1)], min_val=0, max_val=EDGES)
                        sp.dma_start(idx_sl[:, k, j, :], idx_scr[bass.ds(first, P), :]).then_inc(idx_in[k], 16)
                        sp.dma_start(ea_sl[:, k, j, :], ea_scr[bass.ds(first, P), :]).then_inc(ea_in[k], 16)
                if isinstance(i, int) and c == PAIRS - 3:
                    sp.wait_ge(both_gath[(PAIRS - 1) % 2], ((PAIRS - 1) // 2 + 1) * 32)
                    sp.dma_start(w_raw[:], T["W3"].rearrange("(k p) n -> p k n", p=P)).then_inc(S["w3_in"], 16)

            steps(sp, step, FIRST, LAST, LO, HI, UNROLL)

        @block.gpsimd
        def _(pool):
            nc.gpsimd.memset(carrier[:, 0, :], 0.0).then_inc(S["src_free"], 1)
            nc.gpsimd.memset(carrier[:, 1, :], 0.0).then_inc(S["dst_free"], 1)
            nc.gpsimd.memset(carrier[:, 2, :], 0.0).then_inc(S["ea_free"], 1)

            def carry(n, row, passed):
                pool.wait_ge(passed, n + 1)
                nc.gpsimd.tensor_tensor(carrier[:, row, 0:1], carrier[:, row, 1:2], carrier[:, row, 1:2], ALU.add).then_inc(passed, 1)

            def step(i, c):
                b, kb, b_used = pair(i, c + 2)
                g, kg, used = pair(i, c + 3)

                def source_rows():
                    pool.wait_ge(idx_in[kg], used * 32 + 32)
                    need(pool, S["pre_ready"], g - 1)
                    carry(g, 0, S["src_free"])
                    for j in range(2):
                        pool.indirect_dma_start(out=gath[:, kg, j, :], out_offset=None, in_=src_table[:, :],
                                                in_offset=bass.IndirectOffsetOnAxis(ap=idx_sl[:, kg, j, 0:1], axis=0)).then_inc(src_gath[kg], 16)

                second_step = isinstance(i, int) and c == -2
                if second_step:
                    source_rows()
                if within(b, PAIRS):
                    pool.wait_ge(src_gath[kb], b_used * 32 + 32)
                    carry(b, 1, S["dst_free"])
                    for j in range(2):
                        pool.indirect_dma_start(out=gath[:, kb, j, :], out_offset=None, in_=dst_table[:, :],
                                                in_offset=bass.IndirectOffsetOnAxis(ap=idx_sl[:, kb, j, 1:2], axis=0),
                                                compute_op=ALU.add).then_inc(both_gath[kb], 16)
                if within(b, PAIRS):
                    pool.wait_ge(ea_in[kb], b_used * 32 + 32)
                    need(pool, S["eaT_ps"], b - 1)
                    carry(b, 2, S["ea_free"])
                    nc.gpsimd.tensor_copy(ea_hl[:, kb, :, 0:EDIM], ea_sl[:, kb]).then_inc(S["ea_hi"], 1)
                    pool.wait_ge(S["ea_hi"], b + 1)
                    nc.gpsimd.tensor_tensor(ea_hl[:, kb, :, EDIM:2 * EDIM], ea_sl[:, kb], f32(ea_hl[:, kb, :, 0:EDIM]), ALU.subtract).then_inc(S["split"], 1)
                if within(g, PAIRS) and not second_step:
                    source_rows()
                q, k, _ = pair(i, c - 3)
                if within(q, PAIRS):
                    pool.wait_ge(S["msg_hi_ready"], q + 1)
                    need(pool, S["sum_ps"], q - 1)
                    nc.gpsimd.tensor_tensor(msg_lo[:, k], act2[:, k], f32(msg_hi[:, k]), ALU.subtract).then_inc(S["msg_lo_ready"], 1)
                for w in of_step(pool_parts, i, c):
                    pool.wait_ge(S["w3_hi"], hi_order.index(w) + 1)
                    nc.gpsimd.tensor_tensor(w3l[:, w, :], w_raw[:, w, :], f32(w3h[:, w, :]), ALU.subtract).then_inc(S["w3_lo"], 1)

            steps(pool, step, FIRST, LAST, LO, HI, UNROLL)

        @block.scalar
        def _(act):
            nc.scalar.preload_act_table_set(EXP_LN_SET)

            def step(i, c):
                q, k, _ = pair(i, c)
                first = within(q, PAIRS)
                q2, k2, _ = pair(i, c - 2)
                second = within(q2, PAIRS)
                if second:
                    act.wait_ge(S["lin2_ps"], q2 + 1)
                    need(act, S["msg_lo_ready"], q2 - 1)
                    nc.scalar.activation(act2[:, k2], ps_2[:, k2], ACT.Exp, scale=-1.0).then_inc(S["exp2"], 1)
                r, kr, _ = pair(i, c - 1)
                if within(r, PAIRS):
                    act.wait_ge(S["hT_ps"], r + 1)
                    need(act, S["lin2_ps"], r - 1)
                    nc.scalar.activation(hTh[:, kr], ps_h[:], ACT.Copy).then_inc(S["hT_hi"], 1)
                if first:
                    act.wait_ge(S["inc1"], q + 1)
                    nc.scalar.activation(act1[:, k], act1[:, k], ACT.Square).then_inc(S["sq1"], 1)
                if second:
                    act.wait_ge(S["inc2"], q2 + 1)
                    nc.scalar.activation(act2[:, k2], act2[:, k2], ACT.Square).then_inc(S["sq2"], 1)
                if first:
                    act.wait_ge(S["sq1"], q + 1)
                    nc.scalar.activation(act1[:, k], act1[:, k], ACT.Ln, bias=half_col[:], scale=0.5).then_inc(S["ln1"], 1)
                if second:
                    act.wait_ge(S["sq2"], q2 + 1)
                    nc.scalar.activation(act2[:, k2], act2[:, k2], ACT.Ln, bias=half_col[:], scale=0.5).then_inc(S["ln2"], 1)
                if first:
                    act.wait_ge(S["ln1"], q + 1)
                    nc.scalar.activation(act1[:, k], act1[:, k], ACT.Exp, scale=-1.0).then_inc(S["quot1"], 1)
                n, kn, _ = pair(i, c + 1)
                if within(n, PAIRS):
                    act.wait_ge(S["pre_ready"], n + 1)
                    need(act, S["hT_ps"], n - 1)
                    nc.scalar.activation(act1[:, kn], pre[:, kn], ACT.Exp).then_inc(S["exp1"], 1)
                if second:
                    act.wait_ge(S["ln2"], q2 + 1)
                    nc.scalar.activation(act2[:, k2], act2[:, k2], ACT.Exp, scale=-1.0).then_inc(S["quot2"], 1)
                for w in of_step(act_parts, i, c):
                    act.wait_ge(S["w3_in"], 16)
                    nc.scalar.activation(w3h[:, w, :], w_raw[:, w, :], ACT.Copy).then_inc(S["w3_hi"], 1)

            steps(act, step, FIRST, LAST, LO, HI, UNROLL)

        @block.vector
        def _(dve):
            def lo_parts(i, c):
                for w in of_step(dve_parts, i, c):
                    dve.wait_ge(S["w3_hi"], hi_order.index(w) + 1)
                    nc.vector.tensor_tensor(w3l[:, w, :], w_raw[:, w, :], f32(w3h[:, w, :]), ALU.subtract).then_inc(S["w3_lo"], 1)

            def step(i, c):
                q, k, _ = pair(i, c)
                first = within(q, PAIRS)
                q2, k2, _ = pair(i, c - 2)
                n, kn, used = pair(i, c + 1)
                if within(n, PAIRS):
                    dve.wait_ge(S["eaT_ps"], n + 1)
                    need(dve, S["lin1_ps"], n - 1)
                    nc.vector.tensor_copy(eaT[:, kn], ps_1[:, :, 0:P]).then_inc(S["eaT_ready"], 1)
                g, kg, _ = pair(i, c - 3)
                if c > PAIRS + 1:
                    lo_parts(i, c)
                if within(g, PAIRS):
                    dve.wait_ge(S["quot2"], g + 1)
                    nc.vector.scalar_tensor_tensor(out=act2[:, kg], in0=act2[:, kg], scalar=1.0, in1=ps_2[:, kg],
                                                   op0=ALU.subtract, op1=ALU.mult).then_inc(S["msg_ready"], 1)
                if c == PAIRS + 1:
                    lo_parts(i, c)
                if within(q2, PAIRS):
                    dve.wait_ge(S["exp2"], q2 + 1)
                    nc.vector.tensor_scalar(act2[:, k2], act2[:, k2], EXP_MAX, 1.0, ALU.min, ALU.add).then_inc(S["inc2"], 1)
                if within(g, PAIRS):
                    need(dve, S["sum_ps"], g - 1)
                    dve.wait_ge(S["msg_ready"], g + 1)
                    nc.vector.tensor_copy(msg_hi[:, kg], act2[:, kg]).then_inc(S["msg_hi_ready"], 1)
                if within(n, PAIRS):
                    dve.wait_ge(S["lin1_ps"], n + 1)
                    dve.wait_ge(both_gath[kn], used * 32 + 32)
                    need(dve, S["h_ready"], n - 1)
                    nc.vector.tensor_tensor(pre[:, kn], ps_1[:], gath[:, kn], ALU.add).then_inc(S["pre_ready"], 1)
                a, ka, _ = pair(i, c - 4)
                if within(a, PAIRS):
                    rows = []
                    for j in range(2):
                        b = dve.value_load(block_i[0:1, bass.ds(a * 2 + j, 1)], min_val=0, max_val=BLOCKS - 1)
                        rows.append(agg[:, bass.ds(b, 1), :].rearrange("p a d -> p (a d)"))
                r, kr, _ = pair(i, c - 1)
                if within(r, PAIRS):
                    dve.wait_ge(S["hT_hi"], r + 1)
                    nc.vector.tensor_tensor(hTl[:, kr], ps_h[:], f32(hTh[:, kr]), ALU.subtract).then_inc(S["hT_lo"], 1)
                for j in range(2):
                    if within(a, PAIRS):
                        dve.wait_ge(S["sum_ps"], a + 1)
                        need(dve, S["summed"], a * 2 + j)
                        nc.vector.tensor_tensor(rows[j], rows[j], ps_1[0:NB, j, :], ALU.add).then_inc(S["summed"], 1)
                    if within(g, PAIRS):
                        dve.wait_ge(S["dst_ready"], g + 1)
                        nc.vector.tensor_scalar(onehot[:, kg, j, :], iota_n[:], dloc[:, bass.ds(g * 2 + j, 1)], None, ALU.is_equal).then_inc(S["onehot_ready"], 1)
                if first:
                    dve.wait_ge(S["quot1"], q + 1)
                    nc.vector.scalar_tensor_tensor(out=act1[:, k], in0=act1[:, k], scalar=1.0, in1=pre[:, k],
                                                   op0=ALU.subtract, op1=ALU.mult).then_inc(S["h_ready"], 1)
                l, kl, lused = pair(i, c + 2)
                if within(l, PAIRS):
                    dve.wait_ge(idx_in[kl], lused * 32 + 32)
                    nc.vector.tensor_tensor(dloc[:, bass.ds(l * 2, 2)], idx_sl[:, kl, :, 2], block_off[:, bass.ds(l * 2, 2)], ALU.subtract).then_inc(S["dst_ready"], 1)
                if within(n, PAIRS):
                    dve.wait_ge(S["exp1"], n + 1)
                    nc.vector.tensor_scalar(act1[:, kn], act1[:, kn], EXP_MAX, 1.0, ALU.min, ALU.add).then_inc(S["inc1"], 1)

            steps(dve, step, FIRST, LAST, LO, HI, UNROLL)

        @block.tensor
        def _(pe):
            def step(i, c):
                n, kn, _ = pair(i, c + 1)
                r, kr, _ = pair(i, c - 1)
                m, km, _ = pair(i, c - 4)

                def lin2(j, d, part, weights, last=False):
                    return nc.tensor.matmul(ps_2[:, kr, j, :], part[:, kr, j, d * P:(d + 1) * P], weights[:, d, :], start=False, stop=last)

                if within(n, PAIRS):
                    pe.wait_ge(S["split"], n + 1)
                    need(pe, S["pre_ready"], n)
                    need(pe, S["summed"], (n - 5) * 2)
                    for j in range(2):
                        ins = nc.tensor.transpose(ps_1[:, j, 0:P], f32(ea_hl[:, kn, j, :]), ident[:])
                    ins.then_inc(S["eaT_ps"], 1)
                if within(r, PAIRS):
                    pe.wait_ge(S["h_ready"], r + 1)
                    need(pe, S["hT_lo"], r)
                    for j in range(2):
                        for d in range(KC):
                            ins = nc.tensor.transpose(ps_h[:, j, d * P:(d + 1) * P], act1[:, kr, j, d * P:(d + 1) * P], ident[:])
                    ins.then_inc(S["hT_ps"], 1)
                if within(n, PAIRS):
                    pe.wait_ge(S["eaT_ready"], n + 1)
                    for j in range(2):
                        nc.tensor.matmul(ps_1[:, j, :], eaT[:, kn, j, :], Wch[:], start=True, stop=False)
                        ins = nc.tensor.matmul(ps_1[:, j, :], eaT[:, kn, j, :], Wcl[:], start=False, stop=True)
                    ins.then_inc(S["lin1_ps"], 1)
                if within(r, PAIRS):
                    need(pe, S["msg_ready"], r - 1)
                    for j in range(2):
                        nc.tensor.matmul(ps_2[:, kr, j, :], minus_r[:], bias_r[:, 1, :], start=True, stop=False)
                    pe.wait_ge(S["hT_hi"], r + 1)
                    for d in range(KC):
                        lin2(0, d, hTh, W2h)
                        lin2(0, d, hTh, W2l)
                if within(m, PAIRS):
                    need(pe, S["summed"], m * 2)
                    pe.wait_ge(S["onehot_ready"], m * 2 + 2)
                    pe.wait_ge(S["msg_lo_ready"], m + 1)
                    pe.wait_ge(S["pre_ready"], min(m + 6, PAIRS) if isinstance(m, int) else m + 6)
                    for j in range(2):
                        nc.tensor.matmul(ps_1[0:NE, j, :], onehot[:, km, j, :], msg_hi[:, km, j, :], start=True, stop=False)
                        ins = nc.tensor.matmul(ps_1[0:NE, j, :], onehot[:, km, j, :], msg_lo[:, km, j, :], start=False, stop=True)
                    ins.then_inc(S["sum_ps"], 1)
                if within(r, PAIRS):
                    for d in range(KC):
                        lin2(1, d, hTh, W2h)
                        lin2(1, d, hTh, W2l)
                    pe.wait_ge(S["hT_lo"], r + 1)
                    for j in range(2):
                        for d in range(KC):
                            ins = lin2(j, d, hTl, W2h, d == KC - 1)
                    ins.then_inc(S["lin2_ps"], 1)

            steps(pe, step, FIRST, LAST, LO, HI, UNROLL)
            pe.wait_ge(S["w3_lo"], 2 * KC)
    nc.clear_and_free_semaphores(sems)
    nc.all_engine_barrier()


def node_phase(nc, T):
    ident, minus_r, plus_r, bias_r = T["ident"], T["minus_r"], T["plus_r"], T["bias_r"]
    half_col, eps_col, agg, xn_all = T["half_col"], T["eps_col"], T["agg"], T["xn_all"]
    w_raw, w3h, w3l = T["w_raw"], T["w3h"], T["w3l"]
    x1_all, lg, xl_scr = T["x1_all"], T["lg"], T["xl_scr"]
    E = EXPERTS
    KK = 2 * KC

    ctx = ExitStack()
    with ctx:
        def sb(name, shape, dt=F32):
            return ctx.enter_context(nc.sbuf_tensor(name, shape, dt))

        def pb(name, shape):
            return ctx.enter_context(nc.psum_tensor(name, shape, F32))

        def sem(name):
            return ctx.enter_context(nc.semaphore("n_" + name))

        w4h = sb("w4h", [P, KC, HID], F32R)
        w4l = sb("w4l", [P, KC, HID], F32R)
        gamma_b = sb("gamma_b", [NB, HID])
        beta_b = sb("beta_b", [NB, HID])
        x_sl = sb("x_sl", [NB, 2, HID])
        cat_op = sb("cat_op", [NE, 2, 2 * HID])
        catTh = sb("catTh", [P, 2, KK * NE], F32R)
        catTl = sb("catTl", [P, 2, KK * NE], F32R)
        u = sb("u", [NE, 2, HID])
        uTh = sb("uTh", [P, 2, KC * NE], F32R)
        uTl = sb("uTl", [P, 2, KC * NE], F32R)
        y = sb("y", [NB, 2, HID])
        gate = sb("gate", [E, HID])
        gateT = sb("gateT", [P, KC, 2, E], F32R)
        xlTh = sb("xlTh", [P, KC * NE], F32R)
        xlTl = sb("xlTl", [P, KC * NE], F32R)
        xl_op = sb("xl_op", [NE, 2, HID])
        stats = sb("n_stats", [NB, 2, 6])
        mv = sb("n_mv", [NB, 2, 2])
        rs = sb("n_rs", [NB, 2, 5])

        ps_c = pb("ps_c", [P, 2, 512])
        ps_u = pb("ps_u", [P, 2, 512])
        ps_v = pb("ps_v", [P, 512])
        ps_o = pb("ps_o", [P, 2, 512])
        ps_x = pb("ps_x", [P, 512])

        names = ("cat_zeroed u_zeroed first_op w4_in w4_hi w4_lo gb_in zeroed op_ready cat_ps cat_hi cat_lo lin_ps bounded exp sq ln quot "
                 "u_ready uT_ps uT_hi uT_lo out_ps y_ready xb_ready x1_ready y_stats y_scaled x1_stats post_y post_x var_y rstd_y var_x rstd_x xl_ready x1_done xlT_ps xlT_hi xlT_lo gate_in gateT_ps gate_hi gate_lo lg_ps lg_out").split()
        S = {n: sem(n) for n in names}
        x_in = [sem(f"x_in{k}") for k in range(2)]
        xl_stored = [sem(f"xl_stored{k}") for k in range(2)]
        block = ctx.enter_context(nc.Block())
        def first_tile(t):
            return isinstance(t, int) and t == 0

        FIRST, LAST, LO, HI = -1, BLOCKS + 4, 5, BLOCKS - 2

        @block.sync
        def _(sp):
            sp.dma_start(gate[:], T["gate_w"]).then_inc(S["gate_in"], 16)
            sp.dma_start(w_raw[:, 0:KC, :], T["W4"].rearrange("(k p) n -> p k n", p=P)).then_inc(S["w4_in"], 16)
            sp.dma_start(gamma_b[:], T["gamma"].rearrange("(a n) -> a n", a=1).to_broadcast([NB, HID])).then_inc(S["gb_in"], 16)
            sp.dma_start(beta_b[:], T["beta"].rearrange("(a n) -> a n", a=1).to_broadcast([NB, HID])).then_inc(S["gb_in"], 16)
            x_rows = T["x"].rearrange("(i p) d -> i p d", p=NB)
            xl_rows = xl_scr.rearrange("(i p) d -> i p d", p=NB)

            def step(i, c):
                z, kz, _ = item(i, c - 3)
                if within(z, BLOCKS):
                    sp.wait_ge(S["xl_ready"], z + 1)
                    sp.dma_start(xl_rows[bass.ds(z, 1)].rearrange("a p d -> (a p) d"), xl_op[0:NB, kz, :]).then_inc(xl_stored[kz], 16)
                t, k, _ = item(i, c + 1)
                if within(t, BLOCKS):
                    need(sp, S["x1_done"], t - 1)
                    sp.dma_start(x_sl[:, k, :], x_rows[bass.ds(t, 1)].rearrange("a p d -> (a p) d")).then_inc(x_in[k], 16)

            steps(sp, step, FIRST, LAST, LO, HI)
            for k in range(2):
                sp.wait_ge(xl_stored[k], 16 * (BLOCKS // 2))

        @block.gpsimd
        def _(pool):
            nc.gpsimd.memset(cat_op[:, 1], 0.0).then_inc(S["zeroed"], 1)
            nc.gpsimd.memset(xl_op[:], 0.0).then_inc(S["zeroed"], 1)
            pool.wait_ge(S["zeroed"], 2)

            def step(i, c):
                t, k, _ = item(i, c + 1)
                if within(t, BLOCKS) and not first_tile(t):
                    need(pool, S["cat_ps"], t - 1)
                    nc.gpsimd.tensor_copy(cat_op[0:NB, k, 0:HID], xn_all[:, bass.ds(t, 1), :].rearrange("p a d -> p (a d)"))
                    nc.gpsimd.tensor_copy(cat_op[0:NB, k, HID:2 * HID], agg[:, bass.ds(t, 1), :].rearrange("p a d -> p (a d)")).then_inc(S["op_ready"], 1)
                p, kp, used = item(i, c - 1)
                if within(p, BLOCKS):
                    pool.wait_ge(S["gb_in"], 32)
                    pool.wait_ge(x_in[kp], used * 16 + 16)
                    nc.gpsimd.tensor_tensor(x_sl[:, kp, :], x_sl[:, kp, :], beta_b[:], ALU.add).then_inc(S["xb_ready"], 1)

            steps(pool, step, FIRST, LAST, LO, HI)

        @block.scalar
        def _(act):
            nc.scalar.preload_act_table_set(EXP_LN_SET)
            act.wait_ge(S["cat_zeroed"], 1)
            nc.scalar.activation(cat_op[0:NB, 0, 0:HID], xn_all[:, 0, :], ACT.Copy).then_inc(S["first_op"], 1)
            act.wait_ge(S["gateT_ps"], 1)
            nc.scalar.activation(gateT[:, :, 0, :], ps_x[:, 0:KC * E].rearrange("p (q e) -> p q e", e=E), ACT.Copy).then_inc(S["gate_hi"], 1)

            def rstd(n, t, var, ready):
                act.wait_ge(S[var], t + 1)
                nc.scalar.activation(rs[:, n, 0:1], mv[:, n, 1:2], ACT.Ln, bias=eps_col[0:NB, :]).then_inc(S[ready], 1)
                act.wait_ge(S[ready], t * 2 + 1)
                nc.scalar.activation(rs[:, n, 1:2], rs[:, n, 0:1], ACT.Exp, scale=-0.5).then_inc(S[ready], 1)

            def step(i, c):
                p, kp, _ = item(i, c - 2)
                if within(p, BLOCKS):
                    rstd(0, p, "var_y", "rstd_y")
                v, kv, _ = item(i, c - 1)
                if within(v, BLOCKS):
                    act.wait_ge(S["uT_ps"], v + 1)
                    need(act, S["out_ps"], v - 1)
                    nc.scalar.activation(uTh[:, kv, :], ps_v[:, 0:KC * NE], ACT.Copy).then_inc(S["uT_hi"], 1)
                t, k, _ = item(i, c)
                n, kn, _ = item(i, c + 1)
                if within(n, BLOCKS):
                    act.wait_ge(S["cat_ps"], n + 1)
                    need(act, S["lin_ps"], n - 1)
                    nc.scalar.activation(catTh[:, kn, :].rearrange("p (a n) -> p a n", a=2), ps_c[:, :, 0:KC * NE], ACT.Copy).then_inc(S["cat_hi"], 1)
                if first_tile(n):
                    act.wait_ge(S["w4_in"], 16)
                    for q in range(KC):
                        nc.scalar.activation(w4h[:, q, :], w_raw[:, q, :], ACT.Copy).then_inc(S["w4_hi"], 1)
                if within(t, BLOCKS):
                    act.wait_ge(S["bounded"], t + 1)
                    nc.scalar.activation(u[0:NB, k, :], u[0:NB, k, :], ACT.Exp).then_inc(S["exp"], 1)
                if within(t, BLOCKS):
                    act.wait_ge(S["exp"], t + 1)
                    nc.scalar.activation(u[0:NB, k, :], u[0:NB, k, :], ACT.Square, bias=1.0).then_inc(S["sq"], 1)
                z, _, _ = item(i, c - 4)
                if within(z, BLOCKS):
                    act.wait_ge(S["xlT_ps"], z + 1)
                    need(act, S["lg_ps"], z)
                    nc.scalar.activation(xlTh[:], ps_x[:, 0:KC * NE], ACT.Copy).then_inc(S["xlT_hi"], 1)
                if within(t, BLOCKS):
                    act.wait_ge(S["sq"], t + 1)
                    nc.scalar.activation(u[0:NB, k, :], u[0:NB, k, :], ACT.Ln, bias=half_col[0:NB, :], scale=0.5).then_inc(S["ln"], 1)
                    act.wait_ge(S["ln"], t + 1)
                    nc.scalar.activation(u[0:NB, k, :], u[0:NB, k, :], ACT.Exp, scale=-1.0).then_inc(S["quot"], 1)
                if within(p, BLOCKS):
                    act.wait_ge(S["x1_ready"], p + 1)
                    nc.scalar.activation(x1_all[:, bass.ds(p, 1), :].rearrange("p a d -> p (a d)"), y[:, kp, :], ACT.Copy).then_inc(S["x1_done"], 1)
                    rstd(1, p, "var_x", "rstd_x")

            steps(act, step, FIRST, LAST, LO, HI)

        @block.vector
        def _(dve):
            nc.vector.memset(cat_op[:, 0], 0.0).then_inc(S["cat_zeroed"], 1)
            dve.wait_ge(S["cat_zeroed"], 1)
            nc.vector.tensor_copy(cat_op[0:NB, 0, HID:2 * HID], agg[:, 0, :]).then_inc(S["first_op"], 1)
            dve.wait_ge(S["gate_hi"], 1)
            nc.vector.tensor_tensor(gateT[:, :, 1, :], ps_x[:, 0:KC * E].rearrange("p (q e) -> p q e", e=E), f32(gateT[:, :, 0, :]), ALU.subtract).then_inc(S["gate_lo"], 1)
            nc.vector.memset(u[:], 0.0).then_inc(S["u_zeroed"], 1)
            dve.wait_ge(S["gb_in"], 32)
            dve.wait_ge(S["zeroed"], 2)
            dve.wait_ge(S["u_zeroed"], 1)

            NEWTON = 4

            def step(i, c):
                def link(name, m, ins):
                    ins.then_inc(S[name], 1)
                    dve.wait_ge(S[name], m)

                def newton(n, t, ready, name):
                    dve.wait_ge(S[ready], t * 2 + 2)
                    link(name, t * NEWTON + 1, nc.vector.tensor_tensor(rs[:, n, 2:3], rs[:, n, 1:2], rs[:, n, 1:2], ALU.mult))
                    link(name, t * NEWTON + 2, nc.vector.scalar_tensor_tensor(out=rs[:, n, 3:4], in0=mv[:, n, 1:2], scalar=EPS, in1=rs[:, n, 2:3],
                                                                              op0=ALU.add, op1=ALU.mult))
                    link(name, t * NEWTON + 3, nc.vector.tensor_scalar(rs[:, n, 4:5], rs[:, n, 3:4], -0.5, 1.5, ALU.mult, ALU.add))
                    link(name, t * NEWTON + 4, nc.vector.tensor_tensor(rs[:, n, 2:3], rs[:, n, 1:2], rs[:, n, 4:5], ALU.mult))

                tail = isinstance(i, int) and c > BLOCKS + 1

                def logits():
                    l, _, _ = item(i, c - 5)
                    if within(l, BLOCKS):
                        dve.wait_ge(S["lg_ps"], l + 1)
                        nc.vector.tensor_copy(lg[:, bass.ds(l, 1), :].rearrange("p a e -> p (a e)"), ps_x[0:NB, 0:2 * E]).then_inc(S["lg_out"], 1)

                def xl_lo():
                    w, _, _ = item(i, c - 4)
                    if within(w, BLOCKS):
                        dve.wait_ge(S["xlT_hi"], w + 1)
                        nc.vector.tensor_tensor(xlTl[:], ps_x[:, 0:KC * NE], f32(xlTh[:]), ALU.subtract).then_inc(S["xlT_lo"], 1)

                p, kp, _ = item(i, c - 2)
                yk = y[:, kp, :]
                if within(p, BLOCKS):
                    dve.wait_ge(S["out_ps"], p + 1)
                    nc.vector.tensor_tensor(yk, xn_all[:, bass.ds(p, 1), :].rearrange("p a d -> p (a d)"), ps_o[0:NB, kp, :], ALU.subtract).then_inc(S["y_ready"], 1)
                    dve.wait_ge(S["y_ready"], p + 1)
                    nc.vector.bn_stats(out=stats[:, 0, :], in_=yk).then_inc(S["y_stats"], 1)
                    dve.wait_ge(S["y_stats"], p + 1)
                    nc.vector.tensor_copy(rs[:, 0, 4:5], eps_col[0:NB, :])
                    nc.vector.bn_aggr(out=mv[:, 0, :], in_=stats[:, 0, :]).then_inc(S["var_y"], 1)
                if tail:
                    logits()
                    xl_lo()
                z, kz, zused = item(i, c - 3)
                if within(z, BLOCKS):
                    newton(1, z, "rstd_x", "post_x")
                    need(dve, S["xlT_ps"], z - 1)
                    need(dve, xl_stored[kz], zused * 16)
                    nc.vector.tensor_scalar(xl_op[0:NB, kz, :], y[:, kz, :], mv[:, 1, 0:1], rs[:, 1, 2:3], ALU.subtract, ALU.mult).then_inc(S["xl_ready"], 1)
                if within(p, BLOCKS):
                    dve.wait_ge(S["var_y"], p + 1)
                    nc.vector.scalar_tensor_tensor(out=yk, in0=yk, scalar=mv[:, 0, 0:1], in1=gamma_b[:], op0=ALU.subtract, op1=ALU.mult).then_inc(S["y_scaled"], 1)
                v, kv, _ = item(i, c - 1)
                if within(v, BLOCKS):
                    dve.wait_ge(S["uT_hi"], v + 1)
                    nc.vector.tensor_tensor(uTl[:, kv, :], ps_v[:, 0:KC * NE], f32(uTh[:, kv, :]), ALU.subtract).then_inc(S["uT_lo"], 1)
                if not tail:
                    logits()
                n, kn, _ = item(i, c + 1)
                if within(n, BLOCKS):
                    dve.wait_ge(S["cat_hi"], n + 1)
                    nc.vector.tensor_tensor(catTl[:, kn, :].rearrange("p (a n) -> p a n", a=2), ps_c[:, :, 0:KC * NE],
                                            f32(catTh[:, kn, :]).rearrange("p (a n) -> p a n", a=2), ALU.subtract).then_inc(S["cat_lo"], 1)
                t, k, _ = item(i, c)
                if first_tile(n):
                    for q in range(KC):
                        dve.wait_ge(S["w4_hi"], q + 1)
                        nc.vector.tensor_tensor(w4l[:, q, :], w_raw[:, q, :], f32(w4h[:, q, :]), ALU.subtract).then_inc(S["w4_lo"], 1)
                if within(t, BLOCKS):
                    dve.wait_ge(S["lin_ps"], t + 1)
                    need(dve, S["uT_ps"], t - 1)
                    nc.vector.tensor_scalar(u[0:NB, k, :], ps_u[0:NB, k, :], X_MAX, None, ALU.min).then_inc(S["bounded"], 1)
                if not within(t, BLOCKS) and not tail:
                    xl_lo()
                if within(p, BLOCKS):
                    newton(0, p, "rstd_y", "post_y")
                    dve.wait_ge(S["y_scaled"], p + 1)
                    dve.wait_ge(S["xb_ready"], p + 1)
                    nc.vector.scalar_tensor_tensor(out=yk, in0=yk, scalar=rs[:, 0, 2:3], in1=x_sl[:, kp, :], op0=ALU.mult, op1=ALU.add).then_inc(S["x1_ready"], 1)
                    dve.wait_ge(S["x1_ready"], p + 1)
                    nc.vector.bn_stats(out=stats[:, 1, :], in_=yk).then_inc(S["x1_stats"], 1)
                if within(p, BLOCKS):
                    dve.wait_ge(S["x1_stats"], p + 1)
                    nc.vector.tensor_copy(rs[:, 1, 4:5], eps_col[0:NB, :])
                    nc.vector.bn_aggr(out=mv[:, 1, :], in_=stats[:, 1, :]).then_inc(S["var_x"], 1)
                if within(t, BLOCKS):
                    xl_lo()
                if within(t, BLOCKS):
                    dve.wait_ge(S["quot"], t + 1)
                    nc.vector.scalar_tensor_tensor(out=u[0:NB, k, :], in0=u[0:NB, k, :], scalar=1.0, in1=ps_u[0:NB, k, :],
                                                   op0=ALU.subtract, op1=ALU.mult).then_inc(S["u_ready"], 1)

            steps(dve, step, FIRST, LAST, LO, HI)

        @block.tensor
        def _(pe):
            pe.wait_ge(S["gate_in"], 16)
            for q in range(KC):
                ins = nc.tensor.transpose(ps_x[:, q * E:(q + 1) * E], gate[:, q * P:(q + 1) * P], ident[0:E, 0:E])
            ins.then_inc(S["gateT_ps"], 1)
            pe.wait_ge(S["gate_lo"], 1)

            def step(i, c):
                t, k, _ = item(i, c)
                o = ps_u[0:NE, k, :]

                def lin(first, end):
                    for q in range(first, end):
                        hi, lo = catTh[:, k, q * NE:(q + 1) * NE], catTl[:, k, q * NE:(q + 1) * NE]
                        nc.tensor.matmul(o, hi, w3h[:, q, :], start=False, stop=False)
                        nc.tensor.matmul(o, hi, w3l[:, q, :], start=False, stop=False)
                        ins = nc.tensor.matmul(o, lo, w3h[:, q, :], start=False, stop=(q == KK - 1))
                    return ins

                if within(t, BLOCKS):
                    pe.wait_ge(S["cat_lo"], t + 1)
                    need(pe, S["u_ready"], t - 1)
                    nc.tensor.matmul(o, plus_r[:, 0:NE], bias_r[:, 2, :], start=True, stop=False)
                    lin(0, KC)
                v, kv, _ = item(i, c - 1)
                if within(v, BLOCKS):
                    pe.wait_ge(S["u_ready"], v + 1)
                    need(pe, S["uT_lo"], v)
                    for q in range(KC):
                        ins = nc.tensor.transpose(ps_v[:, q * NE:(q + 1) * NE], u[:, kv, q * P:(q + 1) * P], ident[0:NE, 0:NE])
                    ins.then_inc(S["uT_ps"], 1)
                n, kn, _ = item(i, c + 1)
                if within(n, BLOCKS):
                    if first_tile(n):
                        pe.wait_ge(S["first_op"], 2)
                    else:
                        pe.wait_ge(S["op_ready"], n)
                    need(pe, S["cat_lo"], n)
                    for q in range(KK):
                        ins = nc.tensor.transpose(ps_c[:, q // KC, (q % KC) * NE:(q % KC + 1) * NE], cat_op[:, kn, q * P:(q + 1) * P], ident[0:NE, 0:NE])
                    ins.then_inc(S["cat_ps"], 1)
                l, _, _ = item(i, c - 5)
                if within(l, BLOCKS):
                    pe.wait_ge(S["xlT_lo"], l + 1)
                    for q in range(KC):
                        hi, lo = xlTh[:, q * NE:(q + 1) * NE], xlTl[:, q * NE:(q + 1) * NE]
                        nc.tensor.matmul(ps_x[0:NE, 0:2 * E], hi, gateT[:, q].rearrange("p n e -> p (n e)"), start=(q == 0), stop=False)
                        ins = nc.tensor.matmul(ps_x[0:NE, 0:E], lo, gateT[:, q, 0, :], start=False, stop=(q == KC - 1))
                    ins.then_inc(S["lg_ps"], 1)
                if within(t, BLOCKS):
                    lin(KC, KK).then_inc(S["lin_ps"], 1)
                z, kz, _ = item(i, c - 4)
                if within(z, BLOCKS):
                    pe.wait_ge(S["xl_ready"], z + 1)
                    need(pe, S["lg_out"], z)
                    for q in range(KC):
                        ins = nc.tensor.transpose(ps_x[:, q * NE:(q + 1) * NE], xl_op[:, kz, q * P:(q + 1) * P], ident[0:NE, 0:NE])
                    ins.then_inc(S["xlT_ps"], 1)
                if within(v, BLOCKS):
                    pe.wait_ge(S["uT_lo"], v + 1)
                    pe.wait_ge(S["w4_lo"], KC)
                    need(pe, S["y_ready"], v - 1)
                    out2 = ps_o[0:NE, kv, :]
                    nc.tensor.matmul(out2, minus_r[:, 0:NE], bias_r[:, 3, :], start=True, stop=False)
                    for q in range(KC):
                        hi, lo = uTh[:, kv, q * NE:(q + 1) * NE], uTl[:, kv, q * NE:(q + 1) * NE]
                        nc.tensor.matmul(out2, hi, w4h[:, q, :], start=False, stop=False)
                        nc.tensor.matmul(out2, hi, w4l[:, q, :], start=False, stop=False)
                        ins = nc.tensor.matmul(out2, lo, w4h[:, q, :], start=False, stop=(q == KC - 1))
                    ins.then_inc(S["out_ps"], 1)

            steps(pe, step, FIRST, LAST, LO, HI)


def ffn_phase(nc, T):
    ident, ones, tri, lg = T["ident"], T["ones"], T["tri"], T["lg"]
    x1_all, xl_scr, route_scr, out = T["x1_all"], T["xl_scr"], T["route_scr"], T["out"]
    E, FC, RT = EXPERTS, FFN // P, ROUTE_TILES
    WS = 4
    GB = 512 // NB

    ctx = ExitStack()
    with ctx:
        def sb(name, shape, dt=F32):
            return ctx.enter_context(nc.sbuf_tensor(name, shape, dt))

        def pb(name, shape):
            return ctx.enter_context(nc.psum_tensor(name, shape, F32))

        def sem(name):
            return ctx.enter_context(nc.semaphore("f_" + name))

        w1Th = sb("w1Th", [P, E, KC, FFN], F32R)
        w1Tl = sb("w1Tl", [P, E, KC, FFN], F32R)
        order = sb("order", [NB, E])
        best = sb("best", [NB, 4, BLOCKS])
        hot1 = sb("hot1", [NB, BLOCKS, E])
        hot2 = sb("hot2", [NB, BLOCKS, E])
        rank_a = sb("rank_a", [NB, BLOCKS, E])
        rank_b = sb("rank_b", [NB, BLOCKS, E])
        logit = rank_b
        wt = sb("wt", [NB, 4, BLOCKS])
        gw = sb("gw", [NB, BLOCKS, E])
        mask = sb("mask", [NB, E, BLOCKS])
        seen = sb("seen", [NB, E, BLOCKS])
        msum = sb("msum", [NB, E])
        mscan = sb("mscan", [NB, E])
        cnt = sb("cnt", [P, E])
        cnt_i = sb("f_cnt_i", [P, E], I32)
        ntile = sb("ntile", [P, E])
        tend = sb("tend", [P, E])
        inv = sb("inv", [P, E])
        base = sb("base", [NB, E])
        pos_f = sb("f_pos_f", [NB, TOP_K, BLOCKS])
        pos_i = sb("f_pos_i", [NB, TOP_K, BLOCKS], I32)
        token1 = sb("token1", [NB, BLOCKS], I32)
        empty = sb("empty", [RT, P], I32)
        iota_r = sb("iota_r", [P, RT])
        reach = sb("reach", [P, RT, E])
        expert_f = sb("expert_f", [P, RT])
        expert_i = sb("expert_i", [P, RT], I32)
        route_i = sb("route_i", [RT, P], I32)
        route_f = sb("route_f", [RT, P])
        valid = sb("valid", [P, RT])
        row_i = sb("row_i", [P, RT], I32)
        gwT = sb("gwT", [E, NODES])
        w_raw = sb("f_w_raw", [P, WS, FC * HID])
        w1_raw = w_raw[:].rearrange("p s (c d) -> p s c d", c=FC)
        w2_raw = w_raw[:].rearrange("p s (q f) -> p s q f", q=KC)
        carrier = sb("f_carrier", [1, 2])
        row_sl = sb("row_sl", [P, 2, 1], I32)
        xg = sb("xg", [P, 2, HID])
        xgTh = sb("xgTh", [P, 2, HID], F32R)
        xgTl = sb("xgTl", [P, 2, HID], F32R)
        hs = sb("hs", [P, 2, FFN])
        hsum = sb("hsum", [P, FC, E])
        hm = sb("hm", [P, FC, E])
        spread_hm = sb("spread_hm", [P, 2, FC, P])
        junk_y = xg[:].rearrange("p s d -> p (s d)").rearrange("p (q f) -> p q f", q=KC)
        y_col = sb("y_col", [P, 2, KC])
        yT = sb("yT", [P, KC, E])
        ROWS = 2 * 32 + E
        gw3 = w1Th[0:ROWS].rearrange("p e q f -> p (e q f)")[:, 0:NODES + NE - NB]
        y3 = xgTh[0:ROWS, 0, :]

        ps_t = pb("f_ps_t", [P, 2, 512])
        ps_n = pb("f_ps_n", [P, 2, 512])
        ps_s = pb("f_ps_s", [P, 2, 512])
        ps_b = pb("f_ps_b", [P, 512])
        ps_m = pb("f_ps_m", [P, 512])

        names = ("const empty_out step diff exp_out gw_ready mask_ready cnt_ps pos_ready scattered route_in route_ready route_ps rows_ready tiles_ready "
                 "gw_ps gw_out w1T_ps w1T_hi w1T_lo zeroed row_ready xgT_ps xgT_hi xgT_lo h_ps h_act sum_ps summed hm_ready carried "
                 "spread mean_ps y_step y_done yT_ps out_zeroed gw3_hi gw3_lo y3_hi y3_lo res_ps res_done res_out").split()
        S = {n: sem(n) for n in names}
        w1_in, w2_in = ([sem(f"{n}{k}") for k in range(WS)] for n in ("w1_in", "w2_in"))
        gathered = [sem(f"gathered{k}") for k in range(2)]
        block = ctx.enter_context(nc.Block())
        FIRST, LAST, LO, HI, UNROLL = -3, RT + 2, 4, RT - 4, 4

        def tile(i, c):
            return item(i, c, unroll=UNROLL)


        def bank(k, f):
            return (ps_t, ps_s)[k % 2][:, f, :]

        def flat(ap):
            return ap.rearrange("p a b -> p (a b)")

        @block.sync
        def _(sp):
            w1_rows = T["w1"].rearrange("e (c p) d -> e p c d", p=P)
            w2_rows = T["w2"].rearrange("e (q p) f -> e p q f", p=P)

            def load_w1(i, c):
                e, k, _ = item(i, c, WS)
                need(sp, S["w1T_ps"], (e - (WS - 1)) * FC)
                sp.dma_start(w1_raw[:, k], w1_rows[bass.ds(e, 1)].rearrange("a p c d -> (a p) c d")).then_inc(w1_in[k], 16)

            steps(sp, load_w1, 0, E - 1, WS, E - 1, WS)

            def load_w2(i, c):
                e, k, _ = item(i, c, WS)
                if isinstance(e, int) and e < WS:
                    sp.wait_ge(S["w1T_ps"], E * FC)
                    sp.wait_ge(S["h_ps"], RT * (e + 1) // (WS + 1))
                need(sp, S["y_step"], (e - (WS - 1)) * KC)
                sp.dma_start(w2_raw[:, k], w2_rows[bass.ds(e, 1)].rearrange("a p q f -> (a p) q f")).then_inc(w2_in[k], 16)

            steps(sp, load_w2, 0, E - 1, WS, E - 1, WS)
            for t in range(BLOCKS):
                sp.wait_ge(S["res_done"], t + 1)
                sp.dma_start(out[t * NB:(t + 1) * NB, :], x1_all[:, t, :]).then_inc(S["res_out"], 16)
            sp.wait_ge(S["res_out"], 16 * BLOCKS)

        @block.gpsimd
        def _(pool):
            nc.gpsimd.iota(order[:], [[-1, E]], base=E, channel_multiplier=0, allow_small_or_imprecise_dtypes=True).then_inc(S["const"], 1)
            nc.gpsimd.iota(token1[:], [[NB, BLOCKS]], base=1, channel_multiplier=1).then_inc(S["const"], 1)
            nc.gpsimd.iota(iota_r[:], [[1, RT]], base=0, channel_multiplier=0, allow_small_or_imprecise_dtypes=True).then_inc(S["const"], 1)
            nc.gpsimd.memset(empty[:], 0).then_inc(S["const"], 1)
            nc.gpsimd.memset(hsum[:], 0.0).then_inc(S["const"], 1)
            pool.wait_ge(S["const"], 5)
            pool.dma_start(route_scr.rearrange("(t p) a -> t (p a)", p=P), empty[:]).then_inc(S["empty_out"], 16)
            pool.wait_ge(S["empty_out"], 16)
            pool.wait_ge(S["pos_ready"], 1)
            for s in range(TOP_K):
                for b in range(BLOCKS):
                    pool.indirect_dma_start(out=route_scr[:, :], out_offset=bass.IndirectOffsetOnAxis(ap=pos_i[:, s, b:b + 1], axis=0),
                                            in_=token1[:, b:b + 1], in_offset=None).then_inc(S["scattered"], 16)
            pool.wait_ge(S["scattered"], 16 * TOP_K * BLOCKS)
            pool.dma_start(route_i[:], route_scr.rearrange("(t p) a -> t (p a)", p=P)).then_inc(S["route_in"], 16)

            def step(i, c):
                g, k, _ = tile(i, c + 2)
                if within(g, RT):
                    pool.wait_ge(S["row_ready"], g + 1)
                    need(pool, S["xgT_ps"], g - 1)
                    pool.wait_ge(S["carried"], g + 1)
                    nc.gpsimd.tensor_tensor(carrier[:, 0:1], carrier[:, 1:2], carrier[:, 1:2], ALU.add).then_inc(S["carried"], 1)
                    pool.indirect_dma_start(out=xg[:, k, :], out_offset=None, in_=xl_scr[:, :],
                                            in_offset=bass.IndirectOffsetOnAxis(ap=row_sl[:, k, 0:1], axis=0)).then_inc(gathered[k], 16)

            nc.gpsimd.memset(carrier[:], 0.0).then_inc(S["carried"], 1)
            steps(pool, step, FIRST, LAST, LO, HI, UNROLL)
            pool.wait_ge(S["h_ps"], RT)
            for part in (gw3, y3):
                nc.gpsimd.tensor_scalar(part, ones[0:ROWS, 0:1].to_broadcast(list(part.shape)), 0.0, None, ALU.mult).then_inc(S["out_zeroed"], 1)
            pool.wait_ge(S["gw3_hi"], 2)
            nc.gpsimd.tensor_tensor(gw3[64:64 + E, 0:NODES], gwT[:], f32(gw3[0:E, 0:NODES]), ALU.subtract).then_inc(S["gw3_lo"], 1)

        @block.scalar
        def _(act):
            def hi_w1(i, c):
                e, e_slot, _ = item(i, c, WS)
                for f in range(FC):
                    act.wait_ge(S["w1T_ps"], e * FC + (f + 1))
                    nc.scalar.activation(w1Th[:, bass.ds(e, 1), :, f * P:(f + 1) * P].rearrange("p a q f -> p (a q) f"),
                                         bank(e_slot, f).rearrange("p (q f) -> p q f", q=KC), ACT.Copy).then_inc(S["w1T_hi"], 1)

            def softmax_exp():
                act.wait_ge(S["diff"], 1)
                nc.scalar.activation(wt[:, 1, :], wt[:, 0, :], ACT.Exp).then_inc(S["exp_out"], 1)

            steps(act, hi_w1, 0, E - 1, 4, E - 1, 4)
            softmax_exp()
            nc.scalar.preload_act_table_set("silu_and_others")

            def step(i, c):
                n, kn, _ = tile(i, c + 1)
                if within(n, RT):
                    act.wait_ge(S["xgT_ps"], n + 1)
                    need(act, S["h_ps"], n - 1)
                    nc.scalar.activation(xgTh[:, kn, :], ps_t[:, kn, :], ACT.Copy).then_inc(S["xgT_hi"], 1)
                t, k, _ = tile(i, c)
                if within(t, RT):
                    act.wait_ge(S["h_ps"], t + 1)
                    need(act, S["sum_ps"], t - 1)
                    nc.scalar.activation(hs[:, k, :], ps_n[:, k, 0:FFN], ACT.Silu).then_inc(S["h_act"], 1)

            steps(act, step, FIRST, LAST, LO, HI, UNROLL)

            def transposed_weights():
                act.wait_ge(S["gw_ps"], 1)
                for n, ps in enumerate((ps_t[0:E, 0, :], ps_t[0:E, 1, :], ps_b[0:E, :])):
                    cols = slice(n * GB * NB, min((n + 1) * GB, BLOCKS) * NB)
                    nc.scalar.activation(gwT[:, cols], ps[:, 0:cols.stop - cols.start], ACT.Copy).then_inc(S["gw_out"], 1)

            def diagonal(i, c):
                e, k, _ = item(i, c, WS)
                need(act, S["mean_ps"], e - 1)
                for f in range(FC):
                    ins = nc.scalar.activation(spread_hm[:, k % 2, f, :], ident[:], ACT.Copy, scale=hm[:, f, bass.ds(e, 1)])
                ins.then_inc(S["spread"], 1)
                if isinstance(e, int) and e == 1:
                    transposed_weights()

            act.wait_ge(S["hm_ready"], 1)
            steps(act, diagonal, 0, E - 1, WS, E - 1, WS)
            act.wait_ge(S["out_zeroed"], 2)
            act.wait_ge(S["gw_out"], 3)
            for r in (0, 32):
                nc.scalar.activation(gw3[r:r + E, 0:NODES], gwT[:], ACT.Copy).then_inc(S["gw3_hi"], 1)
            act.wait_ge(S["yT_ps"], 1)
            nc.scalar.activation(y3[0:E, :], ps_m[0:E, :], ACT.Copy).then_inc(S["y3_hi"], 1)
            act.wait_ge(S["y3_hi"], 1)
            nc.scalar.activation(y3[64:64 + E, :], f32(y3[0:E, :]), ACT.Copy).then_inc(S["y3_hi"], 1)

        @block.vector
        def _(dve):
            c = Count(dve, S["step"])

            def spread(ap):
                return ap.unsqueeze(2).to_broadcast([NB, BLOCKS, E])

            orders = order[:].unsqueeze(1).to_broadcast([NB, BLOCKS, E])
            dve.wait_ge(S["const"], 5)

            def largest(src, n, hot):
                c.step(nc.vector.tensor_reduce(out=best[:, n, :], in_=src, axis=AX_X, op=ALU.max))
                c.step(nc.vector.tensor_tensor(rank_a[:], src, spread(best[:, n, :]), ALU.is_equal))
                c.step(nc.vector.tensor_tensor(rank_a[:], rank_a[:], orders, ALU.mult))
                c.step(nc.vector.tensor_reduce(out=best[:, 2 + n, :], in_=rank_a[:], axis=AX_X, op=ALU.max))
                c.step(nc.vector.tensor_tensor(hot, orders, spread(best[:, 2 + n, :]), ALU.is_equal))

            c.step(nc.vector.tensor_tensor(logit[:], lg[:, :, 0:E], lg[:, :, E:2 * E], ALU.add))
            largest(logit[:], 0, hot1[:])
            c.step(nc.vector.scalar_tensor_tensor(out=flat(rank_b[:]), in0=flat(hot1[:]), scalar=-1e30, in1=flat(logit[:]), op0=ALU.mult, op1=ALU.add))
            largest(rank_b[:], 1, hot2[:])
            nc.vector.tensor_tensor(wt[:, 0, :], best[:, 1, :], best[:, 0, :], ALU.subtract).then_inc(S["diff"], 1)
            c.step(nc.vector.tensor_tensor(mask[:], hot1[:].rearrange("p b e -> p e b"), hot2[:].rearrange("p b e -> p e b"), ALU.add))
            nc.vector.tensor_reduce(out=msum[:], in_=mask[:], axis=AX_X, op=ALU.add).then_inc(S["mask_ready"], 1)
            dve.wait_ge(S["mask_ready"], 1)
            c.inc(nc.vector.tensor_tensor_scan(out=flat(seen[:]), data0=ones[0:NB, 0:1].to_broadcast([NB, E * BLOCKS]), data1=flat(mask[:]), initial=0.0,
                                               op0=ALU.mult, op1=ALU.add))
            c.inc(nc.vector.tensor_tensor_scan(out=mscan[:], data0=ones[0:NB, 0:E], data1=msum[:], initial=0.0, op0=ALU.mult, op1=ALU.add))
            dve.wait_ge(S["cnt_ps"], 1)
            c.step(nc.vector.tensor_copy(cnt[:], ps_m[:, 0:E]))
            c.step(nc.vector.tensor_scalar(cnt_i[:], cnt[:], float(P - 1), None, ALU.add))
            c.step(nc.vector.tensor_scalar(cnt_i[:], cnt_i[:], 7, None, ALU.arith_shift_right))
            c.step(nc.vector.tensor_copy(ntile[:], cnt_i[:]))
            c.step(nc.vector.tensor_tensor_scan(out=tend[:], data0=ones[:, 0:E], data1=ntile[:], initial=0.0, op0=ALU.mult, op1=ALU.add))
            c.step(nc.vector.tensor_tensor(base[:], tend[0:NB, :], ntile[0:NB, :], ALU.subtract))
            c.step(nc.vector.scalar_tensor_tensor(out=base[:], in0=base[:], scalar=float(P), in1=ps_m[0:NB, 64:64 + E], op0=ALU.mult, op1=ALU.add))
            c.step(nc.vector.tensor_tensor(base[:], base[:], mscan[:], ALU.subtract))
            c.step(nc.vector.scalar_tensor_tensor(out=base[:], in0=msum[:], scalar=-1.0, in1=base[:], op0=ALU.add, op1=ALU.add))
            c.step(nc.vector.tensor_tensor(seen[:], seen[:], base[:].unsqueeze(2).to_broadcast([NB, E, BLOCKS]), ALU.add))
            for s, (hot, rank) in enumerate(((hot1, rank_a), (hot2, rank_b))):
                c.step(nc.vector.tensor_tensor(rank[:], hot[:], seen[:].rearrange("p e b -> p b e"), ALU.mult))
                c.step(nc.vector.tensor_reduce(out=pos_f[:, s, :], in_=rank[:], axis=AX_X, op=ALU.add))
            nc.vector.tensor_copy(flat(pos_i[:]), flat(pos_f[:])).then_inc(S["pos_ready"], 1)
            c.step(nc.vector.tensor_tensor(reach[:], iota_r[:].unsqueeze(2).to_broadcast([P, RT, E]), tend[:].unsqueeze(1).to_broadcast([P, RT, E]), ALU.is_ge))
            c.step(nc.vector.tensor_reduce(out=expert_f[:], in_=reach[:, :, 0:E - 1], axis=AX_X, op=ALU.add))
            nc.vector.tensor_copy(expert_i[:], expert_f[:]).then_inc(S["tiles_ready"], 1)
            c.step(nc.vector.tensor_scalar(inv[:], cnt[:], 1.0, None, ALU.max))
            c.step(nc.vector.reciprocal(inv[:], inv[:]))

            def lo_w1(i, c):
                e, e_slot, _ = item(i, c, WS)
                for f in range(FC):
                    dve.wait_ge(S["w1T_hi"], e * FC + (f + 1))
                    part = (slice(None), bass.ds(e, 1), slice(None), slice(f * P, (f + 1) * P))
                    nc.vector.tensor_tensor(w1Tl[part].rearrange("p a q f -> p (a q) f"), bank(e_slot, f).rearrange("p (q f) -> p q f", q=KC),
                                            f32(w1Th[part]).rearrange("p a q f -> p (a q) f"), ALU.subtract).then_inc(S["w1T_lo"], 1)

            steps(dve, lo_w1, 0, E - 1, 4, E - 1, 4)
            dve.wait_ge(S["route_in"], 16)
            nc.vector.tensor_copy(route_f[:], route_i[:]).then_inc(S["route_ready"], 1)
            dve.wait_ge(S["route_ps"], 1)
            c.inc(nc.vector.tensor_scalar(valid[:], ps_m[:, 0:RT], 0.0, None, ALU.is_gt))
            nc.vector.tensor_scalar(row_i[:], ps_m[:, 0:RT], -1.0, 0.0, ALU.add, ALU.max).then_inc(S["rows_ready"], 1)
            dve.wait_ge(S["rows_ready"], 1)
            c.wait()

            def weights():
                dve.wait_ge(S["exp_out"], 1)
                c.step(nc.vector.tensor_scalar(wt[:, 2, :], wt[:, 1, :], 1.0, None, ALU.add))
                c.step(nc.vector.reciprocal(wt[:, 3, :], wt[:, 2, :]))
                c.step(nc.vector.tensor_tensor(wt[:, 2, :], wt[:, 3, :], wt[:, 1, :], ALU.mult))
                c.inc(nc.vector.tensor_tensor(hot1[:], hot1[:], spread(wt[:, 3, :]), ALU.mult))
                c.step(nc.vector.tensor_tensor(hot2[:], hot2[:], spread(wt[:, 2, :]), ALU.mult))
                nc.vector.tensor_tensor(gw[:], hot1[:], hot2[:], ALU.add).then_inc(S["gw_ready"], 1)

            def step(i, c):
                g, k, used = tile(i, c + 3)
                if within(g, RT):
                    need(dve, gathered[k], used * 16)
                    nc.vector.tensor_copy(row_sl[:, k, :], row_i[:, bass.ds(g, 1)]).then_inc(S["row_ready"], 1)
                if isinstance(i, int) and c == FIRST + 1:
                    weights()
                m, km, _ = tile(i, c - 3)
                if within(m, RT):
                    e = dve.value_load(expert_i[0:1, bass.ds(m, 1)], min_val=0, max_val=E - 1)
                    cols = hsum[:, :, bass.ds(e, 1)].rearrange("p f a -> p (f a)")
                    dve.wait_ge(S["sum_ps"], m + 1)
                    need(dve, S["summed"], m)
                    nc.vector.tensor_tensor(cols, cols, ps_s[:, km, 0:FC], ALU.add).then_inc(S["summed"], 1)
                n, kn, _ = tile(i, c + 1)
                if within(n, RT):
                    dve.wait_ge(S["xgT_hi"], n + 1)
                    nc.vector.tensor_tensor(xgTl[:, kn, :], ps_t[:, kn, :], f32(xgTh[:, kn, :]), ALU.subtract).then_inc(S["xgT_lo"], 1)

            steps(dve, step, FIRST, LAST, LO, HI, UNROLL)
            dve.wait_ge(S["summed"], RT)
            nc.vector.tensor_tensor(hm[:], hsum[:], inv[:].unsqueeze(1).to_broadcast([P, FC, E]), ALU.mult).then_inc(S["hm_ready"], 1)

            def output(i, c):
                e, k, used = item(i, c, WS)
                if within(e, E):
                    dve.wait_ge(w2_in[k], used * 16 + 16)
                    dve.wait_ge(S["mean_ps"], e + 1)
                    need(dve, S["y_step"], e * KC)
                    need(dve, S["y_done"], e - 1)
                    for q in range(KC):
                        nc.vector.tensor_tensor_reduce(out=junk_y[:, q, :], in0=w2_raw[:, k, q, :], in1=ps_n[:, k % 2, 0:FFN], scale=1.0, scalar=0.0,
                                                       op0=ALU.mult, op1=ALU.add, accum_out=y_col[:, k % 2, q:q + 1]).then_inc(S["y_step"], 1)
                d, kd, _ = item(i, c - 1, WS)
                if within(d, E):
                    dve.wait_ge(S["y_step"], d * KC + KC)
                    nc.vector.tensor_copy(yT[:, :, bass.ds(d, 1)].rearrange("p q a -> p (q a)"), y_col[:, kd % 2, :]).then_inc(S["y_done"], 1)

            steps(dve, output, 0, E, WS, E - 1, WS)
            dve.wait_ge(S["y3_hi"], 1)
            nc.vector.tensor_tensor(y3[32:32 + E, :], ps_m[0:E, :], f32(y3[0:E, :]), ALU.subtract).then_inc(S["y3_lo"], 1)
            for t in range(BLOCKS):
                dve.wait_ge(S["res_ps"], t + 1)
                ps = (ps_t[0:NB, t % 2, :], ps_s[0:NB, t % 2, :])[t // 2 % 2]
                nc.vector.tensor_tensor(x1_all[:, t, :], x1_all[:, t, :], ps, ALU.add).then_inc(S["res_done"], 1)

        @block.tensor
        def _(pe):
            pe.wait_ge(S["mask_ready"], 1)
            nc.tensor.matmul(ps_m[:, 0:E], ones[0:NB, :], msum[:], start=True, stop=True)
            nc.tensor.matmul(ps_m[0:NB, 64:64 + E], tri[:], msum[:], start=True, stop=True).then_inc(S["cnt_ps"], 1)

            def transposes(i, c):
                e, k, used = item(i, c, WS)
                pe.wait_ge(w1_in[k], used * 16 + 16)
                for f in range(FC):
                    need(pe, S["w1T_lo"], (e - 2) * FC + (f + 1))
                    for q in range(KC):
                        ins = nc.tensor.transpose(bank(k, f)[:, q * P:(q + 1) * P], w1_raw[:, k, f, q * P:(q + 1) * P], ident[:])
                    ins.then_inc(S["w1T_ps"], 1)

            steps(pe, transposes, 0, E - 1, WS, E - 1, WS)
            pe.wait_ge(S["route_ready"], 1)
            nc.tensor.transpose(ps_m[:, 0:RT], route_f[:], ident[0:RT, 0:RT]).then_inc(S["route_ps"], 1)
            pe.wait_ge(S["w1T_lo"], E * FC)
            pe.wait_ge(S["rows_ready"], 1)
            pe.wait_ge(S["tiles_ready"], 1)

            def step(i, c):
                t, k, _ = tile(i, c)
                if within(t, RT):
                    e = pe.value_load(expert_i[0:1, bass.ds(t, 1)], min_val=0, max_val=E - 1)
                n, kn, used = tile(i, c + 1)
                if within(n, RT):
                    pe.wait_ge(gathered[kn], used * 16 + 16)
                    need(pe, S["xgT_lo"], n - 1)
                    for q in range(KC):
                        ins = nc.tensor.transpose(ps_t[:, kn, q * P:(q + 1) * P], xg[:, kn, q * P:(q + 1) * P], ident[:])
                    ins.then_inc(S["xgT_ps"], 1)
                m, km, _ = tile(i, c - 2)
                if within(m, RT):
                    pe.wait_ge(S["h_act"], m + 1)
                    need(pe, S["summed"], m - 1)
                    for f in range(FC):
                        ins = nc.tensor.matmul(ps_s[:, km, f:f + 1], hs[:, km, f * P:(f + 1) * P], valid[:, bass.ds(m, 1)], start=True, stop=True)
                    ins.then_inc(S["sum_ps"], 1)
                if within(t, RT):
                    wh = w1Th[:, bass.ds(e, 1), :, :].rearrange("p a q f -> p (a q) f")
                    wl = w1Tl[:, bass.ds(e, 1), :, :].rearrange("p a q f -> p (a q) f")
                    pe.wait_ge(S["xgT_lo"], t + 1)
                    need(pe, S["h_act"], t - 1)
                    for q in range(KC):
                        hi, lo = xgTh[:, k, q * P:(q + 1) * P], xgTl[:, k, q * P:(q + 1) * P]
                        nc.tensor.matmul(ps_n[:, k, 0:FFN], hi, wh[:, q, :], start=(q == 0), stop=False)
                        nc.tensor.matmul(ps_n[:, k, 0:FFN], hi, wl[:, q, :], start=False, stop=False)
                        ins = nc.tensor.matmul(ps_n[:, k, 0:FFN], lo, wh[:, q, :], start=False, stop=(q == KC - 1))
                    ins.then_inc(S["h_ps"], 1)

            steps(pe, step, FIRST, LAST, LO, HI, UNROLL)

            pe.wait_ge(S["gw_ready"], 1)
            for b in range(BLOCKS):
                ps = (ps_t[0:E, 0, :], ps_t[0:E, 1, :], ps_b[0:E, :])[b // GB]
                ins = nc.tensor.transpose(ps[:, b % GB * NB:(b % GB + 1) * NB], gw[:, b, :], ident[0:NB, 0:NB])
            ins.then_inc(S["gw_ps"], 1)

            def means(i, c):
                e, k, _ = item(i, c, WS)
                k = k % 2
                pe.wait_ge(S["spread"], e + 1)
                need(pe, S["y_step"], (e - 1) * KC)
                for f in range(FC):
                    ins = nc.tensor.matmul(ps_n[:, k, f * P:(f + 1) * P], ones[:], spread_hm[:, k, f, :], start=True, stop=True)
                ins.then_inc(S["mean_ps"], 1)

            steps(pe, means, 0, E - 1, WS, E - 1, WS)
            pe.wait_ge(S["y_done"], E)
            for q in range(KC):
                ins = nc.tensor.transpose(ps_m[0:E, q * P:(q + 1) * P], yT[:, q, :], ident[:])
            ins.then_inc(S["yT_ps"], 1)
            pe.wait_ge(S["gw3_lo"], 1)
            pe.wait_ge(S["y3_hi"], 2)
            pe.wait_ge(S["y3_lo"], 1)
            for t in range(BLOCKS):
                need(pe, S["res_done"], t - 3)
                ps = (ps_t[0:NE, t % 2, :], ps_s[0:NE, t % 2, :])[t // 2 % 2]
                nc.tensor.matmul(ps, gw3[:, t * NB:t * NB + NE], y3, start=True, stop=True).then_inc(S["res_ps"], 1)


_INS = ["x", "src", "dst", "edge_attr_64", "L0_gnn_W1", "L0_gnn_b1", "L0_gnn_W2", "L0_gnn_b2", "L0_gnn_W3", "L0_gnn_b3",
        "L0_gnn_W4", "L0_gnn_b4", "L0_gnn_gamma", "L0_gnn_beta", "L0_ffn_gate_weight", "L0_ffn_w1", "L0_ffn_w2"]
_OUTS = [((NODES, HID), "float32")]


def kernel(**inputs):
    import numpy as _np
    import concourse.bacc as _bacc
    from concourse import mybir as _mybir
    from concourse.bass_utils import run_bass_kernel_spmd as _run

    nc = _bacc.Bacc("TRN2", target_bir_lowering=False, num_devices=1)
    arrays, args = {}, []
    for name in _INS:
        a = _np.ascontiguousarray(inputs[name])
        arrays[f"in_{name}_dram"] = a
        args.append(nc.dram_tensor(f"in_{name}_dram", a.shape, _mybir.dt.from_np(a.dtype), kind="ExternalInput").ap())
    for i, (shape, dtype) in enumerate(_OUTS):
        dt = _mybir.dt.from_np(_np.dtype(dtype))
        args.append(nc.dram_tensor(f"out_{i}_dram", shape, dt, kind="ExternalOutput").ap())
    gnn_ffn_kernel(nc, *args)
    r = _run(nc, [arrays], core_ids=[0])
    return r.results[0]["out_0_dram"]
```
